# Optimizing a Trainium2 kernel written in Bass

```python
import numpy as np
import jax
import jax.numpy as jnp

def _softmax(x, axis=-1):
    return jax.nn.softmax(x, axis=axis)

def _gelu(x):
    return jax.nn.gelu(x, approximate=True)

def _silu(x):
    return jax.nn.silu(x)

def _sigmoid(x):
    return jax.nn.sigmoid(x)

def _layernorm(x, axis=-1, eps=1e-05):
    m = jnp.mean(x, axis=axis, keepdims=True)
    v = jnp.var(x, axis=axis, keepdims=True)
    return (x - m) / jnp.sqrt(v + eps)

def _scatter_add(tgt, idx, src, axis=0):
    return tgt.at[idx].add(src)

def _segment_sum(src, seg, n):
    return jax.ops.segment_sum(src, seg, n)
kernel_name = 'mk_seq_preln_d2_jaxref_r4_d2b7ec'

def setup_inputs(seed: int=0):
    np.random.seed(seed)
    _w = jnp.asarray

    def _L0_attn_setup():
        import jax, jax.numpy as jnp
        import numpy as np
        D_MODEL = 256
        NUM_HEADS = 16
        HEAD_DIM = D_MODEL // NUM_HEADS
        BATCH = 4
        SEQ = 512

        def circulant(x, c, b):
            d = c.shape[0]
            y = jnp.fft.irfft(jnp.fft.rfft(x, axis=-1) * jnp.fft.rfft(c), n=d, axis=-1)
            return y + b
        key = jax.random.key(seed)
        ks = jax.random.split(key, 9)
        scale = 1.0 / np.sqrt(D_MODEL)
        inp = {'x': jax.random.normal(ks[0], (BATCH, SEQ, D_MODEL), dtype=jnp.float32), 'wq_c': jax.random.normal(ks[1], (D_MODEL,), dtype=jnp.float32) * scale, 'wq_b': jnp.zeros((D_MODEL,), dtype=jnp.float32), 'wk_c': jax.random.normal(ks[2], (D_MODEL,), dtype=jnp.float32) * scale, 'wk_b': jnp.zeros((D_MODEL,), dtype=jnp.float32), 'wv_c': jax.random.normal(ks[3], (D_MODEL,), dtype=jnp.float32) * scale, 'wv_b': jnp.zeros((D_MODEL,), dtype=jnp.float32), 'wo_c': jax.random.normal(ks[4], (D_MODEL,), dtype=jnp.float32) * scale, 'wo_b': jnp.zeros((D_MODEL,), dtype=jnp.float32)}
        return inp
    _L0_attn_in = _L0_attn_setup()

    def _L0_ffn_setup():
        import jax, jax.numpy as jnp
        import numpy as np
        EPS = 0.05
        N_ITERS = 20
        TOP_K = 2

        def _sinkhorn(cost, n_iters=N_ITERS, epsilon=EPS):
            la = cost / epsilon
            for _ in range(n_iters):
                la = la - jax.scipy.special.logsumexp(la, axis=-1, keepdims=True)
                la = la - jax.scipy.special.logsumexp(la, axis=-2, keepdims=True)
            return jnp.exp(la)
        key = jax.random.key(seed)
        k0, k1, k2, k3, k4 = jax.random.split(key, 5)
        B, T, D, F, E = (2, 512, 256, 1024, 8)
        x = jax.random.normal(k0, (B, T, D), dtype=jnp.float32)
        gate_W = jax.random.normal(k1, (E, D), dtype=jnp.float32) * 0.02
        W_gate = jax.random.normal(k2, (E, F, D), dtype=jnp.float32) * 0.02
        W_up = jax.random.normal(k3, (E, F, D), dtype=jnp.float32) * 0.02
        W_down = jax.random.normal(k4, (E, D, F), dtype=jnp.float32) * 0.02
        return {'x': x, 'gate_W': gate_W, 'W_gate': W_gate, 'W_up': W_up, 'W_down': W_down}
    _L0_ffn_in = _L0_ffn_setup()

    def _L1_attn_setup():
        import jax, jax.numpy as jnp
        import numpy as np
        B, S, D = (2, 512, 256)
        H = 16
        K = 21
        HD = D // H

        def _tisa_bias(amplitudes, sharpness, offsets, seq_len):
            rel = jnp.arange(-(seq_len - 1), seq_len, dtype=jnp.float32)
            d = rel[None, None, :] - offsets[:, :, None]
            scores = amplitudes[:, :, None] * jnp.exp(-jnp.abs(sharpness)[:, :, None] * d * d)
            scores = scores.sum(axis=1)
            idx = jnp.arange(seq_len)
            rel_idx = idx[None, :] - idx[:, None] + (seq_len - 1)
            return scores[:, rel_idx]
        key = jax.random.key(seed)
        ks = jax.random.split(key, 7)
        x = jax.random.normal(ks[0], (B, S, D), dtype=jnp.float32)
        w_in = jax.random.normal(ks[1], (D, 3 * D), dtype=jnp.float32) * (1.0 / np.sqrt(D))
        w_gate = jax.random.normal(ks[2], (D, 2 * D), dtype=jnp.float32) * (1.0 / np.sqrt(D))
        b_gate = jnp.zeros((2 * D,), dtype=jnp.float32)
        amplitudes = jax.random.normal(ks[3], (H, K), dtype=jnp.float32) * 0.1
        sharpness = jax.random.uniform(ks[4], (H, K), dtype=jnp.float32, minval=0.05, maxval=0.3)
        max_fv, min_fv = (S // 2, 5)
        offsets = jax.random.uniform(ks[5], (H, K), dtype=jnp.float32, minval=-float(max_fv), maxval=float(max_fv))
        return {'x': x, 'w_in': w_in, 'w_gate': w_gate, 'b_gate': b_gate, 'amplitudes': amplitudes, 'sharpness': sharpness, 'offsets': offsets}
    _L1_attn_in = _L1_attn_setup()

    def _L1_ffn_setup():
        import jax, jax.numpy as jnp
        import numpy as np
        FP8_MAX = 448.0
        key = jax.random.key(seed)
        k_x, k_w, k_b = jax.random.split(key, 3)
        B, S, IN, OUT = (4, 2048, 256, 256)
        x = jax.random.normal(k_x, (B, S, IN), dtype=jnp.float32)
        w_fp32 = jax.random.normal(k_w, (OUT, IN), dtype=jnp.float32)
        weight_fp8 = w_fp32.astype(jnp.float8_e4m3fn).astype(jnp.float32)
        bias = jax.random.normal(k_b, (OUT,), dtype=jnp.float32)
        input_scale = jnp.ones((1,), dtype=jnp.float32)
        weight_scale = jnp.ones((1,), dtype=jnp.float32)
        return {'x': x, 'weight_fp8': weight_fp8, 'bias': bias, 'input_scale': input_scale, 'weight_scale': weight_scale}
    _L1_ffn_in = _L1_ffn_setup()
    _d = {'L0_attn_x': _L0_attn_in['x'], 'L0_attn_wq_c': _L0_attn_in['wq_c'], 'L0_attn_wq_b': _L0_attn_in['wq_b'], 'L0_attn_wk_c': _L0_attn_in['wk_c'], 'L0_attn_wk_b': _L0_attn_in['wk_b'], 'L0_attn_wv_c': _L0_attn_in['wv_c'], 'L0_attn_wv_b': _L0_attn_in['wv_b'], 'L0_attn_wo_c': _L0_attn_in['wo_c'], 'L0_attn_wo_b': _L0_attn_in['wo_b'], 'L0_ffn_gate_W': _L0_ffn_in['gate_W'], 'L0_ffn_W_gate': _L0_ffn_in['W_gate'], 'L0_ffn_W_up': _L0_ffn_in['W_up'], 'L0_ffn_W_down': _L0_ffn_in['W_down'], 'L1_attn_w_in': _L1_attn_in['w_in'], 'L1_attn_w_gate': _L1_attn_in['w_gate'], 'L1_attn_b_gate': _L1_attn_in['b_gate'], 'L1_attn_amplitudes': _L1_attn_in['amplitudes'], 'L1_attn_sharpness': _L1_attn_in['sharpness'], 'L1_attn_offsets': _L1_attn_in['offsets'], 'L1_ffn_weight_fp8': _L1_ffn_in['weight_fp8'], 'L1_ffn_bias': _L1_ffn_in['bias'], 'L1_ffn_input_scale': _L1_ffn_in['input_scale'], 'L1_ffn_weight_scale': _L1_ffn_in['weight_scale']}
    _x0 = _d['L0_attn_x']
    _d['L0_attn_x'] = jax.random.normal(jax.random.fold_in(jax.random.key(seed), 1), (4, 1024, 256), dtype=_x0.dtype)
    del _x0
    return _d

def reference(L0_attn_x, L0_attn_wq_c, L0_attn_wq_b, L0_attn_wk_c, L0_attn_wk_b, L0_attn_wv_c, L0_attn_wv_b, L0_attn_wo_c, L0_attn_wo_b, L0_ffn_gate_W, L0_ffn_W_gate, L0_ffn_W_up, L0_ffn_W_down, L1_attn_w_in, L1_attn_w_gate, L1_attn_b_gate, L1_attn_amplitudes, L1_attn_sharpness, L1_attn_offsets, L1_ffn_weight_fp8, L1_ffn_bias, L1_ffn_input_scale, L1_ffn_weight_scale):

    def _L0_attn_ref(x, wq_c, wq_b, wk_c, wk_b, wv_c, wv_b, wo_c, wo_b):
        import jax, jax.numpy as jnp
        import numpy as np
        D_MODEL = 256
        NUM_HEADS = 16
        HEAD_DIM = D_MODEL // NUM_HEADS
        BATCH = 4
        SEQ = 512

        def circulant(x, c, b):
            d = c.shape[0]
            y = jnp.fft.irfft(jnp.fft.rfft(x, axis=-1) * jnp.fft.rfft(c), n=d, axis=-1)
            return y + b
        bs, seq_len, dm = x.shape
        Q = circulant(x, wq_c, wq_b)
        K = circulant(x, wk_c, wk_b)
        V = circulant(x, wv_c, wv_b)
        Q = Q.reshape(bs, seq_len, NUM_HEADS, HEAD_DIM)
        K = K.reshape(bs, seq_len, NUM_HEADS, HEAD_DIM)
        V = V.reshape(bs, seq_len, NUM_HEADS, HEAD_DIM)
        scale = HEAD_DIM ** (-0.5)
        attn_logits = jnp.einsum('bqhd,bkhd->bhqk', Q, K) * scale
        attn_weights = jax.nn.softmax(attn_logits, axis=-1)
        out_heads = jnp.einsum('bhqk,bkhd->bqhd', attn_weights, V)
        out_merge = out_heads.reshape(bs, seq_len, dm)
        out = circulant(out_merge, wo_c, wo_b)
        return out

    def _L0_ffn_ref(x, gate_W, W_gate, W_up, W_down):
        import jax, jax.numpy as jnp
        import numpy as np
        EPS = 0.05
        N_ITERS = 20
        TOP_K = 2

        def _sinkhorn(cost, n_iters=N_ITERS, epsilon=EPS):
            la = cost / epsilon
            for _ in range(n_iters):
                la = la - jax.scipy.special.logsumexp(la, axis=-1, keepdims=True)
                la = la - jax.scipy.special.logsumexp(la, axis=-2, keepdims=True)
            return jnp.exp(la)
        B, T, D = x.shape
        xf = x.reshape(B * T, D)
        logits = xf @ gate_W.T
        pi = _sinkhorn(-logits)
        _, top_idx = jax.lax.top_k(pi, TOP_K)
        g = jnp.einsum('nd,efd->enf', xf, W_gate)
        u = jnp.einsum('nd,efd->enf', xf, W_up)
        y = jnp.einsum('enf,edf->end', jax.nn.silu(g) * u, W_down)
        n_ar = jnp.arange(xf.shape[0])
        out = jnp.zeros_like(xf)
        for k in range(TOP_K):
            out = out + y[top_idx[:, k], n_ar] * pi[:, k:k + 1]
        return out.reshape(B, T, D)

    def _L1_attn_ref(x, w_in, w_gate, b_gate, amplitudes, sharpness, offsets):
        import jax, jax.numpy as jnp
        import numpy as np
        B, S, D = (2, 512, 256)
        H = 16
        K = 21
        HD = D // H

        def _tisa_bias(amplitudes, sharpness, offsets, seq_len):
            rel = jnp.arange(-(seq_len - 1), seq_len, dtype=jnp.float32)
            d = rel[None, None, :] - offsets[:, :, None]
            scores = amplitudes[:, :, None] * jnp.exp(-jnp.abs(sharpness)[:, :, None] * d * d)
            scores = scores.sum(axis=1)
            idx = jnp.arange(seq_len)
            rel_idx = idx[None, :] - idx[:, None] + (seq_len - 1)
            return scores[:, rel_idx]
        b, s, d = x.shape
        proj = x @ w_in
        k, v, q = jnp.split(proj, 3, axis=-1)

        def heads(t):
            return t.reshape(b, s, H, HD).transpose(0, 2, 1, 3)
        q, k, v = (heads(q), heads(k), heads(v))
        scale = 1.0 / jnp.sqrt(jnp.float32(HD))
        scores = jnp.einsum('bhqd,bhkd->bhqk', q, k) * scale
        scores = scores + _tisa_bias(amplitudes, sharpness, offsets, s)[None]
        weights = jax.nn.softmax(scores, axis=-1)
        attn = jnp.einsum('bhqk,bhkd->bhqd', weights, v)
        out = attn.transpose(0, 2, 1, 3).reshape(b, s, d)
        gated = out @ w_gate + b_gate
        a, g = jnp.split(gated, 2, axis=-1)
        return a * jax.nn.sigmoid(g)

    def _L1_ffn_ref(x, weight_fp8, bias, input_scale, weight_scale):
        import jax, jax.numpy as jnp
        import numpy as np
        FP8_MAX = 448.0
        x_q = jnp.clip(x / input_scale, -FP8_MAX, FP8_MAX)
        x_dq = x_q.astype(jnp.float8_e4m3fn).astype(x.dtype) * input_scale
        w_dq = weight_fp8 * weight_scale
        out = jnp.einsum('bsi,oi->bso', x_dq, w_dq) + bias
        return out
    x = L0_attn_x
    x = x + _L0_attn_ref(_layernorm(x, axis=-1), L0_attn_wq_c, L0_attn_wq_b, L0_attn_wk_c, L0_attn_wk_b, L0_attn_wv_c, L0_attn_wv_b, L0_attn_wo_c, L0_attn_wo_b)
    x = x + _L0_ffn_ref(_layernorm(x, axis=-1), L0_ffn_gate_W, L0_ffn_W_gate, L0_ffn_W_up, L0_ffn_W_down)
    x = x + _L1_attn_ref(_layernorm(x, axis=-1), L1_attn_w_in, L1_attn_w_gate, L1_attn_b_gate, L1_attn_amplitudes, L1_attn_sharpness, L1_attn_offsets)
    x = x + _L1_ffn_ref(_layernorm(x, axis=-1), L1_ffn_weight_fp8, L1_ffn_bias, L1_ffn_input_scale, L1_ffn_weight_scale)
    return x

_drawn_inputs = setup_inputs


def setup_inputs(seed=0):
    import zlib

    import numpy as np

    out = dict(_drawn_inputs(seed))
    spreads = {'L0_attn_wq_b': (0.0, 0.397),
     'L0_attn_wk_b': (0.0, 2.0),
     'L0_attn_wv_b': (0.0, 0.1),
     'L0_attn_wo_b': (0.0, 0.1),
     'L1_attn_b_gate': (0.0, 0.1)}
    factors = {'L0_ffn_gate_W': 8.0,
     'L0_ffn_W_gate': 8.0,
     'L0_ffn_W_up': 8.0,
     'L0_ffn_W_down': 8.0,
     'L1_attn_amplitudes': 64.0,
     'L1_attn_sharpness': 64.0,
     'L1_attn_offsets': 57.49}
    for name, (base, spread) in spreads.items():
        noise = np.random.default_rng([zlib.crc32(name.encode()), seed]).standard_normal(out[name].shape)
        drawn = base * np.exp(spread * noise) if base else spread * noise
        out[name] = jnp.asarray(drawn.astype(out[name].dtype))
    for name, factor in factors.items():
        out[name] = (out[name] * factor).astype(out[name].dtype)
    return out
```

```python
import numpy as np
from contextlib import ExitStack

import concourse.bass as bass
from concourse import mybir

FP32 = mybir.dt.float32
BF16 = mybir.dt.bfloat16
I32 = mybir.dt.int32
ALU = mybir.AluOpType
ACT = mybir.ActivationFunctionType
AX = mybir.AxisListType

P = 128
B, S, D = 4, 1024, 256
N = B * S
NT = N // P
BT = S // P
DC = D // P
H, HD = 16, 16
GH = 4
NG = H // GH
VW = HD + 1
EXPERTS, F = 8, 1024
FC = F // P
LN_EPS = 1e-5
SINKHORN_EPS, SINKHORN_ITERS = 0.05, 20
MOE_TILES = 2 * NT + EXPERTS - 1
SCORE_SCALE = HD ** -0.5
HALF = 512
Q_SLOTS = (0, 0, 0, 1, 1, 2)
K_SLOTS = (0, 1, 2, 0, 1, 0)
QK_ROWS = len(Q_SLOTS) * HD
MAX_PARTS = 3
FAST_RANGE = 60.0
TINY = 1.1754944e-38


class Done:

    def __init__(self, sem, step):
        self.sem, self.step, self.needed, self.value = sem, step, False, None


class Sem:

    def __init__(self, handle):
        self.handle, self.marks = handle, []

    def mark(self, step=1):
        done = Done(self, step)
        self.marks.append(done)
        return done

    def number(self):
        count = 0
        for done in self.marks:
            if done.needed or done.step > 1:
                count += done.step
                done.value = count


class Queues:

    ENGINES = ("tensor", "vector", "scalar", "gpsimd", "sync")

    def __init__(self, nc, ctx, name="main"):
        self.nc, self.ctx, self.name = nc, ctx, name
        self.steps = {e: [] for e in self.ENGINES}
        self.done = {e: Sem(ctx.enter_context(nc.semaphore(f"{name}_{e}_done"))) for e in self.ENGINES}
        self.lanes = {}
        self.branches = []

    def _queue(self, engine, emit, after, done):
        waits = []
        for a in after:
            if a is not None:
                a.needed = True
                waits.append(a)
        self.steps[engine].append((emit, waits, done))
        return done

    def pe(self, emit, *after):
        return self._queue("tensor", emit, after, self.done["tensor"].mark())

    def dve(self, emit, *after):
        return self._queue("vector", emit, after, self.done["vector"].mark())

    def act(self, emit, *after):
        return self._queue("scalar", emit, after, self.done["scalar"].mark())

    def pool(self, emit, *after):
        return self._queue("gpsimd", emit, after, self.done["gpsimd"].mark())

    def lane(self, name):
        if name not in self.lanes:
            self.lanes[name] = Sem(self.ctx.enter_context(self.nc.semaphore(f"{self.name}_{name}")))
        return self.lanes[name]

    def dma(self, lane, out, in_, *after, queue="sync"):
        done = self.lane(lane).mark(16)
        return self._queue(queue, lambda e: e.dma_start(out, in_), after, done)

    def dma_by(self, queue, lane, emit, *after):
        return self._queue(queue, emit, after, self.lane(lane).mark(16))

    def either(self, flag, if_set, if_clear):
        self.branches += [if_set, if_clear]
        for name in self.ENGINES:

            def emit(eng, name=name):
                is_set = eng.value_load(flag, min_val=0, max_val=1)
                with eng.If(is_set > 0):
                    if_set.play(eng, name)
                with eng.If(is_set < 1):
                    if_clear.play(eng, name)

            self.steps[name].append((emit, [], None))

    def barrier(self):
        arrived = [self._queue(e, lambda eng: eng.drain(), (), self.done[e].mark()) for e in self.ENGINES]
        arrived += [lane.marks[-1] for lane in self.lanes.values() if lane.marks]
        for e in self.ENGINES:
            self._queue(e, None, arrived, None)

    def number(self):
        for sem in [*self.done.values(), *self.lanes.values()]:
            sem.number()
        for branch in self.branches:
            branch.number()

    def play(self, eng, name):
        waited = {}
        for emit, waits, done in self.steps[name]:
            for w in waits:
                if waited.get(w.sem, 0) < w.value:
                    eng.wait_ge(w.sem.handle, w.value)
                    waited[w.sem] = w.value
            if emit is not None:
                instruction = emit(eng)
                if done is not None and (done.needed or done.step > 1):
                    instruction.then_inc(done.sem.handle, done.step)

    def emit(self):
        self.number()
        block = self.ctx.enter_context(self.nc.Block())
        block.tensor(lambda eng: self.play(eng, "tensor"))
        block.vector(lambda eng: self.play(eng, "vector"))
        block.scalar(lambda eng: self.play(eng, "scalar"))
        block.gpsimd(lambda eng: self.play(eng, "gpsimd"))
        block.sync(lambda eng: self.play(eng, "sync"))


class Ring:

    def __init__(self, n):
        self.n, self.at, self.readers = n, 0, [()] * n

    def take(self):
        slot = self.at
        self.at = (slot + 1) % self.n
        return slot, self.readers[slot]

    def free(self, slot, *readers):
        self.readers[slot] = readers


class Arena:

    def __init__(self, nc):
        self.nc, self.stack = nc, ExitStack()

    def __call__(self, name, shape, dtype=FP32):
        return self.stack.enter_context(self.nc.sbuf_tensor(name, shape, dtype))

    def close(self):
        self.stack.close()


class Machine:
    pass


def make_constants(m):
    q, sb = m.q, m.keep
    m.ident = sb("ident", [P, P])
    m.ident16 = sb("ident16", [P, P], BF16)
    m.ones = sb("ones", [P, P])
    m.head_ones = sb("head_ones", [P, P // HD], BF16)
    m.ones16 = sb("ones16", [P, P // HD], BF16)
    m.before = sb("before", [P, P])
    z = q.pool(lambda e: e.memset(m.ident[:, :], 0.0))
    z16 = q.pool(lambda e: e.memset(m.ident16[:, :], 0.0))
    o = q.pool(lambda e: e.memset(m.ones[:, :], 1.0))
    o16 = q.pool(lambda e: e.memset(m.ones16[:, :], 1.0))
    i1 = q.pool(lambda e: e.affine_select(out=m.ident[:, :], in_=m.ident[:, :], compare_op=ALU.not_equal,
                                          fill=1.0, base=0, pattern=[[-1, P]], channel_multiplier=1), z)
    i2 = q.pool(lambda e: e.affine_select(out=m.ident16[:, :], in_=m.ident16[:, :],
                                          compare_op=ALU.not_equal, fill=1.0, base=0,
                                          pattern=[[-1, P]], channel_multiplier=1), z16)
    h1 = q.pool(lambda e: e.affine_select(out=m.head_ones[:, :], in_=m.ones16[:, :],
                                          compare_op=ALU.is_ge, fill=0.0, base=0,
                                          pattern=[[-HD, P // HD]], channel_multiplier=1), o16)
    h2 = q.pool(lambda e: e.affine_select(out=m.head_ones[:, :], in_=m.head_ones[:, :],
                                          compare_op=ALU.is_ge, fill=0.0, base=HD - 1,
                                          pattern=[[HD, P // HD]], channel_multiplier=-1), h1)
    b1 = q.pool(lambda e: e.affine_select(out=m.before[:, :], in_=m.ones[:, :], compare_op=ALU.is_ge,
                                          fill=0.0, base=-1, pattern=[[1, P]], channel_multiplier=-1), o)
    m.constants = q.pool(lambda e: e.memset(m.ones16[:, :], 1.0), i1, i2, h2, b1)


def across(row, parts):
    return bass.AP(tensor=row.tensor, offset=row.offset, ap=[[0, parts], *[list(x) for x in row.ap]])


def layernorm(m, w, x, xn, ready):
    q = m.q
    stats, mv, v, y, t = w["stats"], w["mv"], w["v"], w["y"], w["t"]
    marks = [q.dve(lambda e, i=i: e.bn_stats(stats[:, i, :], x[:, i, :]), ready) for i in range(BT)]
    marks = [q.dve(lambda e, i=i: e.bn_aggr(mv[:, i, :], stats[:, i, :]), marks[i]) for i in range(BT)]
    v1 = q.dve(lambda e: e.tensor_scalar(v[:, :], mv[:, :, 1], LN_EPS, None, ALU.add), marks[-1])
    l = q.act(lambda e: e.activation(y[:, :], v[:, :], ACT.Ln), v1)
    l = q.act(lambda e: e.activation(y[:, :], y[:, :], ACT.Exp, scale=-0.5), l)
    a = q.dve(lambda e: e.tensor_tensor(t[:, :], y[:, :], y[:, :], ALU.mult), l)
    a = q.dve(lambda e: e.tensor_tensor(t[:, :], t[:, :], v[:, :], ALU.mult), a)
    a = q.dve(lambda e: e.tensor_scalar(t[:, :], t[:, :], -0.5, 1.5, ALU.mult, ALU.add), a)
    a = q.dve(lambda e: e.tensor_tensor(y[:, :], y[:, :], t[:, :], ALU.mult), a)
    for i in range(BT):
        last = q.dve(lambda e, i=i: e.tensor_scalar(xn[:, i, :], x[:, i, :], mv[:, i, 0:1], y[:, i:i + 1],
                                                    ALU.subtract, ALU.mult), a)
    return last


def layernorm_scratch(sb, name):
    return {"stats": sb(name + "stats", [P, BT, 6]), "mv": sb(name + "mv", [P, BT, 2]),
            "v": sb(name + "v", [P, BT]), "y": sb(name + "y", [P, BT]), "t": sb(name + "t", [P, BT])}


def transpose_batch(m, ring, src, dst, ready, dst_free=()):
    q = m.q
    out = []
    for c in range(DC):
        slot, free = ring.take()
        ps = m.psum[:, slot * S:(slot + 1) * S]
        for t in range(BT):
            tr = q.pe(lambda e, t=t, c=c, ps=ps: e.transpose(ps[:, t * P:(t + 1) * P],
                                                             src[:, t, c * P:(c + 1) * P], m.ident[:, :]),
                      ready, m.constants, *free)
        cp = q.act(lambda e, c=c, ps=ps: e.activation(dst[:, c, :], ps, ACT.Copy), tr, *dst_free)
        ring.free(slot, cp)
        out.append(cp)
    return out


def project(m, layer, open_batch, weights, biases, parts):
    q, nc = m.q, m.nc
    sb = Arena(nc)
    n = f"L{layer}_"
    w = [sb(n + f"w{i}", [P, DC, D]) for i in range(3)]
    b_qk = sb(n + "b_qk", [P, 2, DC])
    b_v = sb(n + "b_v", [P, D])
    x = sb(n + "x", [P, 2, BT, D])
    xn = sb(n + "xn", [P, 2, BT, D])
    xT = sb(n + "xT", [P, 2, DC, S])
    split = [sb(n + f"part{i}", [P, 2, S], BF16) for i in range(3)]
    rest = sb(n + "rest", [P, 2, S])
    square = sb(n + "square", [P, 2, S], BF16)
    lnw = layernorm_scratch(sb, n)
    nmax = m.norms

    got_w = [q.dma(n + "w_in", w[i][:, :, :], weights[i].rearrange("(c p) n -> p c n", p=P), queue="scalar")
             for i in range(3)][-1]
    if biases is None:
        zb = q.dve(lambda e: e.memset(b_qk[:, :, :], 0.0))
        zv = q.dve(lambda e: e.memset(b_v[:, :], 0.0))
        bias_ready = (zb, zv)
    else:
        for i in range(2):
            last = q.dma(n + "b_in", b_qk[:, i, :], biases[i], queue="scalar")
        last = q.dma(n + "b_in", b_v[:, :], across(biases[2], P), queue="scalar")
        bias_ready = (last,)
    ones_in = q.pool(lambda e: e.memset(m.v[:, :, :], 1.0))

    ring = Ring(4)
    x_ring, xT_ring, part_ring, rest_ring, square_ring = Ring(2), Ring(2), Ring(2), Ring(2), Ring(2)

    def prepare(b):
        xs, free = x_ring.take()
        got, kept = open_batch(b, xs, x[:, xs, :, :], free)
        normed = layernorm(m, lnw, x[:, xs, :, :], xn[:, xs, :, :], got)
        ts, t_free = xT_ring.take()
        made = transpose_batch(m, ring, xn[:, xs, :, :], xT[:, ts, :, :], normed, t_free)
        x_ring.free(xs, *made, *kept)
        return ts, made

    ahead = prepare(0)
    for b in range(B):
        ts, made = ahead
        for op in range(2):
            for c in range(DC):
                slot, free = ring.take()
                ps = m.psum[:, slot * S:(slot + 1) * S]
                for j in range(S // HALF):
                    for k in range(DC):
                        mm = q.pe(lambda e, op=op, c=c, j=j, k=k, ps=ps, ts=ts: e.matmul(
                            ps[:, j * HALF:(j + 1) * HALF], w[op][:, k, c * P:(c + 1) * P],
                            xT[:, ts, k, j * HALF:(j + 1) * HALF], start=(k == 0), stop=(k == DC - 1)),
                            got_w, *made, *free)
                bias = b_qk[:, op, c:c + 1]
                s, s_free = part_ring.take()
                hi = q.act(lambda e, s=s, ps=ps, bias=bias: e.activation(split[0][:, s, :], ps, ACT.Identity,
                                                                         bias=bias), mm, *bias_ready, *s_free)
                z, z_free = square_ring.take()
                sq = q.act(lambda e, z=z, s=s: e.activation(square[:, z, :], split[0][:, s, :], ACT.Square),
                           hi, *z_free)
                r, r_free = rest_ring.take()
                rs = q.dve(lambda e, s=s, r=r, ps=ps, bias=bias: e.scalar_tensor_tensor(
                    out=rest[:, r, :], in0=ps, scalar=bias, in1=split[0][:, s, :], op0=ALU.add,
                    op1=ALU.subtract), hi, *r_free)
                ring.free(slot, rs)
                mid = q.pool(lambda e, s=s, r=r: e.tensor_copy(split[1][:, s, :], rest[:, r, :]), rs, *s_free)
                low = q.pool(lambda e, s=s, r=r: e.tensor_tensor(split[2][:, s, :], rest[:, r, :],
                                                                 split[1][:, s, :], ALU.subtract), mid)
                rest_ring.free(r, low)
                sent = [q.dma(n + f"part_out{s}", parts[op, i, b, c * P:(c + 1) * P, :], split[i][:, s, :], done)
                        for i, done in enumerate((hi, mid, low))][-1]
                part_ring.free(s, sent, sq)
                nslot, n_free = ring.take()
                nps = m.psum[0:P // HD, nslot * S:(nslot + 1) * S]
                for j in range(S // HALF):
                    nm = q.pe(lambda e, j=j, z=z, nps=nps: e.matmul(
                        nps[:, j * HALF:(j + 1) * HALF], m.head_ones[:, :],
                        square[:, z, j * HALF:(j + 1) * HALF], start=True, stop=True), sq, *n_free)
                square_ring.free(z, nm)
                mx = q.dve(lambda e, op=op, c=c, b=b, nps=nps: e.reduce_max(
                    nmax[:, op, c * B + b:c * B + b + 1], nps, AX.X), nm)
                ring.free(nslot, mx)
            if op == 0 and b + 1 < B:
                ahead = prepare(b + 1)
        for half in range(2):
            slot, free = ring.take()
            ps = m.psum[:, slot * S:(slot + 1) * S]
            for i in range(BT // 2):
                t = half * (BT // 2) + i
                for k in range(DC):
                    mm = q.pe(lambda e, i=i, t=t, k=k, ps=ps, ts=ts: e.matmul(
                        ps[:, i * D:(i + 1) * D], xT[:, ts, k, t * P:(t + 1) * P], w[2][:, k, :],
                        start=(k == 0), stop=(k == DC - 1)), *free)
            t0 = b * BT + half * (BT // 2)
            for i in range(BT // 2):
                vd = q.dve(lambda e, i=i, t0=t0, ps=ps: e.tensor_tensor(
                    m.v[:, t0 + i, 0:H * VW].rearrange("p (h w) -> p h w", w=VW)[:, :, 0:HD],
                    ps[:, i * D:(i + 1) * D].rearrange("p (h w) -> p h w", w=HD),
                    b_v[:, :].rearrange("p (h w) -> p h w", w=HD), ALU.add), mm, ones_in, *bias_ready)
            ring.free(slot, vd)
        xT_ring.free(ts, mm)
    q.barrier()
    sb.close()


def load_tokens(m, x_dram):
    src = x_dram.rearrange("(b t p) d -> b p t d", p=P, t=BT)

    def open_batch(b, slot, x, free):
        return m.q.dma(f"x_in{slot}", x, src[b, :, :, :], *free), ()

    return open_batch


def score_bound(m, layer, table_range):
    q = m.q
    s = m.bound
    a = q.dve(lambda e: e.tensor_tensor(s[0:H // DC, 0:DC * B], m.norms[:, 0, :], m.norms[:, 1, :], ALU.mult))
    a = q.dve(lambda e: e.reduce_max(s[0:H // DC, 8:9], s[0:H // DC, 0:DC * B], AX.X), a)
    t = q.pe(lambda e: e.transpose(m.psum[0:1, 0:H // DC], s[0:H // DC, 8:9],
                                   m.ident[0:H // DC, 0:H // DC]), a)
    a = q.dve(lambda e: e.reduce_max(s[0:1, 9:10], m.psum[0:1, 0:H // DC], AX.X), t)
    a = q.dve(lambda e: e.tensor_scalar(s[0:1, 9:10], s[0:1, 9:10], 1e-12, 1e15, ALU.max, ALU.min), a)
    a = q.act(lambda e: e.activation(s[0:1, 9:10], s[0:1, 9:10], ACT.Ln), a)
    a = q.act(lambda e: e.activation(s[0:1, 10:11], s[0:1, 9:10], ACT.Exp, scale=0.5), a)
    a = q.dve(lambda e: e.tensor_scalar(s[0:1, 10:11], s[0:1, 10:11], 1.01 * SCORE_SCALE, None, ALU.mult), a)
    if table_range is not None:
        hi = q.dve(lambda e: e.tensor_tensor(s[0:1, 11:12], s[0:1, 10:11], table_range[:, 0:1], ALU.add), a)
        lo = q.dve(lambda e: e.tensor_tensor(s[0:1, 12:13], s[0:1, 10:11], table_range[:, 1:2], ALU.add), a)
    else:
        hi = q.dve(lambda e: e.tensor_copy(s[0:1, 11:12], s[0:1, 10:11]), a)
        lo = q.dve(lambda e: e.tensor_copy(s[0:1, 12:13], s[0:1, 10:11]), a)
    a = q.dve(lambda e: e.tensor_tensor(s[0:1, 13:14], s[0:1, 11:12], s[0:1, 12:13], ALU.add), hi, lo)
    flag = q.dve(lambda e: e.tensor_scalar(m.flag[0:1, 0:1], s[0:1, 13:14], FAST_RANGE, None, ALU.is_le), a)
    b = q.pe(lambda e: e.matmul(m.psum[:, HALF:HALF + 1], m.ones[0:1, :], s[0:1, 11:12], start=True, stop=True), a)
    c = q.dve(lambda e: e.tensor_scalar(m.shift[:, 0:1], m.psum[:, HALF:HALF + 1], -1.0, None, ALU.mult), b)
    return flag, c


def attention(m, layer, parts, tables, om, order, row_max):
    q, nc = m.q, m.nc
    sb = Arena(nc)
    n = f"A{layer}{'r' if row_max else 'f'}_"
    rows = QK_ROWS + MAX_PARTS if row_max else QK_ROWS
    qa = sb(n + "qa", [P, 2, GH, S], BF16)
    ka = sb(n + "ka", [P, 2, GH, S], BF16)
    n_probs = 8
    probs = sb(n + "probs", [P, n_probs, S])
    o_sb = sb(n + "o_sb", [P, 2, S])
    rec = sb(n + "rec", [P, 2, BT, GH])
    TW = 2 * S - P
    if tables is not None:
        bias = sb(n + "bias", [P, 1 if row_max else 2, GH, TW])
        if row_max:
            mirrored = sb(n + "mirrored", [P, 1, GH, TW])
    s_ring, p_ring, qk_ring, o_ring, t_ring = Ring(3), Ring(n_probs), Ring(2), Ring(2), Ring(1 if row_max else 2)
    O = m.psum[:, 3 * S:4 * S]
    o_free = ()
    src = parts.rearrange("o i b (h d) t -> o i b d h t", d=HD)
    if row_max:
        nm = sb(n + "nm", [P, GH * BT])
        rm = sb(n + "rm", [GH * BT, P])
        rmp = sb(n + "rmp", [GH * BT, MAX_PARTS, P], BF16)
        one = q.pool(lambda e: e.memset(ka[QK_ROWS:P, :, :, :], 1.0))

    def load(g, b):
        s, free = qk_ring.take()
        for op, slots, dst in ((0, Q_SLOTS, qa), (1, K_SLOTS, ka)):
            for r, part in enumerate(slots):
                got = q.dma(n + f"qk_in{s}", dst[r * HD:(r + 1) * HD, s, :, :],
                            src[op, part, b, :, g * GH:(g + 1) * GH, :], *free)
        return s, got

    def load_table(g):
        s, free = t_ring.take()
        for i in range(GH):
            for which, dst in enumerate((bias, mirrored) if row_max else (bias,)):
                row = tables[which, g * GH + i, :]
                got = q.dma(n + f"bias_in{s}", dst[:, s, i, :],
                            bass.AP(tensor=row.tensor, offset=row.offset, ap=[[1, P], [1, TW]]), *free)
        return s, got

    todo = []

    def finish(g, b, os_, moved):
        slot, free = s_ring.take()
        ps = m.psum[:, slot * S:(slot + 1) * S]
        for t in range(BT):
            tr = q.pe(lambda e, t=t, os_=os_, ps=ps: e.transpose(
                ps[:, t * P:(t + 1) * P], o_sb[:, os_, t * P:(t + 1) * P], m.ident[:, :]), moved, *free)
        v = ps.rearrange("p (t i c) -> p t i c", i=GH, c=P // GH)
        rc = q.dve(lambda e, v=v, os_=os_: e.reciprocal(rec[:, os_, :, :], v[:, :, :, HD]), tr)
        r = rec[:, os_, :, :]
        r = bass.AP(tensor=r.tensor, offset=r.offset, ap=[*[list(a) for a in r.ap], [0, HD]])
        nr = q.dve(lambda e, v=v, r=r, g=g, b=b: e.tensor_tensor(
            om[:, b * BT:(b + 1) * BT, g * GH * HD:(g + 1) * GH * HD].rearrange("p t (i d) -> p t i d", d=HD),
            v[:, :, :, 0:HD], r, ALU.mult), rc)
        s_ring.free(slot, nr)
        o_ring.free(os_, nr)

    def find_row_max(b, s, got, t_slot, t_got):
        for i in range(GH):
            for t in range(BT):
                slot, free = s_ring.take()
                ps = m.psum[:, slot * S:(slot + 1) * S]
                for j in range(S // HALF):
                    mm = q.pe(lambda e, i=i, t=t, j=j, ps=ps: e.matmul(
                        ps[:, j * HALF:(j + 1) * HALF], qa[0:QK_ROWS, s, i, t * P:(t + 1) * P],
                        ka[0:QK_ROWS, s, i, j * HALF:(j + 1) * HALF], start=True, stop=True), got, *free)
                if tables is not None:
                    row = mirrored[:, t_slot, i, P * t:P * t + S][:, ::-1]
                    mm = q.dve(lambda e, ps=ps, row=row: e.scalar_tensor_tensor(
                        out=ps, in0=ps, scalar=SCORE_SCALE, in1=row, op0=ALU.mult, op1=ALU.add), mm, t_got)
                mx = q.dve(lambda e, i=i, t=t, ps=ps: e.tensor_reduce(
                    out=nm[:, i * BT + t:i * BT + t + 1], in_=ps, axis=AX.X, op=ALU.max, negate=True), mm)
                s_ring.free(slot, mx)
        if tables is not None:
            mx = q.dve(lambda e: e.tensor_scalar(nm[:, :], nm[:, :], 1.0 / SCORE_SCALE, None, ALU.mult), mx)
        slot, free = s_ring.take()
        ps = m.psum[:, slot * S:(slot + 1) * S]
        tr = q.pe(lambda e: e.transpose(ps[0:GH * BT, 0:P], nm[:, :], m.ident[:, :]), mx, *free)
        a = q.dve(lambda e: e.tensor_copy(rmp[:, 0, :], ps[0:GH * BT, 0:P]), tr)
        a = q.dve(lambda e: e.tensor_tensor(rm[:, :], ps[0:GH * BT, 0:P], rmp[:, 0, :], ALU.subtract), a)
        s_ring.free(slot, a)
        a = q.dve(lambda e: e.tensor_copy(rmp[:, 1, :], rm[:, :]), a)
        a = q.dve(lambda e: e.tensor_tensor(rmp[:, 2, :], rm[:, :], rmp[:, 1, :], ALU.subtract), a)
        for i in range(MAX_PARTS):
            row = QK_ROWS + i
            got = q.dma(n + "max_in", qa[row:row + 1, s, :, :].rearrange("a h t -> a (h t)"),
                        rmp[:, i, :], a)
        q.dve(lambda e: e.memset(rm[:, 0:1], 0.0), got)
        return got

    groups = list(order)
    loads = {0: load(*groups[0])}
    table_of, tables_at = {}, {}
    if tables is not None:
        table_of[groups[0][0]] = load_table(groups[0][0])
    quads = []
    state = {}

    def queue_pv():
        nonlocal o_free
        g, b, kt, slots, exps = quads.pop(0)
        for j in range(S // HALF):
            for i in range(GH):
                h = g * GH + i
                pv = q.pe(lambda e, i=i, j=j, h=h, kt=kt, b=b, sl=slots[i]: e.matmul(
                    O[32 * i:32 * (i + 1), j * HALF:(j + 1) * HALF],
                    m.v[:, b * BT + kt, h * VW:h * VW + 32], probs[:, sl, j * HALF:(j + 1) * HALF],
                    start=(kt == 0), stop=(kt == BT - 1)), *exps, *(o_free if kt == 0 else ()))
        for sl in slots:
            p_ring.free(sl, pv)
        if kt == BT - 1:
            os_, free = o_ring.take()
            if tables is None:
                moved = q.dve(lambda e, os_=os_: e.tensor_copy(o_sb[:, os_, :], O), pv, *free)
            else:
                moved = q.act(lambda e, os_=os_: e.activation(o_sb[:, os_, :], O, ACT.Copy), pv, *free)
            o_free = (moved,)
            todo.append([g, b, os_, moved])

    for at, (g, b) in enumerate(groups):
        s, got = loads.pop(at)
        ready = (got,)
        t_slot = None
        if tables is not None:
            if g not in table_of:
                table_of[g] = load_table(g)
            t_slot, t_got = table_of[g]
        if row_max:
            while quads:
                queue_pv()
            while todo:
                finish(*todo.pop(0))
            ready = (got, find_row_max(b, s, got, t_slot, t_got if tables is not None else None), one)
        for kt in range(BT):
            slots, exps = [], []
            for i in range(GH):
                slot, free = s_ring.take()
                ps = m.psum[:, slot * S:(slot + 1) * S]
                for j in range(S // HALF):
                    mm = q.pe(lambda e, i=i, j=j, kt=kt, s=s, ps=ps: e.matmul(
                        ps[:, j * HALF:(j + 1) * HALF], ka[0:rows, s, i, kt * P:(kt + 1) * P],
                        qa[0:rows, s, i, j * HALF:(j + 1) * HALF], start=True, stop=True), *ready, *free)
                scale = SCORE_SCALE
                if tables is not None:
                    u0 = P * kt
                    row = bias[:, t_slot, i, u0:u0 + S][:, ::-1]
                    mm = q.dve(lambda e, ps=ps, row=row: e.scalar_tensor_tensor(
                        out=ps, in0=ps, scalar=SCORE_SCALE, in1=row, op0=ALU.mult, op1=ALU.add), mm, t_got)
                    scale = 1.0
                    last_bias = mm
                sl, p_free = p_ring.take()
                shift = {} if row_max else {"bias": m.shift[:, 0:1]}
                ex = q.act(lambda e, sl=sl, ps=ps, scale=scale, shift=shift: e.activation(
                    probs[:, sl, :], ps, ACT.Exp, scale=scale, **shift), mm, *p_free)
                s_ring.free(slot, ex)
                slots.append(sl)
                exps.append(ex)
                if i == 1 and quads:
                    queue_pv()
                    if kt == 2 and todo:
                        finish(*todo.pop(0))
            quads.append((g, b, kt, slots, exps))
            if kt == 0 and at + 1 < len(groups):
                loads[at + 1] = load(*groups[at + 1])
                g1 = groups[at + 1][0]
                if tables is not None and not row_max and g1 not in table_of:
                    table_of[g1] = load_table(g1)
        qk_ring.free(s, mm if tables is None else ex)
        if tables is not None and not any(x[0] == g for x in groups[at + 1:]):
            t_ring.free(t_slot, last_bias)
    while quads:
        queue_pv()
    while todo:
        finish(*todo.pop(0))
    q.barrier()
    sb.close()


def widen(ap, n):
    return bass.AP(tensor=ap.tensor, offset=ap.offset, ap=[*[list(a) for a in ap.ap], [0, n]])


def repeat(ap, n):
    a = [list(x) for x in ap.ap]
    return bass.AP(tensor=ap.tensor, offset=ap.offset, ap=[a[0], [0, n], *a[1:]])


def close_first_attention(m, om, x_dram, wo_dram, bo_dram, gate_dram, x1_dram, xn1, la):
    q = m.q
    sb = Arena(m.nc)
    wo = sb("wo", [P, DC, D])
    bo = sb("bo", [P, D])
    gate = sb("gate", [P, DC, EXPERTS])
    x = sb("c_x", [P, 2, BT, D])
    x1 = sb("c_x1", [P, 2, BT, D])
    omT = sb("c_omT", [P, 2, DC, S])
    xnT = sb("c_xnT", [P, 2, DC, S])
    lnw = layernorm_scratch(sb, "c_")
    q.dma("close_w", wo[:, :, :], wo_dram.rearrange("(c p) n -> p c n", p=P))
    q.dma("close_w", bo[:, :], across(bo_dram, P))
    got_w = q.dma("close_w", gate[:, :, :], gate_dram.rearrange("(c p) n -> p c n", p=P))
    ring = Ring(4)
    x_ring, x1_ring, omT_ring, xnT_ring = Ring(2), Ring(2), Ring(2), Ring(2)
    x_src = x_dram.rearrange("(b t p) d -> b p t d", p=P, t=BT)
    x1_dst = x1_dram.rearrange("(b t p) d -> b p t d", p=P, t=BT)

    def open_batch(b):
        s, free = x_ring.take()
        got = q.dma(f"c_x_in{s}", x[:, s, :, :], x_src[b, :, :, :], *free)
        biased = q.pool(lambda e, s=s: e.tensor_tensor(x[:, s, :, :], x[:, s, :, :], repeat(bo[:, :], BT),
                                                       ALU.add), got, got_w)
        o, o_free = omT_ring.take()
        r, r_free = x1_ring.take()
        made = transpose_batch(m, ring, om[:, b * BT:(b + 1) * BT, :], omT[:, o, :, :], None, o_free)
        for half in range(2):
            slot, free = ring.take()
            ps = m.psum[:, slot * S:(slot + 1) * S]
            for i in range(BT // 2):
                t = half * (BT // 2) + i
                for k in range(DC):
                    mm = q.pe(lambda e, i=i, t=t, k=k, ps=ps, o=o: e.matmul(
                        ps[:, i * D:(i + 1) * D], omT[:, o, k, t * P:(t + 1) * P], wo[:, k, :],
                        start=(k == 0), stop=(k == DC - 1)), *made, got_w, *free)
            t0 = half * (BT // 2)
            added = q.dve(lambda e, s=s, r=r, half=half, t0=t0, ps=ps: e.tensor_tensor(
                x1[:, r, t0:t0 + BT // 2, :], ps.rearrange("p (t d) -> p t d", d=D),
                x[:, s, half * (BT // 2):(half + 1) * (BT // 2), :], ALU.add), mm, biased, *r_free)
            ring.free(slot, added)
        omT_ring.free(o, mm)
        x_ring.free(s, added)
        normed = layernorm(m, lnw, x1[:, r, :, :], xn1[:, b * BT:(b + 1) * BT, :], added)
        x1_ring.free(r, normed, q.dma(f"x1_out{r}", x1_dst[b, :, :, :], x1[:, r, :, :], added))
        return normed

    def route_batch(b, normed):
        o, o_free = xnT_ring.take()
        made = transpose_batch(m, ring, xn1[:, b * BT:(b + 1) * BT, :], xnT[:, o, :, :], normed, o_free)
        slot, free = ring.take()
        ps = m.psum[:, slot * S:slot * S + BT * EXPERTS]
        for t in range(BT):
            for k in range(DC):
                mm = q.pe(lambda e, t=t, k=k, ps=ps, o=o: e.matmul(
                    ps[:, t * EXPERTS:(t + 1) * EXPERTS], xnT[:, o, k, t * P:(t + 1) * P], gate[:, k, :],
                    start=(k == 0), stop=(k == DC - 1)), *made, *free)
        xnT_ring.free(o, mm)
        got = q.dve(lambda e, b=b, ps=ps: e.tensor_scalar(
            la[:, b * BT:(b + 1) * BT, :], ps.rearrange("p (t e) -> p t e", e=EXPERTS),
            -1.0 / SINKHORN_EPS, None, ALU.mult), mm)
        ring.free(slot, got)

    normed = open_batch(0)
    for b in range(B):
        before = normed
        if b + 1 < B:
            normed = open_batch(b + 1)
        route_batch(b, before)
    q.barrier()
    sb.close()


def sinkhorn(m, la, pi):
    q = m.q
    sb = Arena(m.nc)
    E = EXPERTS
    mx = sb("s_mx", [P, NT])
    ex = sb("s_ex", [P, NT, E])
    sm = sb("s_sm", [P, NT])
    cm = sb("s_cm", [P, E])
    gm = sb("s_gm", [E, 1])
    dg = sb("s_dg", [E, E])
    cs = sb("s_cs", [P, E])
    cl = sb("s_cl", [P, E])
    ps_t = m.psum[0:E, 0:P]
    ps_m = m.psum[:, HALF:HALF + E]
    ps_s = m.psum[:, 2 * HALF:2 * HALF + E]
    by_expert = la[:, :, :].rearrange("p t e -> p e t")
    a = None
    for _ in range(SINKHORN_ITERS):
        a = q.dve(lambda e: e.reduce_max(mx[:, :], la[:, :, :], AX.X), a)
        a = q.dve(lambda e: e.tensor_tensor(la[:, :, :], la[:, :, :], widen(mx[:, :], E), ALU.subtract), a)
        a = q.act(lambda e: e.activation(ex[:, :, :], la[:, :, :], ACT.Exp), a)
        a = q.dve(lambda e: e.reduce_sum(sm[:, :], ex[:, :, :], AX.X), a)
        a = q.act(lambda e: e.activation(sm[:, :], sm[:, :], ACT.Ln), a)
        a = q.dve(lambda e: e.tensor_tensor(la[:, :, :], la[:, :, :], widen(sm[:, :], E), ALU.subtract), a)
        a = q.dve(lambda e: e.reduce_max(cm[:, :], by_expert, AX.X), a)
        a = q.pe(lambda e: e.transpose(ps_t, cm[:, :], m.ident[:, :]), a)
        a = q.dve(lambda e: e.reduce_max(gm[:, :], ps_t, AX.X), a)
        a = q.dve(lambda e: e.tensor_scalar(dg[:, :], m.ident[0:E, 0:E], gm[:, 0:1], None, ALU.mult), a)
        a = q.pe(lambda e: e.matmul(ps_m, m.ones[0:E, :], dg[:, :], start=True, stop=True), a)
        a = q.dve(lambda e: e.tensor_tensor(la[:, :, :], la[:, :, :], repeat(ps_m, NT), ALU.subtract), a)
        a = q.act(lambda e: e.activation(ex[:, :, :], la[:, :, :], ACT.Exp), a)
        a = q.dve(lambda e: e.reduce_sum(cs[:, :], ex[:, :, :].rearrange("p t e -> p e t"), AX.X), a)
        a = q.pe(lambda e: e.matmul(ps_s, m.ones[:, :], cs[:, :], start=True, stop=True), a)
        a = q.act(lambda e: e.activation(cl[:, :], ps_s, ACT.Ln), a)
        a = q.dve(lambda e: e.tensor_tensor(la[:, :, :], la[:, :, :], repeat(cl[:, :], NT), ALU.subtract), a)
    q.act(lambda e: e.activation(pi[:, :, :], la[:, :, :], ACT.Exp), a)
    q.barrier()
    sb.close()


def route(m, pi, slots, plan):
    q = m.q
    sb = Arena(m.nc)
    E = EXPERTS
    key = sb("r_key", [P, NT, E])
    top = sb("r_top", [P, NT])
    eq = sb("r_eq", [P, NT, E])
    rank = sb("r_rank", [P, E])
    pick = [sb(f"r_pick{k}", [P, NT, E]) for k in range(2)]
    both = sb("r_both", [P, NT, E])
    pos = sb("r_pos", [P, NT, E])
    total = sb("r_total", [P, NT, E])
    scan = [sb(f"r_scan{k}", [P, NT, E]) for k in range(2)]
    tiles = sb("r_tiles", [P, E])
    tiles_i = sb("r_tiles_i", [P, E], I32)
    upto = [sb(f"r_upto{k}", [P, E]) for k in range(2)]
    prod = sb("r_prod", [P, NT, E])
    row = sb("r_row", [P, NT])
    J = MOE_TILES
    j_iota = sb("r_j", [1, J])
    ge = sb("r_ge", [1, J, E])
    ex = sb("r_ex", [1, J])
    new = sb("r_new", [1, J])
    run = [sb(f"r_run{k}", [1, J]) for k in range(2)]
    three = sb("r_three", [1, J])
    r0 = q.pool(lambda e: e.iota(rank[:, :], pattern=[[-1, E]], base=E, channel_multiplier=0,
                                 allow_small_or_imprecise_dtypes=True))
    j0 = q.pool(lambda e: e.iota(j_iota[:, :], pattern=[[1, J]], base=0, channel_multiplier=0,
                                 allow_small_or_imprecise_dtypes=True))
    a = q.dve(lambda e: e.tensor_scalar(eq[:, :, :], pi[:, :, :], TINY, None, ALU.is_ge), r0, j0)
    a = q.dve(lambda e: e.tensor_tensor(key[:, :, :], pi[:, :, :], eq[:, :, :], ALU.mult), a)
    for k in range(2):
        a = q.dve(lambda e: e.reduce_max(top[:, :], key[:, :, :], AX.X), a)
        a = q.dve(lambda e: e.tensor_tensor(eq[:, :, :], key[:, :, :], widen(top[:, :], E), ALU.is_equal), a)
        a = q.dve(lambda e: e.tensor_tensor(eq[:, :, :], eq[:, :, :], repeat(rank[:, :], NT), ALU.mult), a)
        a = q.dve(lambda e: e.reduce_max(top[:, :], eq[:, :, :], AX.X), a)
        a = q.dve(lambda e, k=k: e.tensor_tensor(pick[k][:, :, :], eq[:, :, :], widen(top[:, :], E),
                                                 ALU.is_equal), a)
        if k == 0:
            a = q.dve(lambda e: e.scalar_tensor_tensor(out=key[:, :, :], in0=pick[0][:, :, :], scalar=-4.0,
                                                       in1=key[:, :, :], op0=ALU.mult, op1=ALU.add), a)
    a = q.dve(lambda e: e.tensor_tensor(both[:, :, :], pick[0][:, :, :], pick[1][:, :, :], ALU.add), a)
    flat = both[:, :, :].rearrange("p t e -> p (t e)")
    p1 = q.pe(lambda e: e.matmul(m.psum[:, 0:NT * E], m.before[:, :], flat, start=True, stop=True), a)
    p2 = q.pe(lambda e: e.matmul(m.psum[:, HALF:HALF + NT * E], m.ones[:, :], flat, start=True, stop=True), a)
    a = q.dve(lambda e: e.tensor_copy(pos[:, :, :].rearrange("p t e -> p (t e)"), m.psum[:, 0:NT * E]), p1)
    a = q.dve(lambda e: e.tensor_copy(total[:, :, :].rearrange("p t e -> p (t e)"),
                                      m.psum[:, HALF:HALF + NT * E]), p2, a)
    cur, at, step = total, 0, 1
    while step < NT:
        dst = scan[at]
        q.dve(lambda e, cur=cur, dst=dst, step=step: e.tensor_copy(dst[:, 0:step, :], cur[:, 0:step, :]), a)
        a = q.dve(lambda e, cur=cur, dst=dst, step=step: e.tensor_tensor(
            dst[:, step:NT, :], cur[:, step:NT, :], cur[:, 0:NT - step, :], ALU.add), a)
        cur, at, step = dst, 1 - at, 2 * step
    count = cur[:, NT - 1, :]
    a = q.dve(lambda e, cur=cur: e.tensor_tensor(pos[:, :, :], pos[:, :, :], cur[:, :, :], ALU.add), a)
    a = q.dve(lambda e: e.tensor_tensor(pos[:, :, :], pos[:, :, :], total[:, :, :], ALU.subtract), a)
    a = q.dve(lambda e, count=count: e.tensor_scalar(tiles_i[:, :], count, float(P - 1), None, ALU.add), a)
    a = q.dve(lambda e: e.tensor_scalar(tiles_i[:, :], tiles_i[:, :], P.bit_length() - 1, None,
                                        ALU.logical_shift_right), a)
    a = q.dve(lambda e: e.tensor_copy(tiles[:, :], tiles_i[:, :]), a)
    cur, at, step = tiles, 0, 1
    while step < E:
        dst = upto[at]
        q.dve(lambda e, cur=cur, dst=dst, step=step: e.tensor_copy(dst[:, 0:step], cur[:, 0:step]), a)
        a = q.dve(lambda e, cur=cur, dst=dst, step=step: e.tensor_tensor(
            dst[:, step:E], cur[:, step:E], cur[:, 0:E - step], ALU.add), a)
        cur, at, step = dst, 1 - at, 2 * step
    end = cur
    a = q.dve(lambda e, end=end: e.tensor_tensor(tiles[:, :], end[:, :], tiles[:, :], ALU.subtract), a)
    a = q.dve(lambda e: e.scalar_tensor_tensor(out=pos[:, :, :], in0=repeat(tiles[:, :], NT), scalar=float(P),
                                               in1=pos[:, :, :], op0=ALU.mult, op1=ALU.add), a)
    for k in range(2):
        a = q.dve(lambda e, k=k: e.tensor_tensor(prod[:, :, :], pick[k][:, :, :], pos[:, :, :], ALU.mult), a)
        a = q.dve(lambda e: e.reduce_sum(row[:, :], prod[:, :, :], AX.X), a)
        a = q.dve(lambda e, k=k: e.tensor_copy(slots[:, k, :], row[:, :]), a)
    a = q.dve(lambda e, end=end: e.tensor_tensor(ge[:, :, :], widen(j_iota[:, :], E), repeat(end[0:1, :], J),
                                                 ALU.is_ge), a)
    a = q.dve(lambda e: e.reduce_sum(ex[:, :], ge[:, :, :], AX.X), a)
    a = q.dve(lambda e: e.tensor_scalar(ex[:, :], ex[:, :], float(E - 1), None, ALU.min), a)
    q.dve(lambda e: e.memset(new[:, 0:1], 0.0))
    a = q.dve(lambda e: e.tensor_tensor(new[:, 1:J], ex[:, 1:J], ex[:, 0:J - 1], ALU.not_equal), a)
    cur, at, step = new, 0, 1
    while step < J:
        dst = run[at]
        q.dve(lambda e, cur=cur, dst=dst, step=step: e.tensor_copy(dst[:, 0:step], cur[:, 0:step]), a)
        a = q.dve(lambda e, cur=cur, dst=dst, step=step: e.tensor_tensor(
            dst[:, step:J], cur[:, step:J], cur[:, 0:J - step], ALU.add), a)
        cur, at, step = dst, 1 - at, 2 * step
    for least in range(W_BUFS * ((E - 1) // W_BUFS), 0, -W_BUFS):
        a = q.dve(lambda e, cur=cur, least=least: e.tensor_scalar(three[:, :], cur[:, :], float(least), -float(W_BUFS),
                                                     ALU.is_ge, ALU.mult), a)
        a = q.dve(lambda e, cur=cur: e.tensor_tensor(cur[:, :], cur[:, :], three[:, :], ALU.add), a)
    for i, src in enumerate((ex, new, cur)):
        a = q.dve(lambda e, i=i, src=src: e.tensor_copy(plan[0:1, i, :], src[:, :]), a)
    q.barrier()
    sb.close()


W_BUFS = 3
LEAD = W_BUFS - 1


def experts(m, xn1, slots, plan, weights, queue_x, queue_y):
    q = m.q
    sb = Arena(m.nc)
    WIDE = 2 * DC * F + FC * D
    w = sb("e_w", [P, W_BUFS, WIDE])
    x = sb("e_x", [P, 3, D])
    xT = sb("e_xT", [P, 2, DC, P])
    act = sb("e_act", [P, 2, F])
    hid = sb("e_hid", [P, 2, F])
    hT = sb("e_hT", [P, 2, FC, P])
    y = sb("e_y", [P, 2, D])
    J = MOE_TILES
    sent = []
    for k in range(2):
        for t in range(NT):
            sent.append(q.dma_by("gpsimd", "rows_out", lambda e, k=k, t=t: e.indirect_dma_start(
                out=queue_x, out_offset=bass.IndirectOffsetOnAxis(ap=slots[:, k, t:t + 1], axis=0),
                in_=xn1[:, t, :], in_offset=None), m.zeroed))
    sent = sent[-1]
    GU = m.psum[:, 0:2 * F].rearrange("p (a f) -> p a f", a=2)
    HT = m.psum[:, 2 * F:3 * F]
    XT = m.psum[:, 3 * F:3 * F + DC * P]
    Y = m.psum[:, 3 * F + HALF:3 * F + HALF + D]
    x_ring, xT_ring, act_ring, hid_ring, hT_ring, y_ring = Ring(3), Ring(2), Ring(2), Ring(2), Ring(2), Ring(2)
    buffer_of = {}

    def fetch(j, after):

        def emit(eng, j=j):
            expert = eng.value_load(plan[0:1, 0, j:j + 1], min_val=0, max_val=EXPERTS - 1)
            buf = eng.value_load(plan[0:1, 2, j:j + 1], min_val=0, max_val=W_BUFS - 1)
            more = {}
            if j:
                new = eng.value_load(plan[0:1, 1, j:j + 1], min_val=0, max_val=1)
                more = {"cond": new > 0}
            return eng.dma_start(w[:, bass.ds(buf, 1), :],
                                 weights[bass.ds(expert, 1), :, :].rearrange("e p n -> p e n"), **more)

        return q.dma_by("sync", f"weights_in{j % (LEAD + 1)}", emit, after)

    def load_rows(j):
        s, free = x_ring.take()
        return s, q.dma(f"rows_in{s}", x[:, s, :], queue_x[j * P:(j + 1) * P, :], sent, *free, queue="scalar")

    xT_free = [()]
    y_free = [()]

    def turn(s, got):
        for c in range(DC):
            tr = q.pe(lambda e, c=c, s=s: e.transpose(XT[:, c * P:(c + 1) * P], x[:, s, c * P:(c + 1) * P],
                                                      m.ident[:, :]), got, *xT_free[0])
        x_ring.free(s, tr)
        o, free = xT_ring.take()
        cp = q.dve(lambda e, o=o: e.tensor_copy(xT[:, o, :, :].rearrange("p c n -> p (c n)"), XT), tr, *free)
        xT_free[0] = (cp,)
        return o, cp

    def at_buffer(eng, j):
        if buffer_of.get("j") != j:
            buffer_of["j"] = j
            buffer_of["v"] = eng.value_load(plan[0:1, 2, j:j + 1], min_val=0, max_val=W_BUFS - 1)
        return buffer_of["v"]

    def up_product(j, which, o, ready, free):
        for half in range(F // HALF):
            for c in range(DC):
                at = (which * DC + c) * F + half * HALF

                def emit(e, j=j, o=o, c=c, at=at, half=half):
                    moving = w[:, bass.ds(at_buffer(e, j), 1), at:at + HALF].rearrange("p a n -> p (a n)")
                    return e.matmul(GU[:, which, half * HALF:(half + 1) * HALF], xT[:, o, c, :], moving,
                                    start=(c == 0), stop=(c == DC - 1))

                mm = q.pe(emit, *ready, *free)
        return mm

    def turn_hidden(hs, done, free):
        for f in range(FC):
            tr = q.pe(lambda e, f=f, hs=hs: e.transpose(HT[:, f * P:(f + 1) * P], hid[:, hs, f * P:(f + 1) * P],
                                                        m.ident[:, :]), *done, *free)
        return tr

    def down(j, ts, done):
        for f in range(FC):
            at = 2 * DC * F + f * D

            def emit(e, j=j, ts=ts, f=f, at=at):
                moving = w[:, bass.ds(at_buffer(e, j), 1), at:at + D].rearrange("p a n -> p (a n)")
                return e.matmul(Y, hT[:, ts, f, :], moving, start=(f == 0), stop=(f == FC - 1))

            mm = q.pe(emit, *done, *y_free[0])
        o, free = y_ring.take()
        cp = q.act(lambda e, o=o: e.activation(y[:, o, :], Y, ACT.Copy), mm, *free)
        y_free[0] = (cp,)
        y_ring.free(o, q.dma(f"y_out{o}", queue_y[j * P:(j + 1) * P, :], y[:, o, :], cp, queue="scalar"))
        return mm

    weights_got = {j: fetch(j, None) for j in range(LEAD)}
    rows = {j: load_rows(j) for j in range(2)}
    turned = {0: turn(*rows.pop(0))}
    g_free = u_free = ()
    hT_psum_free = ()
    pending = None
    down_done = {}
    for j in range(J):
        o, xready = turned.pop(j)
        ready = (xready, weights_got[j])
        if j + 2 < J:
            rows[j + 2] = load_rows(j + 2)
        g = up_product(j, 0, o, ready, g_free)
        a_s, a_free = act_ring.take()
        sg = q.act(lambda e, a_s=a_s: e.activation(act[:, a_s, :], GU[:, 0, :], ACT.Silu), g, *a_free)
        g_free = (sg,)
        if pending is not None:
            tr = turn_hidden(pending[1], pending[2], hT_psum_free)
            ts, t_free = hT_ring.take()
            flat = hT[:, ts, :, :].rearrange("p f n -> p (f n)")
            c1 = q.dve(lambda e, flat=flat: e.tensor_copy(flat, HT), tr, *t_free)
            hid_ring.free(pending[1], tr)
            hT_psum_free = (c1,)
        u = up_product(j, 1, o, ready, u_free)
        xT_ring.free(o, u)
        h_s, h_free = hid_ring.take()
        hd = q.dve(lambda e, a_s=a_s, h_s=h_s: e.tensor_tensor(hid[:, h_s, :], act[:, a_s, :], GU[:, 1, :],
                                                              ALU.mult), sg, u, *h_free)
        u_free = (hd,)
        act_ring.free(a_s, hd)
        if j + 1 < J:
            turned[j + 1] = turn(*rows.pop(j + 1))
        if pending is not None:
            dd = down(pending[0], ts, (c1,))
            hT_ring.free(ts, dd)
            down_done[pending[0]] = dd
        if j + LEAD < J:
            weights_got[j + LEAD] = fetch(j + LEAD, down_done.get(j - 1))
        pending = (j, h_s, (hd,))
    tr = turn_hidden(pending[1], pending[2], hT_psum_free)
    ts, t_free = hT_ring.take()
    flat = hT[:, ts, :, :].rearrange("p f n -> p (f n)")
    c1 = q.dve(lambda e, flat=flat: e.tensor_copy(flat, HT), tr, *t_free)
    down(pending[0], ts, (c1,))
    q.barrier()
    sb.close()


def combine_tokens(m, sb, x1_dram, x2_dram, pi, slots, queue_y):
    q = m.q
    x1_src = x1_dram.rearrange("(b t p) d -> b p t d", p=P, t=BT)
    x2_dst = x2_dram.rearrange("(b t p) d -> b p t d", p=P, t=BT)
    rows = [sb(f"g_rows{k}", [P, 2, BT, D]) for k in range(2)]
    rings = [Ring(2), Ring(2)]

    def open_batch(b, slot, x, free):
        got = q.dma(f"x1_in{slot}", x, x1_src[b, :, :, :], *free)
        for k in range(2):
            r, r_free = rings[k].take()
            for i in range(BT):
                t = b * BT + i
                here = q.dma_by("gpsimd", f"rows_back{k}{r}", lambda e, k=k, r=r, i=i, t=t: e.indirect_dma_start(
                    out=rows[k][:, r, i, :], out_offset=None, in_=queue_y,
                    in_offset=bass.IndirectOffsetOnAxis(ap=slots[:, k, t:t + 1], axis=0)), *r_free)
            for i in range(BT):
                t = b * BT + i
                done = q.dve(lambda e, k=k, r=r, i=i, t=t, x=x: e.scalar_tensor_tensor(
                    out=x[:, i, :], in0=rows[k][:, r, i, :], scalar=pi[:, t, k:k + 1], in1=x[:, i, :],
                    op0=ALU.mult, op1=ALU.add), here, got)
            rings[k].free(r, done)
            got = done
        return done, (q.dma(f"x2_out{slot}", x2_dst[b, :, :, :], x, done),)

    return open_batch


def bias_tables(m, amplitudes, sharpness, offsets, tables_dram, table_range):
    q = m.q
    sb = Arena(m.nc)
    terms = 21
    groups = 3
    R = H * terms // groups
    W = 2 * S
    coef = sb("b_coef", [R, 3, groups])
    mask = sb("b_mask", [R, groups, H])
    rel = sb("b_rel", [R, W])
    d = sb("b_d", [R, groups, W])
    table = sb("b_table", [H, W])
    mirror = sb("b_mirror", [H, W])
    ends = sb("b_ends", [H, 2])
    ends_row = sb("b_ends_row", [1, 2, H])
    for i, src in enumerate((amplitudes, sharpness, offsets)):
        got = q.dma("coef_in", coef[:, i, :], src)
    a = q.pool(lambda e: e.memset(mask[:, :, :], 1.0))
    a = q.pool(lambda e: e.affine_select(out=mask[:, :, :], in_=mask[:, :, :], compare_op=ALU.is_ge, fill=0.0,
                                         base=0, pattern=[[R, groups], [-terms, H]], channel_multiplier=1), a)
    a = q.pool(lambda e: e.affine_select(out=mask[:, :, :], in_=mask[:, :, :], compare_op=ALU.is_ge, fill=0.0,
                                         base=terms - 1, pattern=[[-R, groups], [terms, H]],
                                         channel_multiplier=-1), a)
    i0 = q.pool(lambda e: e.iota(rel[:, :], pattern=[[1, W]], base=-(S - 1), channel_multiplier=0,
                                 allow_small_or_imprecise_dtypes=True))
    sharp = sb("b_sharp", [R, groups])
    s1 = q.dve(lambda e: e.tensor_scalar(sharp[:, :], coef[:, 1, :], -1.0, None, ALU.mult), got)
    s1 = q.dve(lambda e: e.tensor_tensor(sharp[:, :], sharp[:, :], coef[:, 1, :], ALU.min), s1)
    masked = a
    for g in range(groups):
        mk = q.dve(lambda e, g=g: e.tensor_scalar(mask[:, g, :], mask[:, g, :], coef[:, 0, g:g + 1], None, ALU.mult), masked, got)
        a = q.dve(lambda e, g=g: e.tensor_scalar(d[:, g, :], rel[:, :], coef[:, 2, g:g + 1], None, ALU.subtract), i0, got)
        a = q.dve(lambda e, g=g: e.scalar_tensor_tensor(out=d[:, g, :], in0=d[:, g, :], scalar=sharp[:, g:g + 1],
                                                        in1=d[:, g, :], op0=ALU.mult, op1=ALU.mult), a, s1)
        ex = q.act(lambda e, g=g: e.activation(d[:, g, :], d[:, g, :], ACT.Exp), a)
    for j in range(W // HALF):
        for g in range(groups):
            mm = q.pe(lambda e, j=j, g=g: e.matmul(m.psum[0:H, j * HALF:(j + 1) * HALF], mask[:, g, :],
                                                   d[:, g, j * HALF:(j + 1) * HALF], start=(g == 0),
                                                   stop=(g == groups - 1)), ex, mk)
    L = W - 1
    t1 = q.dve(lambda e: e.tensor_copy(table[:, :], m.psum[0:H, 0:W]), mm)
    t2 = q.dve(lambda e: e.tensor_copy(mirror[:, 0:L], table[:, 0:L][:, ::-1]), t1)
    t2 = q.dve(lambda e: e.tensor_copy(mirror[:, L:W], table[:, L:W]), t2)
    q.dma("tables_out", tables_dram[0, :, :], table[:, :], t1)
    q.dma("tables_out", tables_dram[1, :, :], mirror[:, :], t2)
    x1 = q.dve(lambda e: e.reduce_max(ends[:, 0:1], table[:, 0:L], AX.X), t2)
    x2 = q.dve(lambda e: e.tensor_reduce(out=ends[:, 1:2], in_=table[:, 0:L], axis=AX.X, op=ALU.min, negate=True), x1)
    for k in range(2):
        tr = q.pe(lambda e, k=k: e.transpose(m.psum[0:1, W + k * H:W + (k + 1) * H], ends[:, k:k + 1],
                                             m.ident[0:H, 0:H]), x2)
    a = q.dve(lambda e: e.tensor_copy(ends_row[:, :, :].rearrange("a k h -> a (k h)"),
                                      m.psum[0:1, W:W + 2 * H]), tr)
    a = q.dve(lambda e: e.reduce_max(table_range[:, :], ends_row[:, :, :], AX.X), a)
    q.dve(lambda e: e.tensor_scalar(table_range[:, :], table_range[:, :], 0.0, None, ALU.max), a)
    q.barrier()
    sb.close()


FP8_MAX = 448.0


def close_second_layer(m, om, x2_dram, wg_dram, bg_dram, w8_dram, b8_dram, scales_dram, out_dram):
    q = m.q
    sb = Arena(m.nc)
    wg = sb("f_wg", [P, DC, 2 * D])
    bg = sb("f_bg", [P, 2 * D])
    w8 = sb("f_w8", [P, DC, D])
    b8 = sb("f_b8", [P, D])
    sc = sb("f_sc", [P, 2])
    omT = sb("f_omT", [P, DC, S])
    x = sb("f_x", [P, 2, BT, D])
    gated = sb("f_gated", [P, 2, BT, D])
    xn = sb("f_xn", [P, BT, D])
    step = sb("f_step", [P, BT, D])
    xqT = sb("f_xqT", [P, DC, S])
    lnw = layernorm_scratch(sb, "f_")
    q.dma("f_w_in", wg[:, :, :], wg_dram.rearrange("(c p) n -> p c n", p=P))
    q.dma("f_w_in", w8[:, :, :], w8_dram.rearrange("(c p) n -> p c n", p=P))
    q.dma("f_w_in", bg[:, :], across(bg_dram, P))
    q.dma("f_w_in", b8[:, :], across(b8_dram, P))
    got_w = q.dma("f_w_in", sc[:, :], across(scales_dram, P))
    inv = sb("f_inv", [P, 1])
    r = q.dve(lambda e: e.reciprocal(inv[:, :], sc[:, 0:1]), got_w)
    w8s = q.dve(lambda e: e.tensor_scalar(w8[:, :, :], w8[:, :, :], sc[:, 1:2], None, ALU.mult), got_w)
    ring = Ring(4)
    x_ring, gated_ring = Ring(2), Ring(2)
    x2_src = x2_dram.rearrange("(b t p) d -> b p t d", p=P, t=BT)
    out_dst = out_dram.rearrange("(b t p) d -> b p t d", p=P, t=BT)
    omT_free = xqT_free = step_free = ()
    for b in range(B):
        s, free = x_ring.take()
        got = q.dma(f"x2_in{s}", x[:, s, :, :], x2_src[b, :, :, :], *free)
        made = transpose_batch(m, ring, om[:, b * BT:(b + 1) * BT, :], omT[:, :, :], None, omT_free)
        g_s, g_free = gated_ring.take()
        sig = gated[:, g_s, :, :]
        for i in range(0, BT, 2):
            slot, free = ring.take()
            ps = m.psum[:, slot * S:(slot + 1) * S].rearrange("p (t n) -> p t n", n=2 * D)
            for t in (i, i + 1):
                for k in range(DC):
                    mm = q.pe(lambda e, t=t, i=i, k=k, ps=ps: e.matmul(
                        ps[:, t - i, :], omT[:, k, t * P:(t + 1) * P], wg[:, k, :], start=(k == 0),
                        stop=(k == DC - 1)), *made, got_w, *free)
            d1 = q.dve(lambda e, i=i, ps=ps: e.tensor_tensor(step[:, i:i + 2, :], ps[:, :, 0:D],
                                                             repeat(bg[:, 0:D], 2), ALU.add), mm, *step_free)
            d2 = q.dve(lambda e, i=i, ps=ps, sig=sig: e.tensor_tensor(sig[:, i:i + 2, :], ps[:, :, D:2 * D],
                                                                      repeat(bg[:, D:2 * D], 2), ALU.add),
                       mm, *g_free)
            ring.free(slot, d2)
        omT_free = (mm,)
        sg = q.act(lambda e, sig=sig: e.activation(sig, sig, ACT.Sigmoid), d2)
        a = q.dve(lambda e, sig=sig: e.tensor_tensor(sig, sig, step[:, :, :], ALU.mult), sg, d1)
        x3 = x[:, s, :, :]
        a = q.dve(lambda e, sig=sig, x3=x3: e.tensor_tensor(x3, x3, sig, ALU.add), a, got)
        gated_ring.free(g_s, a)
        a = layernorm(m, lnw, x3, xn[:, :, :], a)
        a = q.dve(lambda e: e.tensor_scalar(xn[:, :, :], xn[:, :, :], inv[:, 0:1], FP8_MAX, ALU.mult, ALU.min), r, a)
        a = q.dve(lambda e: e.tensor_scalar(xn[:, :, :], xn[:, :, :], -FP8_MAX, None, ALU.max), a)
        a = q.dve(lambda e: e.tensor_scalar(step[:, :, :].bitcast(I32), xn[:, :, :].bitcast(I32), 0x7F800000,
                                            None, ALU.bitwise_and), a)
        a = q.dve(lambda e: e.tensor_scalar(step[:, :, :], step[:, :, :], 2.0 ** -6, 1.5 * 2.0 ** 20,
                                            ALU.max, ALU.mult), a)
        a = q.dve(lambda e: e.tensor_tensor(xn[:, :, :], xn[:, :, :], step[:, :, :], ALU.add), a)
        a = q.dve(lambda e: e.tensor_tensor(xn[:, :, :], xn[:, :, :], step[:, :, :], ALU.subtract), a)
        step_free = (a,)
        a = q.dve(lambda e: e.tensor_scalar(xn[:, :, :], xn[:, :, :], sc[:, 0:1], None, ALU.mult), a)
        made = transpose_batch(m, ring, xn, xqT[:, :, :], a, xqT_free)
        xb = q.pool(lambda e, x3=x3: e.tensor_tensor(x3, x3, repeat(b8[:, :], BT), ALU.add), a)
        for half in range(2):
            slot, free = ring.take()
            ps = m.psum[:, slot * S:(slot + 1) * S]
            for i in range(BT // 2):
                t = half * (BT // 2) + i
                for k in range(DC):
                    mm = q.pe(lambda e, i=i, t=t, k=k, ps=ps: e.matmul(
                        ps[:, i * D:(i + 1) * D], xqT[:, k, t * P:(t + 1) * P], w8[:, k, :],
                        start=(k == 0), stop=(k == DC - 1)), *made, w8s, *free)
            h0 = half * (BT // 2)
            a = q.dve(lambda e, x3=x3, h0=h0, ps=ps: e.tensor_tensor(
                x3[:, h0:h0 + BT // 2, :], ps.rearrange("p (t d) -> p t d", d=D), x3[:, h0:h0 + BT // 2, :],
                ALU.add), mm, xb)
            ring.free(slot, a)
        xqT_free = (mm,)
        x_ring.free(s, q.dma(f"out{s}", out_dst[b, :, :, :], x3, a))
    q.barrier()
    sb.close()


def build_program(nc, ctx, t, out_dram):
    m = Machine()
    m.nc, m.q, m.keep = nc, Queues(nc, ctx), Arena(nc)
    q = m.q
    m.psum = ctx.enter_context(nc.psum_tensor("psum", [P, 8 * HALF], FP32))[:, :]

    def scratch(name, shape, dtype=FP32):
        return nc.dram_tensor(name, shape, dtype, kind="Internal").ap()

    parts = scratch("qk_parts", [2, 3, B, D, S], BF16)
    x1_dram, x2_dram = scratch("x1", [N, D]), scratch("x2", [N, D])
    queue_x, queue_y = scratch("queue_x", [MOE_TILES * P, D]), scratch("queue_y", [MOE_TILES * P, D])
    tables = scratch("tables", [2, H, 2 * S])

    make_constants(m)
    m.norms = m.keep("norms", [H // DC, 2, DC * B])
    m.bound = m.keep("bound", [H // DC, 16])
    m.shift = m.keep("shift", [P, 1])
    m.flag = m.keep("flag", [1, 1], I32)
    table_range = m.keep("table_range", [1, 2])
    la = m.keep("la", [P, NT, EXPERTS])
    pi = m.keep("pi", [P, NT, EXPERTS])
    slots = m.keep("slots", [P, 2, NT], I32)
    plan = m.keep("plan", [1, 3, MOE_TILES], I32)
    zeros = m.keep("zeros", [P, D])
    z = q.pool(lambda e: e.memset(zeros[:, :], 0.0))
    m.zeroed = q.dma("zeros_out", queue_x.rearrange("(j p) d -> p j d", p=P), repeat(zeros[:, :], MOE_TILES), z)

    def attend(layer, om, tables, order):
        main = m.q
        paths = []
        for row_max in (False, True):
            m.q = Queues(nc, ctx, f"a{layer}{'rowmax' if row_max else 'shift'}")
            attention(m, layer, parts, tables, om, order, row_max)
            paths.append(m.q)
        m.q = main
        main.either(m.flag[0:1, 0:1], *paths)
        main.barrier()

    bias_tables(m, t["amplitudes"], t["sharpness"], t["offsets"], tables, table_range)

    kept = Arena(nc)
    xn1 = kept("xn1", [P, NT, D])
    first = Arena(nc)
    m.v = first("v0", [P, NT, H * VW + HD])
    om = first("om0", [P, NT, D])
    project(m, 0, load_tokens(m, t["x"]), [t["wq"], t["wk"], t["wv"]], [t["bq"], t["bk"], t["bv"]], parts)
    score_bound(m, 0, None)
    q.barrier()
    attend(0, om, None, [(g, b) for b in range(B) for g in range(NG)])
    close_first_attention(m, om, t["x"], t["wo"], t["bo"], t["gate"], x1_dram, xn1, la)
    first.close()

    sinkhorn(m, la, pi)
    route(m, pi, slots, plan)
    experts(m, xn1, slots, plan, t["experts"], queue_x, queue_y)
    kept.close()

    second = Arena(nc)
    m.v = second("v1", [P, NT, H * VW + HD])
    om = second("om1", [P, NT, D])
    gather = Arena(nc)
    project(m, 1, combine_tokens(m, gather, x1_dram, x2_dram, pi, slots, queue_y),
            [t["w_q"], t["w_k"], t["w_v"]], None, parts)
    gather.close()
    score_bound(m, 1, table_range[:, :])
    q.barrier()
    attend(1, om, tables, [(g, b) for g in range(NG) for b in range(B)])
    close_second_layer(m, om, x2_dram, t["w_gate"], t["b_gate"], t["w8"], t["b8"], t["scales"], out_dram)
    second.close()
    q.emit()


def kernel(**inputs):
    import numpy as np
    import concourse.bacc as bacc
    from concourse import mybir
    from concourse.bass_utils import run_bass_kernel_spmd

    a = {k: np.asarray(v) for k, v in inputs.items()}

    def circulant(c):
        n = np.arange(D)
        return c[(n[None, :] - n[:, None]) % D]

    def by_chunk(v):
        return v.reshape(-1, P).T

    def by_rows(v):
        return v.reshape(3, -1).T

    def expert_rows(wg, wu, wd):
        up = [w.transpose(0, 2, 1).reshape(EXPERTS, DC, P, F).transpose(0, 2, 1, 3).reshape(EXPERTS, P, -1)
              for w in (wg, wu)]
        down = wd.transpose(0, 2, 1).reshape(EXPERTS, FC, P, D).transpose(0, 2, 1, 3).reshape(EXPERTS, P, -1)
        return np.concatenate([*up, down], axis=2)

    w_in = a["L1_attn_w_in"]
    laid = {
        "x": a["L0_attn_x"].reshape(N, D),
        **{f"w{i}": circulant(a[f"L0_attn_w{i}_c"]) for i in "qkvo"},
        **{f"b{i}": by_chunk(a[f"L0_attn_w{i}_b"]) for i in "qk"},
        **{f"b{i}": a[f"L0_attn_w{i}_b"] for i in "vo"},
        "gate": a["L0_ffn_gate_W"].T,
        "experts": expert_rows(a["L0_ffn_W_gate"], a["L0_ffn_W_up"], a["L0_ffn_W_down"]),
        "w_k": w_in[:, 0:D], "w_v": w_in[:, D:2 * D], "w_q": w_in[:, 2 * D:3 * D],
        "w_gate": a["L1_attn_w_gate"], "b_gate": a["L1_attn_b_gate"],
        "amplitudes": by_rows(a["L1_attn_amplitudes"]), "sharpness": by_rows(a["L1_attn_sharpness"]),
        "offsets": by_rows(a["L1_attn_offsets"]),
        "w8": a["L1_ffn_weight_fp8"].T, "b8": a["L1_ffn_bias"],
        "scales": np.concatenate([a["L1_ffn_input_scale"], a["L1_ffn_weight_scale"]]),
    }
    nc = bacc.Bacc("TRN2", target_bir_lowering=False, num_devices=1)
    arrays, tensors = {}, {}
    for name, value in laid.items():
        value = np.ascontiguousarray(value)
        arrays[f"in_{name}"] = value
        tensors[name] = nc.dram_tensor(f"in_{name}", value.shape, mybir.dt.from_np(value.dtype),
                                       kind="ExternalInput").ap()
    out = nc.dram_tensor("out_x", [N, D], FP32, kind="ExternalOutput").ap()
    with ExitStack() as ctx:
        build_program(nc, ctx, tensors, out)
    result = run_bass_kernel_spmd(nc, [arrays], core_ids=[0])
    return result.results[0]["out_x"].reshape(B, S, D)
```

```python
import numpy as np
from contextlib import ExitStack

import concourse.bass as bass
from concourse import mybir

FP32 = mybir.dt.float32
BF16 = mybir.dt.bfloat16
I32 = mybir.dt.int32
ALU = mybir.AluOpType
ACT = mybir.ActivationFunctionType
AX = mybir.AxisListType

P = 128
B, S, D = 4, 1024, 256
N = B * S
NT = N // P
BT = S // P
DC = D // P
H, HD = 16, 16
GH = 4
NG = H // GH
VW = HD + 1
EXPERTS, F = 8, 1024
FC = F // P
LN_EPS = 1e-5
SINKHORN_EPS, SINKHORN_ITERS = 0.05, 20
MOE_TILES = 2 * NT + EXPERTS - 1
SCORE_SCALE = HD ** -0.5
HALF = 512
Q_SLOTS = (0, 0, 0, 1, 1, 2)
K_SLOTS = (0, 1, 2, 0, 1, 0)
QK_ROWS = len(Q_SLOTS) * HD
MAX_PARTS = 3
FAST_RANGE = 60.0
TINY = 1.1754944e-38


class Done:

    def __init__(self, sem, step):
        self.sem, self.step, self.needed, self.value = sem, step, False, None


class Sem:

    def __init__(self, handle):
        self.handle, self.marks = handle, []

    def mark(self, step=1):
        done = Done(self, step)
        self.marks.append(done)
        return done

    def number(self):
        count = 0
        for done in self.marks:
            if done.needed or done.step > 1:
                count += done.step
                done.value = count


class Queues:

    ENGINES = ("tensor", "vector", "scalar", "gpsimd", "sync")

    def __init__(self, nc, ctx, name="main"):
        self.nc, self.ctx, self.name = nc, ctx, name
        self.steps = {e: [] for e in self.ENGINES}
        self.done = {e: Sem(ctx.enter_context(nc.semaphore(f"{name}_{e}_done"))) for e in self.ENGINES}
        self.lanes = {}
        self.branches = []

    def _queue(self, engine, emit, after, done):
        waits = []
        for a in after:
            if a is not None:
                a.needed = True
                waits.append(a)
        self.steps[engine].append((emit, waits, done))
        return done

    def pe(self, emit, *after):
        return self._queue("tensor", emit, after, self.done["tensor"].mark())

    def dve(self, emit, *after):
        return self._queue("vector", emit, after, self.done["vector"].mark())

    def act(self, emit, *after):
        return self._queue("scalar", emit, after, self.done["scalar"].mark())

    def pool(self, emit, *after):
        return self._queue("gpsimd", emit, after, self.done["gpsimd"].mark())

    def lane(self, name):
        if name not in self.lanes:
            self.lanes[name] = Sem(self.ctx.enter_context(self.nc.semaphore(f"{self.name}_{name}")))
        return self.lanes[name]

    def dma(self, lane, out, in_, *after, queue="sync"):
        done = self.lane(lane).mark(16)
        return self._queue(queue, lambda e: e.dma_start(out, in_), after, done)

    def dma_by(self, queue, lane, emit, *after):
        return self._queue(queue, emit, after, self.lane(lane).mark(16))

    def load_tables(self, name):
        self.steps["scalar"].append((lambda e: e.preload_act_table_set(name), [], None))

    def either(self, flag, if_set, if_clear):
        self.branches += [if_set, if_clear]
        for name in self.ENGINES:

            def emit(eng, name=name):
                is_set = eng.value_load(flag, min_val=0, max_val=1)
                with eng.If(is_set > 0):
                    if_set.play(eng, name)
                with eng.If(is_set < 1):
                    if_clear.play(eng, name)

            self.steps[name].append((emit, [], None))

    def barrier(self):
        arrived = [self._queue(e, lambda eng: eng.drain(), (), self.done[e].mark()) for e in self.ENGINES]
        arrived += [lane.marks[-1] for lane in self.lanes.values() if lane.marks]
        for e in self.ENGINES:
            self._queue(e, None, arrived, None)

    def number(self):
        for sem in [*self.done.values(), *self.lanes.values()]:
            sem.number()
        for branch in self.branches:
            branch.number()

    def play(self, eng, name):
        waited = {}
        for emit, waits, done in self.steps[name]:
            for w in waits:
                if waited.get(w.sem, 0) < w.value:
                    eng.wait_ge(w.sem.handle, w.value)
                    waited[w.sem] = w.value
            if emit is not None:
                instruction = emit(eng)
                if done is not None and (done.needed or done.step > 1):
                    instruction.then_inc(done.sem.handle, done.step)

    def emit(self):
        self.number()
        block = self.ctx.enter_context(self.nc.Block())
        block.tensor(lambda eng: self.play(eng, "tensor"))
        block.vector(lambda eng: self.play(eng, "vector"))
        block.scalar(lambda eng: self.play(eng, "scalar"))
        block.gpsimd(lambda eng: self.play(eng, "gpsimd"))
        block.sync(lambda eng: self.play(eng, "sync"))


LN_EXP = "natural_log_exp_and_others"


class Ring:

    def __init__(self, n):
        self.n, self.at, self.readers = n, 0, [()] * n

    def take(self):
        slot = self.at
        self.at = (slot + 1) % self.n
        return slot, self.readers[slot]

    def free(self, slot, *readers):
        self.readers[slot] = readers


class Arena:

    def __init__(self, nc):
        self.nc, self.stack = nc, ExitStack()

    def __call__(self, name, shape, dtype=FP32):
        return self.stack.enter_context(self.nc.sbuf_tensor(name, shape, dtype))

    def close(self):
        self.stack.close()


class Machine:
    pass


def make_constants(m):
    q, sb = m.q, m.keep
    m.ident = sb("ident", [P, P])
    m.ident16 = sb("ident16", [P, P], BF16)
    m.ones = sb("ones", [P, P])
    m.head_ones = sb("head_ones", [P, P // HD], BF16)
    m.ones16 = sb("ones16", [P, P // HD], BF16)
    m.before = sb("before", [P, P])
    z = q.pool(lambda e: e.memset(m.ident[:, :], 0.0))
    z16 = q.pool(lambda e: e.memset(m.ident16[:, :], 0.0))
    o = q.pool(lambda e: e.memset(m.ones[:, :], 1.0))
    o16 = q.pool(lambda e: e.memset(m.ones16[:, :], 1.0))
    i1 = q.pool(lambda e: e.affine_select(out=m.ident[:, :], in_=m.ident[:, :], compare_op=ALU.not_equal,
                                          fill=1.0, base=0, pattern=[[-1, P]], channel_multiplier=1), z)
    i2 = q.pool(lambda e: e.affine_select(out=m.ident16[:, :], in_=m.ident16[:, :],
                                          compare_op=ALU.not_equal, fill=1.0, base=0,
                                          pattern=[[-1, P]], channel_multiplier=1), z16)
    h1 = q.pool(lambda e: e.affine_select(out=m.head_ones[:, :], in_=m.ones16[:, :],
                                          compare_op=ALU.is_ge, fill=0.0, base=0,
                                          pattern=[[-HD, P // HD]], channel_multiplier=1), o16)
    h2 = q.pool(lambda e: e.affine_select(out=m.head_ones[:, :], in_=m.head_ones[:, :],
                                          compare_op=ALU.is_ge, fill=0.0, base=HD - 1,
                                          pattern=[[HD, P // HD]], channel_multiplier=-1), h1)
    b1 = q.pool(lambda e: e.affine_select(out=m.before[:, :], in_=m.ones[:, :], compare_op=ALU.is_ge,
                                          fill=0.0, base=-1, pattern=[[1, P]], channel_multiplier=-1), o)
    m.constants = q.pool(lambda e: e.memset(m.ones16[:, :], 1.0), i1, i2, h2, b1)


def across(row, parts):
    return bass.AP(tensor=row.tensor, offset=row.offset, ap=[[0, parts], *[list(x) for x in row.ap]])


def layernorm(m, w, x, xn, *ready, factor=None):
    q = m.q
    stats, mv, v, y, t = w["stats"], w["mv"], w["v"], w["y"], w["t"]
    marks = [q.dve(lambda e, i=i: e.bn_stats(stats[:, i, :], x[:, i, :]), *ready) for i in range(BT)]
    marks = [q.dve(lambda e, i=i: e.bn_aggr(mv[:, i, :], stats[:, i, :]), marks[i]) for i in range(BT)]
    v1 = q.dve(lambda e: e.tensor_scalar(v[:, :], mv[:, :, 1], LN_EPS, None, ALU.add), marks[-1])
    l = q.act(lambda e: e.activation(y[:, :], v[:, :], ACT.Ln), v1)
    l = q.act(lambda e: e.activation(y[:, :], y[:, :], ACT.Exp, scale=-0.5), l)
    a = q.dve(lambda e: e.tensor_tensor(t[:, :], y[:, :], y[:, :], ALU.mult), l)
    a = q.dve(lambda e: e.tensor_tensor(t[:, :], t[:, :], v[:, :], ALU.mult), a)
    a = q.dve(lambda e: e.tensor_scalar(t[:, :], t[:, :], -0.5, 1.5, ALU.mult, ALU.add), a)
    a = q.dve(lambda e: e.tensor_tensor(y[:, :], y[:, :], t[:, :], ALU.mult), a)
    if factor is not None:
        a = q.dve(lambda e: e.tensor_scalar(y[:, :], y[:, :], factor, None, ALU.mult), a)
    for i in range(BT):
        last = q.dve(lambda e, i=i: e.tensor_scalar(xn[:, i, :], x[:, i, :], mv[:, i, 0:1], y[:, i:i + 1],
                                                    ALU.subtract, ALU.mult), a)
    return last


def layernorm_scratch(sb, name):
    return {"stats": sb(name + "stats", [P, BT, 6]), "mv": sb(name + "mv", [P, BT, 2]),
            "v": sb(name + "v", [P, BT]), "y": sb(name + "y", [P, BT]), "t": sb(name + "t", [P, BT])}


def transpose_batch(m, ring, src, dst, ready, dst_free=()):
    q = m.q
    out = []
    for c in range(DC):
        slot, free = ring.take()
        ps = m.psum[:, slot * S:(slot + 1) * S]
        for t in range(BT):
            tr = q.pe(lambda e, t=t, c=c, ps=ps: e.transpose(ps[:, t * P:(t + 1) * P],
                                                             src[:, t, c * P:(c + 1) * P], m.ident[:, :]),
                      ready, m.constants, *free)
        cp = q.act(lambda e, c=c, ps=ps: e.activation(dst[:, c, :], ps, ACT.Copy), tr, *dst_free)
        ring.free(slot, cp)
        out.append(cp)
    return out


def project(m, layer, open_batch, weights, biases, parts):
    q, nc = m.q, m.nc
    sb = Arena(nc)
    n = f"L{layer}_"
    w = [sb(n + f"w{i}", [P, DC, D]) for i in range(3)]
    b_qk = sb(n + "b_qk", [P, 2, DC])
    b_v = sb(n + "b_v", [P, D])
    x = sb(n + "x", [P, 2, BT, D])
    xn = sb(n + "xn", [P, 2, BT, D])
    xT = sb(n + "xT", [P, 2, DC, S])
    split = [sb(n + f"part{i}", [P, 2, S], BF16) for i in range(3)]
    rest = sb(n + "rest", [P, 2, S])
    square = sb(n + "square", [P, 2, S], BF16)
    lnw = layernorm_scratch(sb, n)
    nmax = m.norms

    got_w = [q.dma(n + "w_in", w[i][:, :, :], weights[i].rearrange("(c p) n -> p c n", p=P), queue="scalar")
             for i in range(3)][-1]
    if biases is None:
        zb = q.dve(lambda e: e.memset(b_qk[:, :, :], 0.0))
        zv = q.dve(lambda e: e.memset(b_v[:, :], 0.0))
        bias_ready = (zb, zv)
    else:
        for i in range(2):
            last = q.dma(n + "b_in", b_qk[:, i, :], biases[i], queue="scalar")
        last = q.dma(n + "b_in", b_v[:, :], across(biases[2], P), queue="scalar")
        bias_ready = (last,)
    ones_in = q.pool(lambda e: e.memset(m.v[:, :, :], 1.0))

    ring = Ring(4)
    x_ring, xT_ring, part_ring, rest_ring, square_ring = Ring(2), Ring(2), Ring(2), Ring(2), Ring(2)

    def fetch(b):
        xs, free = x_ring.take()
        return xs, open_batch(b, xs, x[:, xs, :, :], free)

    def normalise(fetched):
        xs, combine = fetched
        got, kept = combine()
        return xs, kept, layernorm(m, lnw, x[:, xs, :, :], xn[:, xs, :, :], got)

    def turn(xs, kept, normed):
        ts, t_free = xT_ring.take()
        made = transpose_batch(m, ring, xn[:, xs, :, :], xT[:, ts, :, :], normed, t_free)
        x_ring.free(xs, *made, *kept)
        return ts, made

    ahead = turn(*normalise(fetch(0)))
    fetched = fetch(1)
    waiting = []
    for b in range(B):
        ts, made = ahead
        if b + 1 < B:
            normal = normalise(fetched)
        for op in range(2):
            for c in range(DC):
                slot, free = ring.take()
                ps = m.psum[:, slot * S:(slot + 1) * S]
                for j in range(S // HALF):
                    for k in range(DC):
                        mm = q.pe(lambda e, op=op, c=c, j=j, k=k, ps=ps, ts=ts: e.matmul(
                            ps[:, j * HALF:(j + 1) * HALF], w[op][:, k, c * P:(c + 1) * P],
                            xT[:, ts, k, j * HALF:(j + 1) * HALF], start=(k == 0), stop=(k == DC - 1)),
                            got_w, *made, *free)
                bias = b_qk[:, op, c:c + 1]
                s, s_free = part_ring.take()
                hi = q.act(lambda e, s=s, ps=ps, bias=bias: e.activation(split[0][:, s, :], ps, ACT.Identity,
                                                                         bias=bias), mm, *bias_ready, *s_free)
                z, z_free = square_ring.take()
                sq = q.act(lambda e, z=z, s=s: e.activation(square[:, z, :], split[0][:, s, :], ACT.Square),
                           hi, *z_free)
                r, r_free = rest_ring.take()
                rs = q.dve(lambda e, s=s, r=r, ps=ps, bias=bias: e.scalar_tensor_tensor(
                    out=rest[:, r, :], in0=ps, scalar=bias, in1=split[0][:, s, :], op0=ALU.add,
                    op1=ALU.subtract), hi, *r_free)
                ring.free(slot, rs)
                mid = q.act(lambda e, s=s, r=r: e.activation(split[1][:, s, :], rest[:, r, :], ACT.Copy), rs)
                low = q.pool(lambda e, s=s, r=r: e.tensor_tensor(split[2][:, s, :], rest[:, r, :],
                                                                 split[1][:, s, :], ALU.subtract), mid, *s_free)
                rest_ring.free(r, low)
                sent = [q.dma(n + f"part_out{s}", parts[op, i, b, c * P:(c + 1) * P, :], split[i][:, s, :], done)
                        for i, done in enumerate((hi, mid, low))][-1]
                part_ring.free(s, sent, sq)

                def norms(op=op, c=c, b=b, z=z, sq=sq):
                    nslot, n_free = ring.take()
                    nps = m.psum[0:P // HD, nslot * S:(nslot + 1) * S]
                    for j in range(S // HALF):
                        nm = q.pe(lambda e, j=j: e.matmul(
                            nps[:, j * HALF:(j + 1) * HALF], m.head_ones[:, :],
                            square[:, z, j * HALF:(j + 1) * HALF], start=True, stop=True), sq, *n_free)
                    square_ring.free(z, nm)
                    mx = q.dve(lambda e: e.reduce_max(nmax[:, op, c * B + b:c * B + b + 1], nps, AX.X), nm)
                    ring.free(nslot, mx)

                if waiting:
                    waiting.pop(0)()
                waiting.append(norms)
        if b + 1 < B:
            ahead = turn(*normal)
        if b + 2 < B:
            fetched = fetch(b + 2)
        for half in range(2):
            slot, free = ring.take()
            ps = m.psum[:, slot * S:(slot + 1) * S]
            for i in range(BT // 2):
                t = half * (BT // 2) + i
                for k in range(DC):
                    mm = q.pe(lambda e, i=i, t=t, k=k, ps=ps, ts=ts: e.matmul(
                        ps[:, i * D:(i + 1) * D], xT[:, ts, k, t * P:(t + 1) * P], w[2][:, k, :],
                        start=(k == 0), stop=(k == DC - 1)), *free)
            t0 = b * BT + half * (BT // 2)
            for i in range(BT // 2):
                vd = q.dve(lambda e, i=i, t0=t0, ps=ps: e.tensor_tensor(
                    m.v[:, t0 + i, 0:H * VW].rearrange("p (h w) -> p h w", w=VW)[:, :, 0:HD],
                    ps[:, i * D:(i + 1) * D].rearrange("p (h w) -> p h w", w=HD),
                    b_v[:, :].rearrange("p (h w) -> p h w", w=HD), ALU.add), mm, ones_in, *bias_ready)
            ring.free(slot, vd)
            if waiting:
                waiting.pop(0)()
        xT_ring.free(ts, mm)
    q.barrier()
    sb.close()


def load_tokens(m, x_dram):
    src = x_dram.rearrange("(b t p) d -> b p t d", p=P, t=BT)

    def open_batch(b, slot, x, free):
        got = m.q.dma(f"x_in{slot}", x, src[b, :, :, :], *free)
        return lambda: (got, ())

    return open_batch


def score_bound(m, layer, table_range):
    q = m.q
    s = m.bound
    a = q.dve(lambda e: e.tensor_tensor(s[0:H // DC, 0:DC * B], m.norms[:, 0, :], m.norms[:, 1, :], ALU.mult))
    a = q.dve(lambda e: e.reduce_max(s[0:H // DC, 8:9], s[0:H // DC, 0:DC * B], AX.X), a)
    t = q.pe(lambda e: e.transpose(m.psum[0:1, 0:H // DC], s[0:H // DC, 8:9],
                                   m.ident[0:H // DC, 0:H // DC]), a)
    a = q.dve(lambda e: e.reduce_max(s[0:1, 9:10], m.psum[0:1, 0:H // DC], AX.X), t)
    a = q.dve(lambda e: e.tensor_scalar(s[0:1, 9:10], s[0:1, 9:10], 1e-12, 1e15, ALU.max, ALU.min), a)
    a = q.act(lambda e: e.activation(s[0:1, 9:10], s[0:1, 9:10], ACT.Ln), a)
    a = q.act(lambda e: e.activation(s[0:1, 10:11], s[0:1, 9:10], ACT.Exp, scale=0.5), a)
    a = q.dve(lambda e: e.tensor_scalar(s[0:1, 10:11], s[0:1, 10:11], 1.01 * SCORE_SCALE, None, ALU.mult), a)
    if table_range is not None:
        hi = q.dve(lambda e: e.tensor_tensor(s[0:1, 11:12], s[0:1, 10:11], table_range[:, 0:1], ALU.add), a)
        lo = q.dve(lambda e: e.tensor_tensor(s[0:1, 12:13], s[0:1, 10:11], table_range[:, 1:2], ALU.add), a)
    else:
        hi = q.dve(lambda e: e.tensor_copy(s[0:1, 11:12], s[0:1, 10:11]), a)
        lo = q.dve(lambda e: e.tensor_copy(s[0:1, 12:13], s[0:1, 10:11]), a)
    a = q.dve(lambda e: e.tensor_tensor(s[0:1, 13:14], s[0:1, 11:12], s[0:1, 12:13], ALU.add), hi, lo)
    flag = q.dve(lambda e: e.tensor_scalar(m.flag[0:1, 0:1], s[0:1, 13:14], FAST_RANGE, None, ALU.is_le), a)
    b = q.pe(lambda e: e.matmul(m.psum[:, HALF:HALF + 1], m.ones[0:1, :], s[0:1, 11:12], start=True, stop=True), a)
    c = q.dve(lambda e: e.tensor_scalar(m.shift[:, 0:1], m.psum[:, HALF:HALF + 1], -1.0, None, ALU.mult), b)
    return flag, c


def attention(m, layer, parts, tables, om, order, row_max):
    q, nc = m.q, m.nc
    sb = Arena(nc)
    n = f"A{layer}{'r' if row_max else 'f'}_"
    rows = QK_ROWS + MAX_PARTS if row_max else QK_ROWS
    qa = sb(n + "qa", [P, 2, GH, S], BF16)
    ka = sb(n + "ka", [P, 2, GH, S], BF16)
    n_probs = 8
    probs = sb(n + "probs", [P, n_probs, S])
    o_sb = sb(n + "o_sb", [P, 2, S])
    rec = sb(n + "rec", [P, 2, BT, GH])
    TW = 2 * S - P
    if tables is not None:
        bias = sb(n + "bias", [P, 1 if row_max else 2, GH, TW])
        if row_max:
            mirrored = sb(n + "mirrored", [P, 1, GH, TW])
    s_ring, p_ring, qk_ring, o_ring, t_ring = Ring(3), Ring(n_probs), Ring(2), Ring(2), Ring(1 if row_max else 2)
    O = m.psum[:, 3 * S:4 * S]
    o_free = ()
    src = parts.rearrange("o i b (h d) t -> o i b d h t", d=HD)
    q.load_tables(LN_EXP)
    if row_max:
        nm = sb(n + "nm", [P, GH * BT])
        rm = sb(n + "rm", [GH * BT, P])
        rmp = sb(n + "rmp", [GH * BT, MAX_PARTS, P], BF16)
        one = q.pool(lambda e: e.memset(ka[QK_ROWS:P, :, :, :], 1.0))

    def load(g, b):
        s, free = qk_ring.take()
        for op, slots, dst in ((0, Q_SLOTS, qa), (1, K_SLOTS, ka)):
            for r, part in enumerate(slots):
                got = q.dma(n + f"qk_in{s}", dst[r * HD:(r + 1) * HD, s, :, :],
                            src[op, part, b, :, g * GH:(g + 1) * GH, :], *free)
        return s, got

    def load_table(g):
        s, free = t_ring.take()
        for i in range(GH):
            for which, dst in enumerate((bias, mirrored) if row_max else (bias,)):
                row = tables[which, g * GH + i, :]
                got = q.dma(n + f"bias_in{s}", dst[:, s, i, :],
                            bass.AP(tensor=row.tensor, offset=row.offset, ap=[[1, P], [1, TW]]), *free)
        return s, got

    todo = []

    def finish(g, b, os_, moved):
        slot, free = s_ring.take()
        ps = m.psum[:, slot * S:(slot + 1) * S]
        for t in range(BT):
            tr = q.pe(lambda e, t=t, os_=os_, ps=ps: e.transpose(
                ps[:, t * P:(t + 1) * P], o_sb[:, os_, t * P:(t + 1) * P], m.ident[:, :]), moved, *free)
        v = ps.rearrange("p (t i c) -> p t i c", i=GH, c=P // GH)
        rc = q.dve(lambda e, v=v, os_=os_: e.reciprocal(rec[:, os_, :, :], v[:, :, :, HD]), tr)
        r = rec[:, os_, :, :]
        r = bass.AP(tensor=r.tensor, offset=r.offset, ap=[*[list(a) for a in r.ap], [0, HD]])
        nr = q.dve(lambda e, v=v, r=r, g=g, b=b: e.tensor_tensor(
            om[:, b * BT:(b + 1) * BT, g * GH * HD:(g + 1) * GH * HD].rearrange("p t (i d) -> p t i d", d=HD),
            v[:, :, :, 0:HD], r, ALU.mult), rc)
        s_ring.free(slot, nr)
        o_ring.free(os_, nr)

    def find_row_max(b, s, got, t_slot, t_got):
        for i in range(GH):
            for t in range(BT):
                slot, free = s_ring.take()
                ps = m.psum[:, slot * S:(slot + 1) * S]
                for j in range(S // HALF):
                    mm = q.pe(lambda e, i=i, t=t, j=j, ps=ps: e.matmul(
                        ps[:, j * HALF:(j + 1) * HALF], qa[0:QK_ROWS, s, i, t * P:(t + 1) * P],
                        ka[0:QK_ROWS, s, i, j * HALF:(j + 1) * HALF], start=True, stop=True), got, *free)
                if tables is not None:
                    row = mirrored[:, t_slot, i, P * t:P * t + S][:, ::-1]
                    mm = q.dve(lambda e, ps=ps, row=row: e.scalar_tensor_tensor(
                        out=ps, in0=ps, scalar=SCORE_SCALE, in1=row, op0=ALU.mult, op1=ALU.add), mm, t_got)
                mx = q.dve(lambda e, i=i, t=t, ps=ps: e.tensor_reduce(
                    out=nm[:, i * BT + t:i * BT + t + 1], in_=ps, axis=AX.X, op=ALU.max, negate=True), mm)
                s_ring.free(slot, mx)
        if tables is not None:
            mx = q.dve(lambda e: e.tensor_scalar(nm[:, :], nm[:, :], 1.0 / SCORE_SCALE, None, ALU.mult), mx)
        slot, free = s_ring.take()
        ps = m.psum[:, slot * S:(slot + 1) * S]
        tr = q.pe(lambda e: e.transpose(ps[0:GH * BT, 0:P], nm[:, :], m.ident[:, :]), mx, *free)
        a = q.dve(lambda e: e.tensor_copy(rmp[:, 0, :], ps[0:GH * BT, 0:P]), tr)
        a = q.dve(lambda e: e.tensor_tensor(rm[:, :], ps[0:GH * BT, 0:P], rmp[:, 0, :], ALU.subtract), a)
        s_ring.free(slot, a)
        a = q.dve(lambda e: e.tensor_copy(rmp[:, 1, :], rm[:, :]), a)
        a = q.dve(lambda e: e.tensor_tensor(rmp[:, 2, :], rm[:, :], rmp[:, 1, :], ALU.subtract), a)
        for i in range(MAX_PARTS):
            row = QK_ROWS + i
            got = q.dma(n + "max_in", qa[row:row + 1, s, :, :].rearrange("a h t -> a (h t)"),
                        rmp[:, i, :], a)
        q.dve(lambda e: e.memset(rm[:, 0:1], 0.0), got)
        return got

    groups = list(order)
    loads = {0: load(*groups[0])}
    table_of, tables_at = {}, {}
    if tables is not None:
        table_of[groups[0][0]] = load_table(groups[0][0])
    quads = []
    state = {}

    def queue_pv(j):
        nonlocal o_free
        g, b, kt, slots, exps = quads[0]
        for i in range(GH):
            h = g * GH + i
            pv = q.pe(lambda e, i=i, j=j, h=h, kt=kt, b=b, sl=slots[i]: e.matmul(
                O[32 * i:32 * (i + 1), j * HALF:(j + 1) * HALF],
                m.v[:, b * BT + kt, h * VW:h * VW + 32], probs[:, sl, j * HALF:(j + 1) * HALF],
                start=(kt == 0), stop=(kt == BT - 1)), *exps, *(o_free if kt == 0 else ()))
        if j == 0:
            return
        quads.pop(0)
        for sl in slots:
            p_ring.free(sl, pv)
        if kt == BT - 1:
            os_, free = o_ring.take()
            if tables is None:
                moved = q.dve(lambda e, os_=os_: e.tensor_copy(o_sb[:, os_, :], O), pv, *free)
            else:
                moved = q.act(lambda e, os_=os_: e.activation(o_sb[:, os_, :], O, ACT.Copy), pv, *free)
            o_free = (moved,)
            todo.append([g, b, os_, moved])

    def drain():
        while quads:
            for j in range(S // HALF):
                queue_pv(j)
        while todo:
            finish(*todo.pop(0))

    for at, (g, b) in enumerate(groups):
        s, got = loads.pop(at)
        ready = (got,)
        t_slot = None
        if tables is not None:
            if g not in table_of:
                table_of[g] = load_table(g)
            t_slot, t_got = table_of[g]
        if row_max:
            drain()
            ready = (got, find_row_max(b, s, got, t_slot, t_got if tables is not None else None), one)
        for kt in range(BT):
            slots, exps = [], []
            for i in range(GH):
                slot, free = s_ring.take()
                ps = m.psum[:, slot * S:(slot + 1) * S]
                for j in range(S // HALF):
                    mm = q.pe(lambda e, i=i, j=j, kt=kt, s=s, ps=ps: e.matmul(
                        ps[:, j * HALF:(j + 1) * HALF], ka[0:rows, s, i, kt * P:(kt + 1) * P],
                        qa[0:rows, s, i, j * HALF:(j + 1) * HALF], start=True, stop=True), *ready, *free)
                sl, p_free = p_ring.take()
                shift = {} if row_max else {"bias": m.shift[:, 0:1]}
                if tables is None:
                    ex = q.act(lambda e, sl=sl, ps=ps, shift=shift: e.activation(
                        probs[:, sl, :], ps, ACT.Exp, scale=SCORE_SCALE, **shift), mm, *p_free)
                    s_ring.free(slot, ex)
                else:
                    row = bias[:, t_slot, i, P * kt:P * kt + S][:, ::-1]
                    biased = q.dve(lambda e, sl=sl, ps=ps, row=row: e.scalar_tensor_tensor(
                        out=probs[:, sl, :], in0=ps, scalar=SCORE_SCALE, in1=row, op0=ALU.mult, op1=ALU.add),
                        mm, t_got, *p_free)
                    s_ring.free(slot, biased)
                    ex = q.act(lambda e, sl=sl, shift=shift: e.activation(
                        probs[:, sl, :], probs[:, sl, :], ACT.Exp, **shift), biased)
                slots.append(sl)
                exps.append(ex)
                if i >= 2 and quads:
                    queue_pv(i - 2)
                if i == 3 and kt == 2 and todo:
                    finish(*todo.pop(0))
            quads.append((g, b, kt, slots, exps))
            if kt == 0 and at + 1 < len(groups):
                loads[at + 1] = load(*groups[at + 1])
                g1 = groups[at + 1][0]
                if tables is not None and not row_max and g1 not in table_of:
                    table_of[g1] = load_table(g1)
        qk_ring.free(s, mm)
        if tables is not None and not any(x[0] == g for x in groups[at + 1:]):
            t_ring.free(t_slot, biased)
    drain()
    q.barrier()
    sb.close()


def widen(ap, n):
    return bass.AP(tensor=ap.tensor, offset=ap.offset, ap=[*[list(a) for a in ap.ap], [0, n]])


def repeat(ap, n):
    a = [list(x) for x in ap.ap]
    return bass.AP(tensor=ap.tensor, offset=ap.offset, ap=[a[0], [0, n], *a[1:]])


def close_first_attention(m, om, x_dram, wo_dram, bo_dram, gate_dram, x1_dram, rows_dram, la):
    q = m.q
    sb = Arena(m.nc)
    wo = sb("wo", [P, DC, D])
    bo = sb("bo", [P, D])
    gate = sb("gate", [P, DC, EXPERTS])
    x = sb("c_x", [P, 3, BT, D])
    x1 = sb("c_x1", [P, 3, BT, D])
    omT = sb("c_omT", [P, 2, DC, S])
    xn1 = sb("c_xn1", [P, NT, D])
    xnT = sb("c_xnT", [P, 2, DC, S])
    lnw = layernorm_scratch(sb, "c_")
    q.dma("close_w", wo[:, :, :], wo_dram.rearrange("(c p) n -> p c n", p=P))
    q.dma("close_w", bo[:, :], across(bo_dram, P))
    got_w = q.dma("close_w", gate[:, :, :], gate_dram.rearrange("(c p) n -> p c n", p=P))
    ring = Ring(4)
    x_ring, x1_ring, omT_ring, xnT_ring = Ring(3), Ring(3), Ring(2), Ring(2)
    x_src = x_dram.rearrange("(b t p) d -> b p t d", p=P, t=BT)
    x1_dst = x1_dram.rearrange("(b t p) d -> b p t d", p=P, t=BT)

    def open_batch(b):
        s, free = x_ring.take()
        got = q.dma(f"c_x_in{s}", x[:, s, :, :], x_src[b, :, :, :], *free)
        biased = q.pool(lambda e, s=s: e.tensor_tensor(x[:, s, :, :], x[:, s, :, :], repeat(bo[:, :], BT),
                                                       ALU.add), got, got_w)
        o, o_free = omT_ring.take()
        r, r_free = x1_ring.take()
        made = transpose_batch(m, ring, om[:, b * BT:(b + 1) * BT, :], omT[:, o, :, :], None, o_free)
        for half in range(2):
            slot, free = ring.take()
            ps = m.psum[:, slot * S:(slot + 1) * S]
            for i in range(BT // 2):
                t = half * (BT // 2) + i
                for k in range(DC):
                    mm = q.pe(lambda e, i=i, t=t, k=k, ps=ps, o=o: e.matmul(
                        ps[:, i * D:(i + 1) * D], omT[:, o, k, t * P:(t + 1) * P], wo[:, k, :],
                        start=(k == 0), stop=(k == DC - 1)), *made, got_w, *free)
            t0 = half * (BT // 2)
            added = q.dve(lambda e, s=s, r=r, half=half, t0=t0, ps=ps: e.tensor_tensor(
                x1[:, r, t0:t0 + BT // 2, :], ps.rearrange("p (t d) -> p t d", d=D),
                x[:, s, half * (BT // 2):(half + 1) * (BT // 2), :], ALU.add), mm, biased, *r_free)
            ring.free(slot, added)
        omT_ring.free(o, mm)
        x_ring.free(s, added)
        normed = layernorm(m, lnw, x1[:, r, :, :], xn1[:, b * BT:(b + 1) * BT, :], added)
        x1_ring.free(r, normed, q.dma(f"x1_out{r}", x1_dst[b, :, :, :], x1[:, r, :, :], added))
        q.dma("rows_out", rows_dram.rearrange("(p t) d -> p t d", p=P)[:, b * BT:(b + 1) * BT, :],
              xn1[:, b * BT:(b + 1) * BT, :], normed)
        return normed

    def route_batch(b, normed):
        o, o_free = xnT_ring.take()
        made = transpose_batch(m, ring, xn1[:, b * BT:(b + 1) * BT, :], xnT[:, o, :, :], normed, o_free)
        slot, free = ring.take()
        ps = m.psum[:, slot * S:slot * S + BT * EXPERTS]
        for t in range(BT):
            for k in range(DC):
                mm = q.pe(lambda e, t=t, k=k, ps=ps, o=o: e.matmul(
                    ps[:, t * EXPERTS:(t + 1) * EXPERTS], xnT[:, o, k, t * P:(t + 1) * P], gate[:, k, :],
                    start=(k == 0), stop=(k == DC - 1)), *made, *free)
        xnT_ring.free(o, mm)
        got = q.dve(lambda e, b=b, ps=ps: e.tensor_scalar(
            la[:, b * BT:(b + 1) * BT, :], ps.rearrange("p (t e) -> p t e", e=EXPERTS),
            -1.0 / SINKHORN_EPS, None, ALU.mult), mm)
        ring.free(slot, got)

    opened = [open_batch(b) for b in range(2)]
    for b in range(B):
        if b + 2 < B:
            opened.append(open_batch(b + 2))
        route_batch(b, opened[b])
    q.barrier()
    sb.close()


def sinkhorn(m, la, pi, beside):
    next(beside)
    q = m.q
    sb = Arena(m.nc)
    E = EXPERTS
    mx = sb("s_mx", [P, NT])
    ex = sb("s_ex", [P, NT, E])
    sm = sb("s_sm", [P, NT])
    cm = sb("s_cm", [P, E])
    gm = sb("s_gm", [E, 1])
    dg = sb("s_dg", [E, E])
    cs = sb("s_cs", [P, E])
    cl = sb("s_cl", [P, E])
    ps_t = m.psum[0:E, 0:P]
    ps_m = m.psum[:, HALF:HALF + E]
    ps_s = m.psum[:, 2 * HALF:2 * HALF + E]
    by_expert = la[:, :, :].rearrange("p t e -> p e t")
    a = None
    for _ in range(SINKHORN_ITERS):
        next(beside, None)
        a = q.dve(lambda e: e.reduce_max(mx[:, :], la[:, :, :], AX.X), a)
        a = q.dve(lambda e: e.tensor_tensor(la[:, :, :], la[:, :, :], widen(mx[:, :], E), ALU.subtract), a)
        a = q.act(lambda e: e.activation(ex[:, :, :], la[:, :, :], ACT.Exp), a)
        a = q.dve(lambda e: e.reduce_sum(sm[:, :], ex[:, :, :], AX.X), a)
        a = q.act(lambda e: e.activation(sm[:, :], sm[:, :], ACT.Ln), a)
        a = q.dve(lambda e: e.tensor_tensor(la[:, :, :], la[:, :, :], widen(sm[:, :], E), ALU.subtract), a)
        a = q.dve(lambda e: e.reduce_max(cm[:, :], by_expert, AX.X), a)
        a = q.pe(lambda e: e.transpose(ps_t, cm[:, :], m.ident[:, :]), a)
        a = q.dve(lambda e: e.reduce_max(gm[:, :], ps_t, AX.X), a)
        a = q.dve(lambda e: e.tensor_scalar(dg[:, :], m.ident[0:E, 0:E], gm[:, 0:1], None, ALU.mult), a)
        a = q.pe(lambda e: e.matmul(ps_m, m.ones[0:E, :], dg[:, :], start=True, stop=True), a)
        a = q.dve(lambda e: e.tensor_tensor(la[:, :, :], la[:, :, :], repeat(ps_m, NT), ALU.subtract), a)
        a = q.act(lambda e: e.activation(ex[:, :, :], la[:, :, :], ACT.Exp), a)
        a = q.dve(lambda e: e.reduce_sum(cs[:, :], ex[:, :, :].rearrange("p t e -> p e t"), AX.X), a)
        a = q.pe(lambda e: e.matmul(ps_s, m.ones[:, :], cs[:, :], start=True, stop=True), a)
        a = q.act(lambda e: e.activation(cl[:, :], ps_s, ACT.Ln), a)
        a = q.dve(lambda e: e.tensor_tensor(la[:, :, :], la[:, :, :], repeat(cl[:, :], NT), ALU.subtract), a)
    for _ in beside:
        pass
    q.act(lambda e: e.activation(pi[:, :, :], la[:, :, :], ACT.Exp), a)
    q.barrier()
    sb.close()


def route(m, pi, slots, tokens, plan):
    q = m.q
    sb = Arena(m.nc)
    E = EXPERTS
    key = sb("r_key", [P, NT, E])
    top = sb("r_top", [P, NT])
    eq = sb("r_eq", [P, NT, E])
    rank = sb("r_rank", [P, E])
    pick = [sb(f"r_pick{k}", [P, NT, E]) for k in range(2)]
    both = sb("r_both", [P, NT, E])
    pos = sb("r_pos", [P, NT, E])
    total = sb("r_total", [P, NT, E])
    scan = [sb(f"r_scan{k}", [P, NT, E]) for k in range(2)]
    tiles = sb("r_tiles", [P, E])
    tiles_i = sb("r_tiles_i", [P, E], I32)
    upto = [sb(f"r_upto{k}", [P, E]) for k in range(2)]
    prod = sb("r_prod", [P, NT, E])
    row = sb("r_row", [P, 2, NT])
    place_i = sb("r_place_i", [P, 2, 2 * NT], I32)
    place = sb("r_place", [P, 2, 2 * NT])
    name = sb("r_name", [P, NT])
    n_hot = 8
    row_hot = sb("r_row_hot", [P, n_hot, P])
    tile_hot = sb("r_tile_hot", [P, n_hot, MOE_TILES])
    count_up = sb("r_count_up", [P, P])
    J = MOE_TILES
    j_iota = sb("r_j", [1, J])
    ge = sb("r_ge", [1, J, E])
    ex = sb("r_ex", [1, J])
    new = sb("r_new", [1, J])
    run = [sb(f"r_run{k}", [1, J]) for k in range(2)]
    three = sb("r_three", [1, J])
    r0 = q.pool(lambda e: e.iota(rank[:, :], pattern=[[-1, E]], base=E, channel_multiplier=0,
                                 allow_small_or_imprecise_dtypes=True))
    j0 = q.pool(lambda e: e.iota(j_iota[:, :], pattern=[[1, J]], base=0, channel_multiplier=0,
                                 allow_small_or_imprecise_dtypes=True))
    c0 = q.pool(lambda e: e.iota(count_up[:, :], pattern=[[1, P]], base=0, channel_multiplier=0,
                                 allow_small_or_imprecise_dtypes=True))
    j0 = q.pool(lambda e: e.iota(name[:, :], pattern=[[1, NT]], base=0, channel_multiplier=NT,
                                 allow_small_or_imprecise_dtypes=True), j0, c0)
    a = q.dve(lambda e: e.tensor_scalar(eq[:, :, :], pi[:, :, :], TINY, None, ALU.is_ge), r0, j0)
    a = q.dve(lambda e: e.tensor_tensor(key[:, :, :], pi[:, :, :], eq[:, :, :], ALU.mult), a)
    for k in range(2):
        a = q.dve(lambda e: e.reduce_max(top[:, :], key[:, :, :], AX.X), a)
        a = q.dve(lambda e: e.tensor_tensor(eq[:, :, :], key[:, :, :], widen(top[:, :], E), ALU.is_equal), a)
        a = q.dve(lambda e: e.tensor_tensor(eq[:, :, :], eq[:, :, :], repeat(rank[:, :], NT), ALU.mult), a)
        a = q.dve(lambda e: e.reduce_max(top[:, :], eq[:, :, :], AX.X), a)
        a = q.dve(lambda e, k=k: e.tensor_tensor(pick[k][:, :, :], eq[:, :, :], widen(top[:, :], E),
                                                 ALU.is_equal), a)
        if k == 0:
            a = q.dve(lambda e: e.scalar_tensor_tensor(out=key[:, :, :], in0=pick[0][:, :, :], scalar=-4.0,
                                                       in1=key[:, :, :], op0=ALU.mult, op1=ALU.add), a)
    a = q.dve(lambda e: e.tensor_tensor(both[:, :, :], pick[0][:, :, :], pick[1][:, :, :], ALU.add), a)
    flat = both[:, :, :].rearrange("p t e -> p (t e)")
    p1 = q.pe(lambda e: e.matmul(m.psum[:, 0:NT * E], m.before[:, :], flat, start=True, stop=True), a)
    p2 = q.pe(lambda e: e.matmul(m.psum[:, HALF:HALF + NT * E], m.ones[:, :], flat, start=True, stop=True), a)
    a = q.dve(lambda e: e.tensor_copy(pos[:, :, :].rearrange("p t e -> p (t e)"), m.psum[:, 0:NT * E]), p1)
    a = q.dve(lambda e: e.tensor_copy(total[:, :, :].rearrange("p t e -> p (t e)"),
                                      m.psum[:, HALF:HALF + NT * E]), p2, a)
    cur, at, step = total, 0, 1
    while step < NT:
        dst = scan[at]
        q.dve(lambda e, cur=cur, dst=dst, step=step: e.tensor_copy(dst[:, 0:step, :], cur[:, 0:step, :]), a)
        a = q.dve(lambda e, cur=cur, dst=dst, step=step: e.tensor_tensor(
            dst[:, step:NT, :], cur[:, step:NT, :], cur[:, 0:NT - step, :], ALU.add), a)
        cur, at, step = dst, 1 - at, 2 * step
    count = cur[:, NT - 1, :]
    a = q.dve(lambda e, cur=cur: e.tensor_tensor(pos[:, :, :], pos[:, :, :], cur[:, :, :], ALU.add), a)
    a = q.dve(lambda e: e.tensor_tensor(pos[:, :, :], pos[:, :, :], total[:, :, :], ALU.subtract), a)
    a = q.dve(lambda e, count=count: e.tensor_scalar(tiles_i[:, :], count, float(P - 1), None, ALU.add), a)
    a = q.dve(lambda e: e.tensor_scalar(tiles_i[:, :], tiles_i[:, :], P.bit_length() - 1, None,
                                        ALU.logical_shift_right), a)
    a = q.dve(lambda e: e.tensor_copy(tiles[:, :], tiles_i[:, :]), a)
    cur, at, step = tiles, 0, 1
    while step < E:
        dst = upto[at]
        q.dve(lambda e, cur=cur, dst=dst, step=step: e.tensor_copy(dst[:, 0:step], cur[:, 0:step]), a)
        a = q.dve(lambda e, cur=cur, dst=dst, step=step: e.tensor_tensor(
            dst[:, step:E], cur[:, step:E], cur[:, 0:E - step], ALU.add), a)
        cur, at, step = dst, 1 - at, 2 * step
    end = cur
    a = q.dve(lambda e, end=end: e.tensor_tensor(tiles[:, :], end[:, :], tiles[:, :], ALU.subtract), a)
    a = q.dve(lambda e: e.scalar_tensor_tensor(out=pos[:, :, :], in0=repeat(tiles[:, :], NT), scalar=float(P),
                                               in1=pos[:, :, :], op0=ALU.mult, op1=ALU.add), a)
    for k in range(2):
        a = q.dve(lambda e, k=k: e.tensor_tensor(prod[:, :, :], pick[k][:, :, :], pos[:, :, :], ALU.mult), a)
        a = q.dve(lambda e, k=k: e.reduce_sum(row[:, k, :], prod[:, :, :], AX.X), a)
    a = q.dve(lambda e: e.tensor_copy(slots[:, :, :], row[:, :, :]), a)
    flat_slots = slots[:, :, :].rearrange("p k t -> p (k t)")
    h = q.dve(lambda e: e.tensor_scalar(place_i[:, 0, :], flat_slots, P.bit_length() - 1, None,
                                        ALU.logical_shift_right), a)
    h = q.dve(lambda e: e.tensor_scalar(place_i[:, 1, :], flat_slots, P - 1, None, ALU.bitwise_and), h)
    h = q.dve(lambda e: e.tensor_copy(place[:, :, :], place_i[:, :, :]), h)
    hot_ring = Ring(n_hot)
    T = m.psum[:, 2 * HALF:2 * HALF + MOE_TILES]
    for i in range(2 * NT):
        s, free = hot_ring.take()
        r_hot = q.dve(lambda e, s=s, i=i: e.tensor_scalar(row_hot[:, s, :], count_up[:, :],
                                                          place[:, 1, i:i + 1], None, ALU.is_equal), h, *free)
        t_hot = q.dve(lambda e, s=s, i=i: e.tensor_scalar(tile_hot[:, s, :], count_up[:, 0:MOE_TILES],
                                                          place[:, 0, i:i + 1], name[:, i % NT:i % NT + 1],
                                                          ALU.is_equal, ALU.mult), h)
        mm = q.pe(lambda e, s=s, i=i: e.matmul(T, row_hot[:, s, :], tile_hot[:, s, :], start=(i == 0),
                                               stop=(i == 2 * NT - 1)), r_hot, t_hot)
        hot_ring.free(s, mm)
    got = q.dve(lambda e: e.tensor_copy(tokens[:, :], T), mm)
    a = q.dve(lambda e, end=end: e.tensor_tensor(ge[:, :, :], widen(j_iota[:, :], E), repeat(end[0:1, :], J),
                                                 ALU.is_ge), a)
    a = q.dve(lambda e: e.reduce_sum(ex[:, :], ge[:, :, :], AX.X), a)
    a = q.dve(lambda e: e.tensor_scalar(ex[:, :], ex[:, :], float(E - 1), None, ALU.min), a)
    q.dve(lambda e: e.memset(new[:, 0:1], 0.0))
    a = q.dve(lambda e: e.tensor_tensor(new[:, 1:J], ex[:, 1:J], ex[:, 0:J - 1], ALU.not_equal), a)
    cur, at, step = new, 0, 1
    while step < J:
        dst = run[at]
        q.dve(lambda e, cur=cur, dst=dst, step=step: e.tensor_copy(dst[:, 0:step], cur[:, 0:step]), a)
        a = q.dve(lambda e, cur=cur, dst=dst, step=step: e.tensor_tensor(
            dst[:, step:J], cur[:, step:J], cur[:, 0:J - step], ALU.add), a)
        cur, at, step = dst, 1 - at, 2 * step
    for least in range(W_BUFS * ((E - 1) // W_BUFS), 0, -W_BUFS):
        a = q.dve(lambda e, cur=cur, least=least: e.tensor_scalar(three[:, :], cur[:, :], float(least), -float(W_BUFS),
                                                     ALU.is_ge, ALU.mult), a)
        a = q.dve(lambda e, cur=cur: e.tensor_tensor(cur[:, :], cur[:, :], three[:, :], ALU.add), a)
    for i, src in enumerate((ex, new, cur)):
        a = q.dve(lambda e, i=i, src=src: e.tensor_copy(plan[0:1, i, :], src[:, :]), a)
    q.barrier()
    sb.close()


W_BUFS = 3
LEAD = W_BUFS - 1


def experts(m, tokens, plan, weights, rows_dram, queue_y):
    q = m.q
    sb = Arena(m.nc)
    WIDE = 2 * DC * F + FC * D
    w = sb("e_w", [P, W_BUFS, WIDE])
    x = sb("e_x", [P, 3, D])
    xT = sb("e_xT", [P, 2, DC, P])
    act = sb("e_act", [P, 2, F])
    hid = sb("e_hid", [P, 2, F])
    hT = sb("e_hT", [P, 2, FC, P])
    y = sb("e_y", [P, 2, D])
    J = MOE_TILES
    GU = m.psum[:, 0:2 * F].rearrange("p (a f) -> p a f", a=2)
    HT = m.psum[:, 2 * F:3 * F]
    XT = m.psum[:, 3 * F:3 * F + DC * P]
    Y = m.psum[:, 3 * F + HALF:3 * F + HALF + D]
    x_ring, xT_ring, act_ring, hid_ring, hT_ring, y_ring = Ring(3), Ring(2), Ring(2), Ring(2), Ring(2), Ring(2)
    buffer_of = {}

    def fetch(j, after):

        def emit(eng, j=j):
            expert = eng.value_load(plan[0:1, 0, j:j + 1], min_val=0, max_val=EXPERTS - 1)
            buf = eng.value_load(plan[0:1, 2, j:j + 1], min_val=0, max_val=W_BUFS - 1)
            more = {}
            if j:
                new = eng.value_load(plan[0:1, 1, j:j + 1], min_val=0, max_val=1)
                more = {"cond": new > 0}
            return eng.dma_start(w[:, bass.ds(buf, 1), :],
                                 weights[bass.ds(expert, 1), :, :].rearrange("e p n -> p e n"), **more)

        return q.dma_by("sync", f"weights_in{j % (LEAD + 1)}", emit, after)

    def load_rows(j):
        s, free = x_ring.take()
        return s, q.dma_by("gpsimd", f"rows_in{s}", lambda e: e.indirect_dma_start(
            out=x[:, s, :], out_offset=None, in_=rows_dram,
            in_offset=bass.IndirectOffsetOnAxis(ap=tokens[:, j:j + 1], axis=0)), *free)

    xT_free = [()]
    y_free = [()]

    def turn(s, got):
        for c in range(DC):
            tr = q.pe(lambda e, c=c, s=s: e.transpose(XT[:, c * P:(c + 1) * P], x[:, s, c * P:(c + 1) * P],
                                                      m.ident[:, :]), got, *xT_free[0])
        x_ring.free(s, tr)
        o, free = xT_ring.take()
        cp = q.dve(lambda e, o=o: e.tensor_copy(xT[:, o, :, :].rearrange("p c n -> p (c n)"), XT), tr, *free)
        xT_free[0] = (cp,)
        return o, cp

    def at_buffer(eng, j):
        if buffer_of.get("j") != j:
            buffer_of["j"] = j
            buffer_of["v"] = eng.value_load(plan[0:1, 2, j:j + 1], min_val=0, max_val=W_BUFS - 1)
        return buffer_of["v"]

    def up_product(j, which, o, ready, free):
        for half in range(F // HALF):
            for c in range(DC):
                at = (which * DC + c) * F + half * HALF

                def emit(e, j=j, o=o, c=c, at=at, half=half):
                    moving = w[:, bass.ds(at_buffer(e, j), 1), at:at + HALF].rearrange("p a n -> p (a n)")
                    return e.matmul(GU[:, which, half * HALF:(half + 1) * HALF], xT[:, o, c, :], moving,
                                    start=(c == 0), stop=(c == DC - 1))

                mm = q.pe(emit, *ready, *free)
        return mm

    def turn_hidden(hs, done, free):
        for f in range(FC):
            tr = q.pe(lambda e, f=f, hs=hs: e.transpose(HT[:, f * P:(f + 1) * P], hid[:, hs, f * P:(f + 1) * P],
                                                        m.ident[:, :]), *done, *free)
        return tr

    def down(j, ts, done):
        for f in range(FC):
            at = 2 * DC * F + f * D

            def emit(e, j=j, ts=ts, f=f, at=at):
                moving = w[:, bass.ds(at_buffer(e, j), 1), at:at + D].rearrange("p a n -> p (a n)")
                return e.matmul(Y, hT[:, ts, f, :], moving, start=(f == 0), stop=(f == FC - 1))

            mm = q.pe(emit, *done, *y_free[0])
        o, free = y_ring.take()
        cp = q.act(lambda e, o=o: e.activation(y[:, o, :], Y, ACT.Copy), mm, *free)
        y_free[0] = (cp,)
        y_ring.free(o, q.dma(f"y_out{o}", queue_y[j * P:(j + 1) * P, :], y[:, o, :], cp, queue="scalar"))
        return mm

    weights_got = {j: fetch(j, None) for j in range(LEAD)}
    rows = {j: load_rows(j) for j in range(2)}
    turned = {0: turn(*rows.pop(0))}
    g_free = u_free = ()
    hT_psum_free = ()
    pending = None
    down_done = {}
    for j in range(J):
        o, xready = turned.pop(j)
        ready = (xready, weights_got[j])
        if j + 2 < J:
            rows[j + 2] = load_rows(j + 2)
        g = up_product(j, 0, o, ready, g_free)
        a_s, a_free = act_ring.take()
        sg = q.act(lambda e, a_s=a_s: e.activation(act[:, a_s, :], GU[:, 0, :], ACT.Silu), g, *a_free)
        g_free = (sg,)
        if pending is not None:
            tr = turn_hidden(pending[1], pending[2], hT_psum_free)
            ts, t_free = hT_ring.take()
            flat = hT[:, ts, :, :].rearrange("p f n -> p (f n)")
            c1 = q.dve(lambda e, flat=flat: e.tensor_copy(flat, HT), tr, *t_free)
            hid_ring.free(pending[1], tr)
            hT_psum_free = (c1,)
        u = up_product(j, 1, o, ready, u_free)
        xT_ring.free(o, u)
        h_s, h_free = hid_ring.take()
        hd = q.dve(lambda e, a_s=a_s, h_s=h_s: e.tensor_tensor(hid[:, h_s, :], act[:, a_s, :], GU[:, 1, :],
                                                              ALU.mult), sg, u, *h_free)
        u_free = (hd,)
        act_ring.free(a_s, hd)
        if j + 1 < J:
            turned[j + 1] = turn(*rows.pop(j + 1))
        if pending is not None:
            dd = down(pending[0], ts, (c1,))
            hT_ring.free(ts, dd)
            down_done[pending[0]] = dd
        if j + LEAD < J:
            weights_got[j + LEAD] = fetch(j + LEAD, down_done.get(j - 1))
        pending = (j, h_s, (hd,))
    tr = turn_hidden(pending[1], pending[2], hT_psum_free)
    ts, t_free = hT_ring.take()
    flat = hT[:, ts, :, :].rearrange("p f n -> p (f n)")
    c1 = q.dve(lambda e, flat=flat: e.tensor_copy(flat, HT), tr, *t_free)
    down(pending[0], ts, (c1,))
    q.barrier()
    sb.close()


def combine_tokens(m, sb, x1_dram, x2_dram, pi, slots, queue_y):
    q = m.q
    x1_src = x1_dram.rearrange("(b t p) d -> b p t d", p=P, t=BT)
    x2_dst = x2_dram.rearrange("(b t p) d -> b p t d", p=P, t=BT)
    rows = [sb(f"g_rows{k}", [P, 2, BT, D]) for k in range(2)]
    rings = [Ring(2), Ring(2)]

    def open_batch(b, slot, x, free):
        got = q.dma(f"x1_in{slot}", x, x1_src[b, :, :, :], *free)
        gathered = {}
        for k in range(2):
            r, r_free = rings[k].take()
            for i in range(BT):
                t = b * BT + i
                here = q.dma_by("gpsimd", f"rows_back{k}{r}", lambda e, k=k, r=r, i=i, t=t: e.indirect_dma_start(
                    out=rows[k][:, r, i, :], out_offset=None, in_=queue_y,
                    in_offset=bass.IndirectOffsetOnAxis(ap=slots[:, k, t:t + 1], axis=0)), *r_free)
            gathered[k] = (r, here)
        return lambda: combine(b, slot, x, got, gathered)

    def combine(b, slot, x, got, gathered):
        for k in range(2):
            r, here = gathered[k]
            for i in range(BT):
                t = b * BT + i
                done = q.dve(lambda e, k=k, r=r, i=i, t=t, x=x: e.scalar_tensor_tensor(
                    out=x[:, i, :], in0=rows[k][:, r, i, :], scalar=pi[:, t, k:k + 1], in1=x[:, i, :],
                    op0=ALU.mult, op1=ALU.add), here, got)
            rings[k].free(r, done)
            got = done
        return done, (q.dma(f"x2_out{slot}", x2_dst[b, :, :, :], x, done),)

    return open_batch


def bias_tables(m, sb, amplitudes, sharpness, offsets, tables_dram, table_range):
    q = m.q
    terms = 21
    groups = 3
    R = H * terms // groups
    W = 2 * S
    coef = sb("b_coef", [R, 3, groups])
    mask = sb("b_mask", [R, groups, H])
    rel = sb("b_rel", [R, W])
    d = sb("b_d", [R, groups, W])
    table = sb("b_table", [H, W])
    mirror = sb("b_mirror", [H, W])
    ends = sb("b_ends", [H, 2])
    ends_row = sb("b_ends_row", [1, 2, H])
    for i, src in enumerate((amplitudes, sharpness, offsets)):
        got = q.dma("coef_in", coef[:, i, :], src)
    a = q.pool(lambda e: e.memset(mask[:, :, :], 1.0))
    a = q.pool(lambda e: e.affine_select(out=mask[:, :, :], in_=mask[:, :, :], compare_op=ALU.is_ge, fill=0.0,
                                         base=0, pattern=[[R, groups], [-terms, H]], channel_multiplier=1), a)
    a = q.pool(lambda e: e.affine_select(out=mask[:, :, :], in_=mask[:, :, :], compare_op=ALU.is_ge, fill=0.0,
                                         base=terms - 1, pattern=[[-R, groups], [terms, H]],
                                         channel_multiplier=-1), a)
    i0 = q.pool(lambda e: e.iota(rel[:, :], pattern=[[1, W]], base=-(S - 1), channel_multiplier=0,
                                 allow_small_or_imprecise_dtypes=True))
    sharp = sb("b_sharp", [R, groups])
    s1 = q.dve(lambda e: e.tensor_scalar(sharp[:, :], coef[:, 1, :], -1.0, None, ALU.mult), got)
    s1 = q.dve(lambda e: e.tensor_tensor(sharp[:, :], sharp[:, :], coef[:, 1, :], ALU.min), s1)
    masked = a
    for g in range(groups):
        mk = q.dve(lambda e, g=g: e.tensor_scalar(mask[:, g, :], mask[:, g, :], coef[:, 0, g:g + 1], None, ALU.mult), masked, got)
        a = q.dve(lambda e, g=g: e.tensor_scalar(d[:, g, :], rel[:, :], coef[:, 2, g:g + 1], None, ALU.subtract), i0, got)
        a = q.dve(lambda e, g=g: e.scalar_tensor_tensor(out=d[:, g, :], in0=d[:, g, :], scalar=sharp[:, g:g + 1],
                                                        in1=d[:, g, :], op0=ALU.mult, op1=ALU.mult), a, s1)
        ex = q.act(lambda e, g=g: e.activation(d[:, g, :], d[:, g, :], ACT.Exp), a)
        yield
    for j in range(W // HALF):
        for g in range(groups):
            mm = q.pe(lambda e, j=j, g=g: e.matmul(m.psum[0:H, W + j * HALF:W + (j + 1) * HALF], mask[:, g, :],
                                                   d[:, g, j * HALF:(j + 1) * HALF], start=(g == 0),
                                                   stop=(g == groups - 1)), ex, mk)
        yield
    L = W - 1
    t1 = q.dve(lambda e: e.tensor_copy(table[:, :], m.psum[0:H, W:2 * W]), mm)
    t2 = q.dve(lambda e: e.tensor_copy(mirror[:, 0:L], table[:, 0:L][:, ::-1]), t1)
    t2 = q.dve(lambda e: e.tensor_copy(mirror[:, L:W], table[:, L:W]), t2)
    q.dma("tables_out", tables_dram[0, :, :], table[:, :], t1)
    yield
    q.dma("tables_out", tables_dram[1, :, :], mirror[:, :], t2)
    x1 = q.dve(lambda e: e.reduce_max(ends[:, 0:1], table[:, 0:L], AX.X), t2)
    x2 = q.dve(lambda e: e.tensor_reduce(out=ends[:, 1:2], in_=table[:, 0:L], axis=AX.X, op=ALU.min, negate=True), x1)
    for k in range(2):
        tr = q.pe(lambda e, k=k: e.transpose(m.psum[0:1, W + k * H:W + (k + 1) * H], ends[:, k:k + 1],
                                             m.ident[0:H, 0:H]), x2)
        yield
    a = q.dve(lambda e: e.tensor_copy(ends_row[:, :, :].rearrange("a k h -> a (k h)"),
                                      m.psum[0:1, W:W + 2 * H]), tr)
    a = q.dve(lambda e: e.reduce_max(table_range[:, :], ends_row[:, :, :], AX.X), a)
    q.dve(lambda e: e.tensor_scalar(table_range[:, :], table_range[:, :], 0.0, None, ALU.max), a)


FP8_MAX = 448.0


def close_second_layer(m, om, x2_dram, wg_dram, bg_dram, w8_dram, b8_dram, scales_dram, out_dram):
    q = m.q
    sb = Arena(m.nc)
    wg = sb("f_wg", [P, DC, 2 * D])
    bg = sb("f_bg", [P, 2 * D])
    w8 = sb("f_w8", [P, DC, D])
    b8 = sb("f_b8", [P, D])
    sc = sb("f_sc", [P, 2])
    inv = sb("f_inv", [P, 1])
    omT = sb("f_omT", [P, DC, S])
    x = sb("f_x", [P, 2, BT, D])
    gated = sb("f_gated", [P, BT, 2, D])
    xn = sb("f_xn", [P, 2, BT, D])
    step = sb("f_step", [P, BT, D])
    xqT = sb("f_xqT", [P, DC, S])
    lnw = layernorm_scratch(sb, "f_")
    x2_src = x2_dram.rearrange("(b t p) d -> b p t d", p=P, t=BT)
    out_dst = out_dram.rearrange("(b t p) d -> b p t d", p=P, t=BT)
    ring = Ring(4)
    x_ring, xn_ring = Ring(2), Ring(2)
    omT_ring, xqT_ring, gated_ring, step_ring = Ring(1), Ring(1), Ring(1), Ring(1)

    def fetch(b):
        s, free = x_ring.take()
        return s, q.dma(f"x2_in{s}", x[:, s, :, :], x2_src[b, :, :, :], *free)

    fetched = [fetch(b) for b in range(2)]
    q.dma("f_w_in", wg[:, :, :], wg_dram.rearrange("(c p) n -> p c n", p=P), queue="scalar")
    q.dma("f_w_in", w8[:, :, :], w8_dram.rearrange("(c p) n -> p c n", p=P), queue="scalar")
    q.dma("f_w_in", bg[:, :], across(bg_dram, P), queue="scalar")
    q.dma("f_w_in", b8[:, :], across(b8_dram, P), queue="scalar")
    got_w = q.dma("f_w_in", sc[:, :], across(scales_dram, P), queue="scalar")
    r = q.dve(lambda e: e.reciprocal(inv[:, :], sc[:, 0:1]), got_w)
    w8s = q.dve(lambda e: e.tensor_scalar(w8[:, :, :], w8[:, :, :], sc[:, 1:2], sc[:, 0:1], ALU.mult, ALU.mult),
                got_w)

    def gate_and_round(b):
        s, got = fetched[b]
        x3 = x[:, s, :, :]
        _, free = omT_ring.take()
        made = transpose_batch(m, ring, om[:, b * BT:(b + 1) * BT, :], omT[:, :, :], None, free)
        _, g_free = gated_ring.take()
        for i in range(0, BT, 2):
            slot, free = ring.take()
            ps = m.psum[:, slot * S:(slot + 1) * S]
            for t in (i, i + 1):
                for k in range(DC):
                    mm = q.pe(lambda e, t=t, i=i, k=k, ps=ps: e.matmul(
                        ps[:, (t - i) * 2 * D:(t - i + 1) * 2 * D], omT[:, k, t * P:(t + 1) * P], wg[:, k, :],
                        start=(k == 0), stop=(k == DC - 1)), *made, got_w, *free)
            d = q.dve(lambda e, i=i, ps=ps: e.tensor_tensor(
                gated[:, i:i + 2, :, :].rearrange("p t a n -> p t (a n)"),
                ps.rearrange("p (t n) -> p t n", n=2 * D), repeat(bg[:, :], 2), ALU.add), mm, *g_free)
            ring.free(slot, d)
        omT_ring.free(0, mm)
        sg = q.act(lambda e: e.activation(gated[:, :, 1, :], gated[:, :, 1, :], ACT.Sigmoid), d)
        a = q.dve(lambda e: e.tensor_tensor(gated[:, :, 0, :], gated[:, :, 0, :], gated[:, :, 1, :], ALU.mult),
                  sg, d)
        a = q.pool(lambda e, x3=x3: e.tensor_tensor(x3, x3, gated[:, :, 0, :], ALU.add), a, got)
        gated_ring.free(0, a)
        n, n_free = xn_ring.take()
        y = xn[:, n, :, :]
        a = layernorm(m, lnw, x3, y, a, r, *n_free, factor=inv[:, 0:1])
        a = q.dve(lambda e, y=y: e.tensor_scalar(y, y, FP8_MAX, -FP8_MAX, ALU.min, ALU.max), a)
        _, s_free = step_ring.take()
        a = q.dve(lambda e, y=y: e.tensor_scalar(step[:, :, :].bitcast(I32), y.bitcast(I32), 0x7F800000,
                                                 None, ALU.bitwise_and), a, *s_free)
        a = q.dve(lambda e: e.tensor_scalar(step[:, :, :], step[:, :, :], 2.0 ** -6, 1.5 * 2.0 ** 20,
                                            ALU.max, ALU.mult), a)
        a = q.dve(lambda e, y=y: e.tensor_tensor(y, y, step[:, :, :], ALU.add), a)
        a = q.dve(lambda e, y=y: e.tensor_tensor(y, y, step[:, :, :], ALU.subtract), a)
        step_ring.free(0, a)
        xb = q.pool(lambda e, x3=x3: e.tensor_tensor(x3, x3, repeat(b8[:, :], BT), ALU.add), a)
        return s, n, a, xb

    def product(b, s, n, rounded, xb):
        x3 = x[:, s, :, :]
        _, free = xqT_ring.take()
        made = transpose_batch(m, ring, xn[:, n, :, :], xqT[:, :, :], rounded, free)
        xn_ring.free(n, *made)
        for half in range(2):
            slot, free = ring.take()
            ps = m.psum[:, slot * S:(slot + 1) * S]
            for i in range(BT // 2):
                t = half * (BT // 2) + i
                for k in range(DC):
                    mm = q.pe(lambda e, i=i, t=t, k=k, ps=ps: e.matmul(
                        ps[:, i * D:(i + 1) * D], xqT[:, k, t * P:(t + 1) * P], w8[:, k, :],
                        start=(k == 0), stop=(k == DC - 1)), *made, w8s, *free)
            h0 = half * (BT // 2)
            a = q.dve(lambda e, x3=x3, h0=h0, ps=ps: e.tensor_tensor(
                x3[:, h0:h0 + BT // 2, :], ps.rearrange("p (t d) -> p t d", d=D), x3[:, h0:h0 + BT // 2, :],
                ALU.add), mm, xb)
            ring.free(slot, a)
        xqT_ring.free(0, mm)
        x_ring.free(s, q.dma(f"out{s}", out_dst[b, :, :, :], x3, a))
        if b + 2 < B:
            fetched.append(fetch(b + 2))

    ahead = gate_and_round(0)
    for b in range(B):
        now = ahead
        if b + 1 < B:
            ahead = gate_and_round(b + 1)
        product(b, *now)
    q.barrier()
    sb.close()


def build_program(nc, ctx, t, out_dram):
    m = Machine()
    m.nc, m.q, m.keep = nc, Queues(nc, ctx), Arena(nc)
    q = m.q
    m.psum = ctx.enter_context(nc.psum_tensor("psum", [P, 8 * HALF], FP32))[:, :]

    def scratch(name, shape, dtype=FP32):
        return nc.dram_tensor(name, shape, dtype, kind="Internal").ap()

    parts = scratch("qk_parts", [2, 3, B, D, S], BF16)
    x1_dram, x2_dram = scratch("x1", [N, D]), scratch("x2", [N, D])
    rows, queue_y = scratch("token_rows", [N, D]), scratch("queue_y", [MOE_TILES * P, D])
    tables = scratch("tables", [2, H, 2 * S])

    make_constants(m)
    m.norms = m.keep("norms", [H // DC, 2, DC * B])
    m.bound = m.keep("bound", [H // DC, 16])
    m.shift = m.keep("shift", [P, 1])
    m.flag = m.keep("flag", [1, 1], I32)
    table_range = m.keep("table_range", [1, 2])
    la = m.keep("la", [P, NT, EXPERTS])
    pi = m.keep("pi", [P, NT, EXPERTS])
    slots = m.keep("slots", [P, 2, NT], I32)
    plan = m.keep("plan", [1, 3, MOE_TILES], I32)
    tokens = m.keep("tokens", [P, MOE_TILES], I32)

    def attend(layer, om, tables, order):
        main = m.q
        paths = []
        for row_max in (False, True):
            m.q = Queues(nc, ctx, f"a{layer}{'rowmax' if row_max else 'shift'}")
            attention(m, layer, parts, tables, om, order, row_max)
            paths.append(m.q)
        m.q = main
        main.either(m.flag[0:1, 0:1], *paths)
        main.barrier()
        main.load_tables(LN_EXP)

    q.load_tables(LN_EXP)
    first = Arena(nc)
    m.v = first("v0", [P, NT, H * VW + HD])
    om = first("om0", [P, NT, D])
    project(m, 0, load_tokens(m, t["x"]), [t["wq"], t["wk"], t["wv"]], [t["bq"], t["bk"], t["bv"]], parts)
    score_bound(m, 0, None)
    q.barrier()
    attend(0, om, None, [(g, b) for b in range(B) for g in range(NG)])
    close_first_attention(m, om, t["x"], t["wo"], t["bo"], t["gate"], x1_dram, rows, la)
    first.close()

    beside = Arena(nc)
    sinkhorn(m, la, pi, bias_tables(m, beside, t["amplitudes"], t["sharpness"], t["offsets"], tables, table_range))
    beside.close()
    route(m, pi, slots, tokens, plan)
    experts(m, tokens, plan, t["experts"], rows, queue_y)
    q.load_tables(LN_EXP)

    second = Arena(nc)
    m.v = second("v1", [P, NT, H * VW + HD])
    om = second("om1", [P, NT, D])
    gather = Arena(nc)
    project(m, 1, combine_tokens(m, gather, x1_dram, x2_dram, pi, slots, queue_y),
            [t["w_q"], t["w_k"], t["w_v"]], None, parts)
    gather.close()
    score_bound(m, 1, table_range[:, :])
    q.barrier()
    attend(1, om, tables, [(g, b) for g in range(NG) for b in range(B)])
    close_second_layer(m, om, x2_dram, t["w_gate"], t["b_gate"], t["w8"], t["b8"], t["scales"], out_dram)
    second.close()
    q.emit()


def kernel(**inputs):
    import numpy as np
    import concourse.bacc as bacc
    from concourse import mybir
    from concourse.bass_utils import run_bass_kernel_spmd

    a = {k: np.asarray(v) for k, v in inputs.items()}

    def circulant(c):
        n = np.arange(D)
        return c[(n[None, :] - n[:, None]) % D]

    def by_chunk(v):
        return v.reshape(-1, P).T

    def by_rows(v):
        return v.reshape(3, -1).T

    def expert_rows(wg, wu, wd):
        up = [w.transpose(0, 2, 1).reshape(EXPERTS, DC, P, F).transpose(0, 2, 1, 3).reshape(EXPERTS, P, -1)
              for w in (wg, wu)]
        down = wd.transpose(0, 2, 1).reshape(EXPERTS, FC, P, D).transpose(0, 2, 1, 3).reshape(EXPERTS, P, -1)
        return np.concatenate([*up, down], axis=2)

    w_in = a["L1_attn_w_in"]
    laid = {
        "x": a["L0_attn_x"].reshape(N, D),
        **{f"w{i}": circulant(a[f"L0_attn_w{i}_c"]) for i in "qkvo"},
        **{f"b{i}": by_chunk(a[f"L0_attn_w{i}_b"]) for i in "qk"},
        **{f"b{i}": a[f"L0_attn_w{i}_b"] for i in "vo"},
        "gate": a["L0_ffn_gate_W"].T,
        "experts": expert_rows(a["L0_ffn_W_gate"], a["L0_ffn_W_up"], a["L0_ffn_W_down"]),
        "w_k": w_in[:, 0:D], "w_v": w_in[:, D:2 * D], "w_q": w_in[:, 2 * D:3 * D],
        "w_gate": a["L1_attn_w_gate"], "b_gate": a["L1_attn_b_gate"],
        "amplitudes": by_rows(a["L1_attn_amplitudes"]), "sharpness": by_rows(a["L1_attn_sharpness"]),
        "offsets": by_rows(a["L1_attn_offsets"]),
        "w8": a["L1_ffn_weight_fp8"].T, "b8": a["L1_ffn_bias"],
        "scales": np.concatenate([a["L1_ffn_input_scale"], a["L1_ffn_weight_scale"]]),
    }
    nc = bacc.Bacc("TRN2", target_bir_lowering=False, num_devices=1)
    arrays, tensors = {}, {}
    for name, value in laid.items():
        value = np.ascontiguousarray(value)
        arrays[f"in_{name}"] = value
        tensors[name] = nc.dram_tensor(f"in_{name}", value.shape, mybir.dt.from_np(value.dtype),
                                       kind="ExternalInput").ap()
    out = nc.dram_tensor("out_x", [N, D], FP32, kind="ExternalOutput").ap()
    with ExitStack() as ctx:
        build_program(nc, ctx, tensors, out)
    result = run_bass_kernel_spmd(nc, [arrays], core_ids=[0])
    return result.results[0]["out_x"].reshape(B, S, D)
```

```python
import numpy as np
from contextlib import ExitStack
from itertools import chain

import concourse.bass as bass
from concourse import mybir

FP32 = mybir.dt.float32
BF16 = mybir.dt.bfloat16
FP32R = mybir.dt.float32r
I32 = mybir.dt.int32
ALU = mybir.AluOpType
ACT = mybir.ActivationFunctionType
AX = mybir.AxisListType

P = 128
B, S, D = 4, 1024, 256
N = B * S
NT = N // P
BT = S // P
DC = D // P
H, HD = 16, 16
GH = 4
NG = H // GH
VW = HD + 1
EXPERTS, F = 8, 1024
FC = F // P
LN_EPS = 1e-5
SINKHORN_EPS, SINKHORN_ITERS = 0.05, 20
MOE_TILES = 2 * NT + EXPERTS - 1
SCORE_SCALE = HD ** -0.5
HALF = 512
Q_SLOTS = (0, 0, 0, 1, 1, 2)
K_SLOTS = (0, 1, 2, 0, 1, 0)
QK_ROWS = len(Q_SLOTS) * HD
MAX_PARTS = 3
FAST_RANGE = 60.0
TINY = 1.1754944e-38


class Done:

    def __init__(self, sem, step):
        self.sem, self.step, self.needed, self.value = sem, step, False, None


class Sem:

    def __init__(self, handle):
        self.handle, self.marks = handle, []

    def mark(self, step=1):
        done = Done(self, step)
        self.marks.append(done)
        return done

    def number(self):
        count = 0
        for done in self.marks:
            if done.needed or done.step > 1:
                count += done.step
                done.value = count


class Queues:

    ENGINES = ("tensor", "vector", "scalar", "gpsimd", "sync")

    def __init__(self, nc, ctx, name="main"):
        self.nc, self.ctx, self.name = nc, ctx, name
        self.steps = {e: [] for e in self.ENGINES}
        self.done = {e: Sem(ctx.enter_context(nc.semaphore(f"{name}_{e}_done"))) for e in self.ENGINES}
        self.lanes = {}
        self.branches = []

    def _queue(self, engine, emit, after, done):
        waits = []
        for a in after:
            if a is not None:
                a.needed = True
                waits.append(a)
        self.steps[engine].append((emit, waits, done))
        return done

    def pe(self, emit, *after):
        return self._queue("tensor", emit, after, self.done["tensor"].mark())

    def dve(self, emit, *after):
        return self._queue("vector", emit, after, self.done["vector"].mark())

    def act(self, emit, *after):
        return self._queue("scalar", emit, after, self.done["scalar"].mark())

    def pool(self, emit, *after):
        return self._queue("gpsimd", emit, after, self.done["gpsimd"].mark())

    def lane(self, name):
        if name not in self.lanes:
            self.lanes[name] = Sem(self.ctx.enter_context(self.nc.semaphore(f"{self.name}_{name}")))
        return self.lanes[name]

    def dma(self, lane, out, in_, *after, queue="sync"):
        done = self.lane(lane).mark(16)
        return self._queue(queue, lambda e: e.dma_start(out, in_), after, done)

    def dma_by(self, queue, lane, emit, *after):
        return self._queue(queue, emit, after, self.lane(lane).mark(16))

    def load_tables(self, name):
        self.steps["scalar"].append((lambda e: e.preload_act_table_set(name), [], None))

    def either(self, flag, if_set, if_clear):
        self.branches += [if_set, if_clear]
        for name in self.ENGINES:

            def emit(eng, name=name):
                is_set = eng.value_load(flag, min_val=0, max_val=1)
                with eng.If(is_set > 0):
                    if_set.play(eng, name)
                with eng.If(is_set < 1):
                    if_clear.play(eng, name)

            self.steps[name].append((emit, [], None))

    def barrier(self):
        arrived = [self._queue(e, lambda eng: eng.drain(), (), self.done[e].mark()) for e in self.ENGINES]
        arrived += [lane.marks[-1] for lane in self.lanes.values() if lane.marks]
        for e in self.ENGINES:
            self._queue(e, None, arrived, None)

    def number(self):
        for sem in [*self.done.values(), *self.lanes.values()]:
            sem.number()
        for branch in self.branches:
            branch.number()

    def play(self, eng, name):
        waited = {}
        for emit, waits, done in self.steps[name]:
            for w in waits:
                if waited.get(w.sem, 0) < w.value:
                    eng.wait_ge(w.sem.handle, w.value)
                    waited[w.sem] = w.value
            if emit is not None:
                instruction = emit(eng)
                if done is not None and (done.needed or done.step > 1):
                    instruction.then_inc(done.sem.handle, done.step)

    def emit(self):
        self.number()
        block = self.ctx.enter_context(self.nc.Block())
        block.tensor(lambda eng: self.play(eng, "tensor"))
        block.vector(lambda eng: self.play(eng, "vector"))
        block.scalar(lambda eng: self.play(eng, "scalar"))
        block.gpsimd(lambda eng: self.play(eng, "gpsimd"))
        block.sync(lambda eng: self.play(eng, "sync"))


LN_EXP = "natural_log_exp_and_others"


class Ring:

    def __init__(self, n):
        self.n, self.at, self.readers = n, 0, [()] * n

    def take(self):
        slot = self.at
        self.at = (slot + 1) % self.n
        return slot, self.readers[slot]

    def free(self, slot, *readers):
        self.readers[slot] = readers


class Arena:

    def __init__(self, nc):
        self.nc, self.stack = nc, ExitStack()

    def __call__(self, name, shape, dtype=FP32):
        return self.stack.enter_context(self.nc.sbuf_tensor(name, shape, dtype))

    def close(self):
        self.stack.close()


class Machine:
    pass


def make_constants(m):
    q, sb = m.q, m.keep
    m.ident = sb("ident", [P, P])
    m.ident16 = sb("ident16", [P, P], BF16)
    m.ones = sb("ones", [P, P])
    m.head_ones = sb("head_ones", [P, P // HD], BF16)
    m.ones16 = sb("ones16", [P, P // HD], BF16)
    m.before = sb("before", [P, P])
    z = q.pool(lambda e: e.memset(m.ident[:, :], 0.0))
    z16 = q.pool(lambda e: e.memset(m.ident16[:, :], 0.0))
    o = q.pool(lambda e: e.memset(m.ones[:, :], 1.0))
    o16 = q.pool(lambda e: e.memset(m.ones16[:, :], 1.0))
    i1 = q.pool(lambda e: e.affine_select(out=m.ident[:, :], in_=m.ident[:, :], compare_op=ALU.not_equal,
                                          fill=1.0, base=0, pattern=[[-1, P]], channel_multiplier=1), z)
    i2 = q.pool(lambda e: e.affine_select(out=m.ident16[:, :], in_=m.ident16[:, :],
                                          compare_op=ALU.not_equal, fill=1.0, base=0,
                                          pattern=[[-1, P]], channel_multiplier=1), z16)
    h1 = q.pool(lambda e: e.affine_select(out=m.head_ones[:, :], in_=m.ones16[:, :],
                                          compare_op=ALU.is_ge, fill=0.0, base=0,
                                          pattern=[[-HD, P // HD]], channel_multiplier=1), o16)
    h2 = q.pool(lambda e: e.affine_select(out=m.head_ones[:, :], in_=m.head_ones[:, :],
                                          compare_op=ALU.is_ge, fill=0.0, base=HD - 1,
                                          pattern=[[HD, P // HD]], channel_multiplier=-1), h1)
    b1 = q.pool(lambda e: e.affine_select(out=m.before[:, :], in_=m.ones[:, :], compare_op=ALU.is_ge,
                                          fill=0.0, base=-1, pattern=[[1, P]], channel_multiplier=-1), o)
    m.constants = q.pool(lambda e: e.memset(m.ones16[:, :], 1.0), i1, i2, h2, b1)


def across(row, parts):
    return bass.AP(tensor=row.tensor, offset=row.offset, ap=[[0, parts], *[list(x) for x in row.ap]])


def layernorm(m, w, x, xn, *ready, factor=None):
    steps = layernorm_steps(m, w, x, xn, *ready, factor=factor)
    while True:
        try:
            next(steps)
        except StopIteration as end:
            return end.value


def layernorm_steps(m, w, x, xn, *ready, factor=None):
    q = m.q
    stats, mv, v, y, t = w["stats"], w["mv"], w["v"], w["y"], w["t"]
    marks = [q.dve(lambda e, i=i: e.bn_stats(stats[:, i, :], x[:, i, :]), *ready) for i in range(BT)]
    marks = [q.dve(lambda e, i=i: e.bn_aggr(mv[:, i, :], stats[:, i, :]), marks[i]) for i in range(BT)]
    v1 = q.dve(lambda e: e.tensor_scalar(v[:, :], mv[:, :, 1], LN_EPS, None, ALU.add), marks[-1])
    yield
    l = q.act(lambda e: e.activation(y[:, :], v[:, :], ACT.Ln), v1)
    l = q.act(lambda e: e.activation(y[:, :], y[:, :], ACT.Exp, scale=-0.5), l)
    yield
    a = q.dve(lambda e: e.tensor_tensor(t[:, :], y[:, :], y[:, :], ALU.mult), l)
    a = q.dve(lambda e: e.tensor_tensor(t[:, :], t[:, :], v[:, :], ALU.mult), a)
    a = q.dve(lambda e: e.tensor_scalar(t[:, :], t[:, :], -0.5, 1.5, ALU.mult, ALU.add), a)
    a = q.dve(lambda e: e.tensor_tensor(y[:, :], y[:, :], t[:, :], ALU.mult), a)
    if factor is not None:
        a = q.dve(lambda e: e.tensor_scalar(y[:, :], y[:, :], factor, None, ALU.mult), a)
    for i in range(BT):
        last = q.dve(lambda e, i=i: e.tensor_scalar(xn[:, i, :], x[:, i, :], mv[:, i, 0:1], y[:, i:i + 1],
                                                    ALU.subtract, ALU.mult), a)
    return last


def layernorm_scratch(sb, name):
    return {"stats": sb(name + "stats", [P, BT, 6]), "mv": sb(name + "mv", [P, BT, 2]),
            "v": sb(name + "v", [P, BT]), "y": sb(name + "y", [P, BT]), "t": sb(name + "t", [P, BT])}


def transpose_batch(m, ring, src, dst, ready, dst_free=()):
    q = m.q
    out = []
    for c in range(DC):
        slot, free = ring.take()
        ps = m.psum[:, slot * S:(slot + 1) * S]
        for t in range(BT):
            tr = q.pe(lambda e, t=t, c=c, ps=ps: e.transpose(ps[:, t * P:(t + 1) * P],
                                                             src[:, t, c * P:(c + 1) * P], m.ident[:, :]),
                      ready, m.constants, *free)
        cp = q.act(lambda e, c=c, ps=ps: e.activation(dst[:, c, :], ps, ACT.Copy), tr, *dst_free)
        ring.free(slot, cp)
        out.append(cp)
    return out


def project(m, layer, open_batch, weights, biases, parts):
    q, nc = m.q, m.nc
    sb = Arena(nc)
    n = f"L{layer}_"
    w = [sb(n + f"w{i}", [P, DC, D]) for i in range(3)]
    b_qk = sb(n + "b_qk", [P, 2, DC])
    b_v = sb(n + "b_v", [P, D])
    x = sb(n + "x", [P, 2, BT, D])
    xn = sb(n + "xn", [P, 2, BT, D])
    xT = sb(n + "xT", [P, 2, DC, S])
    split = [sb(n + f"part{i}", [P, 2, S], BF16) for i in range(3)]
    rest = sb(n + "rest", [P, 2, S])
    square = sb(n + "square", [P, 2, S], BF16)
    lnw = layernorm_scratch(sb, n)
    nmax = m.norms
    low_by = q.pool if layer == 0 else q.dve

    got_w = [q.dma(n + "w_in", w[i][:, :, :], weights[i].rearrange("(c p) n -> p c n", p=P), queue="scalar")
             for i in range(3)][-1]
    if biases is None:
        zb = q.dve(lambda e: e.memset(b_qk[:, :, :], 0.0))
        zv = q.dve(lambda e: e.memset(b_v[:, :], 0.0))
        bias_ready = (zb, zv)
    else:
        for i in range(2):
            last = q.dma(n + "b_in", b_qk[:, i, :], biases[i], queue="scalar")
        last = q.dma(n + "b_in", b_v[:, :], across(biases[2], P), queue="scalar")
        bias_ready = (last,)
    ones_in = low_by(lambda e: e.memset(m.v[:, :, :], 1.0))

    ring = Ring(4)
    x_ring, xT_ring, part_ring, rest_ring, square_ring = Ring(2), Ring(2), Ring(2), Ring(2), Ring(2)

    def fetch(b):
        xs, free = x_ring.take()
        return xs, open_batch(b, xs, x[:, xs, :, :], free)

    def normalise(fetched):
        xs, combine = fetched
        got, kept = combine()
        return xs, kept, layernorm(m, lnw, x[:, xs, :, :], xn[:, xs, :, :], got)

    def turn(xs, kept, normed):
        ts, t_free = xT_ring.take()
        made = transpose_batch(m, ring, xn[:, xs, :, :], xT[:, ts, :, :], normed, t_free)
        x_ring.free(xs, *made, *kept)
        return ts, made

    ahead = turn(*normalise(fetch(0)))
    fetched = fetch(1)
    waiting = []
    for b in range(B):
        ts, made = ahead
        if b + 1 < B:
            normal = normalise(fetched)
        for op in range(2):
            for c in range(DC):
                slot, free = ring.take()
                ps = m.psum[:, slot * S:(slot + 1) * S]
                for j in range(S // HALF):
                    for k in range(DC):
                        mm = q.pe(lambda e, op=op, c=c, j=j, k=k, ps=ps, ts=ts: e.matmul(
                            ps[:, j * HALF:(j + 1) * HALF], w[op][:, k, c * P:(c + 1) * P],
                            xT[:, ts, k, j * HALF:(j + 1) * HALF], start=(k == 0), stop=(k == DC - 1)),
                            got_w, *made, *free)
                bias = b_qk[:, op, c:c + 1]
                s, s_free = part_ring.take()
                hi = q.act(lambda e, s=s, ps=ps, bias=bias: e.activation(split[0][:, s, :], ps, ACT.Identity,
                                                                         bias=bias), mm, *bias_ready, *s_free)
                z, z_free = square_ring.take()
                sq = q.act(lambda e, z=z, s=s: e.activation(square[:, z, :], split[0][:, s, :], ACT.Square),
                           hi, *z_free)
                r, r_free = rest_ring.take()
                rs = q.dve(lambda e, s=s, r=r, ps=ps, bias=bias: e.scalar_tensor_tensor(
                    out=rest[:, r, :], in0=ps, scalar=bias, in1=split[0][:, s, :], op0=ALU.add,
                    op1=ALU.subtract), hi, *r_free)
                ring.free(slot, rs)
                mid = q.act(lambda e, s=s, r=r: e.activation(split[1][:, s, :], rest[:, r, :], ACT.Copy), rs)
                low = low_by(lambda e, s=s, r=r: e.tensor_tensor(split[2][:, s, :], rest[:, r, :],
                                                                 split[1][:, s, :], ALU.subtract), mid, *s_free)
                rest_ring.free(r, low)
                sent = [q.dma(n + f"part_out{s}", parts[op, i, b, c * P:(c + 1) * P, :], split[i][:, s, :], done)
                        for i, done in enumerate((hi, mid, low))][-1]
                part_ring.free(s, sent, sq)

                def norms(op=op, c=c, b=b, z=z, sq=sq):
                    nslot, n_free = ring.take()
                    nps = m.psum[0:P // HD, nslot * S:(nslot + 1) * S]
                    for j in range(S // HALF):
                        nm = q.pe(lambda e, j=j: e.matmul(
                            nps[:, j * HALF:(j + 1) * HALF], m.head_ones[:, :],
                            square[:, z, j * HALF:(j + 1) * HALF], start=True, stop=True), sq, *n_free)
                    square_ring.free(z, nm)
                    mx = q.dve(lambda e: e.reduce_max(nmax[:, op, c * B + b:c * B + b + 1], nps, AX.X), nm)
                    ring.free(nslot, mx)

                if waiting:
                    waiting.pop(0)()
                waiting.append(norms)
        if b + 1 < B:
            ahead = turn(*normal)
        if b + 2 < B:
            fetched = fetch(b + 2)
        for half in range(2):
            slot, free = ring.take()
            ps = m.psum[:, slot * S:(slot + 1) * S]
            for i in range(BT // 2):
                t = half * (BT // 2) + i
                for k in range(DC):
                    mm = q.pe(lambda e, i=i, t=t, k=k, ps=ps, ts=ts: e.matmul(
                        ps[:, i * D:(i + 1) * D], xT[:, ts, k, t * P:(t + 1) * P], w[2][:, k, :],
                        start=(k == 0), stop=(k == DC - 1)), *free)
            t0 = b * BT + half * (BT // 2)
            for i in range(BT // 2):
                vd = q.dve(lambda e, i=i, t0=t0, ps=ps: e.tensor_tensor(
                    m.v[:, t0 + i, 0:H * VW].rearrange("p (h w) -> p h w", w=VW)[:, :, 0:HD],
                    ps[:, i * D:(i + 1) * D].rearrange("p (h w) -> p h w", w=HD),
                    b_v[:, :].rearrange("p (h w) -> p h w", w=HD), ALU.add), mm, ones_in, *bias_ready)
            ring.free(slot, vd)
            if waiting:
                waiting.pop(0)()
        xT_ring.free(ts, mm)
    q.barrier()
    sb.close()


def load_tokens(m, x_dram):
    src = x_dram.rearrange("(b t p) d -> b p t d", p=P, t=BT)

    def open_batch(b, slot, x, free):
        got = m.q.dma(f"x_in{slot}", x, src[b, :, :, :], *free)
        return lambda: (got, ())

    return open_batch


def score_bound(m, layer, table_range):
    q = m.q
    s = m.bound
    a = q.dve(lambda e: e.tensor_tensor(s[0:H // DC, 0:DC * B], m.norms[:, 0, :], m.norms[:, 1, :], ALU.mult))
    a = q.dve(lambda e: e.reduce_max(s[0:H // DC, 8:9], s[0:H // DC, 0:DC * B], AX.X), a)
    t = q.pe(lambda e: e.transpose(m.psum[0:1, 0:H // DC], s[0:H // DC, 8:9],
                                   m.ident[0:H // DC, 0:H // DC]), a)
    a = q.dve(lambda e: e.reduce_max(s[0:1, 9:10], m.psum[0:1, 0:H // DC], AX.X), t)
    a = q.dve(lambda e: e.tensor_scalar(s[0:1, 9:10], s[0:1, 9:10], 1e-12, 1e15, ALU.max, ALU.min), a)
    a = q.act(lambda e: e.activation(s[0:1, 9:10], s[0:1, 9:10], ACT.Ln), a)
    a = q.act(lambda e: e.activation(s[0:1, 10:11], s[0:1, 9:10], ACT.Exp, scale=0.5), a)
    a = q.dve(lambda e: e.tensor_scalar(s[0:1, 10:11], s[0:1, 10:11], 1.01 * SCORE_SCALE, None, ALU.mult), a)
    if table_range is not None:
        hi = q.dve(lambda e: e.tensor_tensor(s[0:1, 11:12], s[0:1, 10:11], table_range[:, 0:1], ALU.add), a)
        lo = q.dve(lambda e: e.tensor_tensor(s[0:1, 12:13], s[0:1, 10:11], table_range[:, 1:2], ALU.add), a)
    else:
        hi = q.dve(lambda e: e.tensor_copy(s[0:1, 11:12], s[0:1, 10:11]), a)
        lo = q.dve(lambda e: e.tensor_copy(s[0:1, 12:13], s[0:1, 10:11]), a)
    a = q.dve(lambda e: e.tensor_tensor(s[0:1, 13:14], s[0:1, 11:12], s[0:1, 12:13], ALU.add), hi, lo)
    flag = q.dve(lambda e: e.tensor_scalar(m.flag[0:1, 0:1], s[0:1, 13:14], FAST_RANGE, None, ALU.is_le), a)
    b = q.pe(lambda e: e.matmul(m.psum[:, HALF:HALF + 1], m.ones[0:1, :], s[0:1, 11:12], start=True, stop=True), a)
    c = q.dve(lambda e: e.tensor_scalar(m.shift[:, 0:1], m.psum[:, HALF:HALF + 1], -1.0, None, ALU.mult), b)
    return flag, c


def attention(m, layer, parts, tables, om, order, row_max, beside=None):
    q, nc = m.q, m.nc
    sb = Arena(nc)
    n = f"A{layer}{'r' if row_max else 'f'}_"
    rows = QK_ROWS + MAX_PARTS if row_max else QK_ROWS
    qa = sb(n + "qa", [P, 2, GH, S], BF16)
    ka = sb(n + "ka", [P, 2, GH, S], BF16)
    n_probs = 8
    probs = sb(n + "probs", [P, n_probs, S])
    o_sb = sb(n + "o_sb", [P, 2, S])
    rec = sb(n + "rec", [P, 2, BT, GH])
    TW = 2 * S - P
    if tables is not None:
        bias = sb(n + "bias", [P, 1 if row_max else 2, GH, TW])
        if row_max:
            mirrored = sb(n + "mirrored", [P, 1, GH, TW])
    s_ring, p_ring, qk_ring, o_ring, t_ring = Ring(3), Ring(n_probs), Ring(2), Ring(2), Ring(1 if row_max else 2)
    O = m.psum[:, 3 * S:4 * S]
    o_free = ()
    src = parts.rearrange("o i b (h d) t -> o i b d h t", d=HD)
    q.load_tables(LN_EXP)
    if row_max:
        nm = sb(n + "nm", [P, GH * BT])
        rm = sb(n + "rm", [GH * BT, P])
        rmp = sb(n + "rmp", [GH * BT, MAX_PARTS, P], BF16)
        one = q.pool(lambda e: e.memset(ka[QK_ROWS:P, :, :, :], 1.0))

    def load(g, b):
        s, free = qk_ring.take()
        for op, slots, dst in ((0, Q_SLOTS, qa), (1, K_SLOTS, ka)):
            for r, part in enumerate(slots):
                got = q.dma(n + f"qk_in{s}", dst[r * HD:(r + 1) * HD, s, :, :],
                            src[op, part, b, :, g * GH:(g + 1) * GH, :], *free)
        return s, got

    def load_table(g):
        s, free = t_ring.take()
        for i in range(GH):
            for which, dst in enumerate((bias, mirrored) if row_max else (bias,)):
                row = tables[which, g * GH + i, :]
                got = q.dma(n + f"bias_in{s}", dst[:, s, i, :],
                            bass.AP(tensor=row.tensor, offset=row.offset, ap=[[1, P], [1, TW]]), *free)
        return s, got

    todo = []
    jobs = []
    if beside is not None:
        beside.start()

    def finish(g, b, os_, moved):
        slot, free = s_ring.take()
        ps = m.psum[:, slot * S:(slot + 1) * S]
        for t in range(BT):
            tr = q.pe(lambda e, t=t, os_=os_, ps=ps: e.transpose(
                ps[:, t * P:(t + 1) * P], o_sb[:, os_, t * P:(t + 1) * P], m.ident[:, :]), moved, *free)
        v = ps.rearrange("p (t i c) -> p t i c", i=GH, c=P // GH)
        rc = q.dve(lambda e, v=v, os_=os_: e.reciprocal(rec[:, os_, :, :], v[:, :, :, HD]), tr)
        r = rec[:, os_, :, :]
        r = bass.AP(tensor=r.tensor, offset=r.offset, ap=[*[list(a) for a in r.ap], [0, HD]])
        nr = q.dve(lambda e, v=v, r=r, g=g, b=b: e.tensor_tensor(
            om[:, b * BT:(b + 1) * BT, g * GH * HD:(g + 1) * GH * HD].rearrange("p t (i d) -> p t i d", d=HD),
            v[:, :, :, 0:HD], r, ALU.mult), rc)
        s_ring.free(slot, nr)
        o_ring.free(os_, nr)
        if beside is not None and g == order[-1][0]:
            jobs.append(beside.batch(b, s_ring, nr))

    def find_row_max(b, s, got, t_slot, t_got):
        for i in range(GH):
            for t in range(BT):
                slot, free = s_ring.take()
                ps = m.psum[:, slot * S:(slot + 1) * S]
                for j in range(S // HALF):
                    mm = q.pe(lambda e, i=i, t=t, j=j, ps=ps: e.matmul(
                        ps[:, j * HALF:(j + 1) * HALF], qa[0:QK_ROWS, s, i, t * P:(t + 1) * P],
                        ka[0:QK_ROWS, s, i, j * HALF:(j + 1) * HALF], start=True, stop=True), got, *free)
                if tables is not None:
                    row = mirrored[:, t_slot, i, P * t:P * t + S][:, ::-1]
                    mm = q.dve(lambda e, ps=ps, row=row: e.scalar_tensor_tensor(
                        out=ps, in0=ps, scalar=SCORE_SCALE, in1=row, op0=ALU.mult, op1=ALU.add), mm, t_got)
                mx = q.dve(lambda e, i=i, t=t, ps=ps: e.tensor_reduce(
                    out=nm[:, i * BT + t:i * BT + t + 1], in_=ps, axis=AX.X, op=ALU.max, negate=True), mm)
                s_ring.free(slot, mx)
        if tables is not None:
            mx = q.dve(lambda e: e.tensor_scalar(nm[:, :], nm[:, :], 1.0 / SCORE_SCALE, None, ALU.mult), mx)
        slot, free = s_ring.take()
        ps = m.psum[:, slot * S:(slot + 1) * S]
        tr = q.pe(lambda e: e.transpose(ps[0:GH * BT, 0:P], nm[:, :], m.ident[:, :]), mx, *free)
        a = q.dve(lambda e: e.tensor_copy(rmp[:, 0, :], ps[0:GH * BT, 0:P]), tr)
        a = q.dve(lambda e: e.tensor_tensor(rm[:, :], ps[0:GH * BT, 0:P], rmp[:, 0, :], ALU.subtract), a)
        s_ring.free(slot, a)
        a = q.dve(lambda e: e.tensor_copy(rmp[:, 1, :], rm[:, :]), a)
        a = q.dve(lambda e: e.tensor_tensor(rmp[:, 2, :], rm[:, :], rmp[:, 1, :], ALU.subtract), a)
        for i in range(MAX_PARTS):
            row = QK_ROWS + i
            got = q.dma(n + "max_in", qa[row:row + 1, s, :, :].rearrange("a h t -> a (h t)"),
                        rmp[:, i, :], a)
        q.dve(lambda e: e.memset(rm[:, 0:1], 0.0), got)
        return got

    groups = list(order)
    loads = {0: load(*groups[0])}
    table_of = {}
    if tables is not None:
        table_of[groups[0][0]] = load_table(groups[0][0])
    quads = []

    def queue_pv(j):
        nonlocal o_free
        g, b, kt, slots, exps = quads[0]
        for i in range(GH):
            h = g * GH + i
            pv = q.pe(lambda e, i=i, j=j, h=h, kt=kt, b=b, sl=slots[i]: e.matmul(
                O[32 * i:32 * (i + 1), j * HALF:(j + 1) * HALF],
                m.v[:, b * BT + kt, h * VW:h * VW + 32], probs[:, sl, j * HALF:(j + 1) * HALF],
                start=(kt == 0), stop=(kt == BT - 1)), *exps, *(o_free if kt == 0 else ()))
        if j == 0:
            return
        quads.pop(0)
        for sl in slots:
            p_ring.free(sl, pv)
        if kt == BT - 1:
            os_, free = o_ring.take()
            if tables is None:
                moved = q.dve(lambda e, os_=os_: e.tensor_copy(o_sb[:, os_, :], O), pv, *free)
            else:
                moved = q.act(lambda e, os_=os_: e.activation(o_sb[:, os_, :], O, ACT.Copy), pv, *free)
            o_free = (moved,)
            todo.append([g, b, os_, moved])

    def drain():
        while quads:
            for j in range(S // HALF):
                queue_pv(j)
        while todo:
            finish(*todo.pop(0))
        while jobs:
            for _ in jobs.pop(0):
                pass

    for at, (g, b) in enumerate(groups):
        s, got = loads.pop(at)
        ready = (got,)
        t_slot = None
        if tables is not None:
            if g not in table_of:
                table_of[g] = load_table(g)
            t_slot, t_got = table_of[g]
        if row_max:
            drain()
            ready = (got, find_row_max(b, s, got, t_slot, t_got if tables is not None else None), one)
        for kt in range(BT):
            slots, exps = [], []
            for i in range(GH):
                slot, free = s_ring.take()
                ps = m.psum[:, slot * S:(slot + 1) * S]
                for j in range(S // HALF):
                    mm = q.pe(lambda e, i=i, j=j, kt=kt, s=s, ps=ps: e.matmul(
                        ps[:, j * HALF:(j + 1) * HALF], ka[0:rows, s, i, kt * P:(kt + 1) * P],
                        qa[0:rows, s, i, j * HALF:(j + 1) * HALF], start=True, stop=True), *ready, *free)
                sl, p_free = p_ring.take()
                shift = {} if row_max else {"bias": m.shift[:, 0:1]}
                if tables is None:
                    ex = q.act(lambda e, sl=sl, ps=ps, shift=shift: e.activation(
                        probs[:, sl, :], ps, ACT.Exp, scale=SCORE_SCALE, **shift), mm, *p_free)
                    s_ring.free(slot, ex)
                else:
                    row = bias[:, t_slot, i, P * kt:P * kt + S][:, ::-1]
                    biased = q.dve(lambda e, sl=sl, ps=ps, row=row: e.scalar_tensor_tensor(
                        out=probs[:, sl, :], in0=ps, scalar=SCORE_SCALE, in1=row, op0=ALU.mult, op1=ALU.add),
                        mm, t_got, *p_free)
                    s_ring.free(slot, biased)
                    ex = q.act(lambda e, sl=sl, shift=shift: e.activation(
                        probs[:, sl, :], probs[:, sl, :], ACT.Exp, **shift), biased)
                slots.append(sl)
                exps.append(ex)
                if i >= 2 and quads:
                    queue_pv(i - 2)
                if i == 3 and kt == 2 and todo:
                    finish(*todo.pop(0))
                if i == 1 and jobs and next(jobs[0], jobs) is jobs:
                    jobs.pop(0)
            quads.append((g, b, kt, slots, exps))
            if kt == 0 and at + 1 < len(groups):
                loads[at + 1] = load(*groups[at + 1])
                g1 = groups[at + 1][0]
                if tables is not None and not row_max and g1 not in table_of:
                    table_of[g1] = load_table(g1)
        qk_ring.free(s, mm)
        if tables is not None and not any(x[0] == g for x in groups[at + 1:]):
            t_ring.free(t_slot, biased)
    drain()
    q.barrier()
    sb.close()


def widen(ap, n):
    return bass.AP(tensor=ap.tensor, offset=ap.offset, ap=[*[list(a) for a in ap.ap], [0, n]])


def repeat(ap, n):
    a = [list(x) for x in ap.ap]
    return bass.AP(tensor=ap.tensor, offset=ap.offset, ap=[a[0], [0, n], *a[1:]])


class FirstClose:

    def __init__(self, m, om, x_dram, wo_dram, bo_dram, gate_dram, x1_dram, rows_dram, la):
        self.m, self.om, self.la = m, om, la
        self.sb = sb = Arena(m.nc)
        self.wo = sb("wo", [P, DC, D])
        self.bo = sb("bo", [P, D])
        self.gate = sb("gate", [P, DC, EXPERTS])
        self.x, self.x1, self.xn1 = (sb(f"c_{name}", [P, BT, D]) for name in ("x", "x1", "xn1"))
        self.omT, self.xnT = (sb(f"c_{name}", [P, DC, S]) for name in ("omT", "xnT"))
        self.lnw = layernorm_scratch(sb, "c_")
        self.x_src = x_dram.rearrange("(b t p) d -> b p t d", p=P, t=BT)
        self.x1_dst = x1_dram.rearrange("(b t p) d -> b p t d", p=P, t=BT)
        self.rows_dst = rows_dram.rearrange("(p b t) d -> b p t d", b=B, t=BT)
        for dst, src in ((self.wo[:, :, :], wo_dram.rearrange("(c p) n -> p c n", p=P)),
                         (self.bo[:, :], across(bo_dram, P)),
                         (self.gate[:, :, :], gate_dram.rearrange("(c p) n -> p c n", p=P))):
            m.q.dma("close_w", dst, src)

    def start(self):
        self.x_free = self.x1_free = self.xn1_free = self.omT_free = self.xnT_free = ()

    def turn(self, src, dst, ring, ready, dst_free):
        q, made = self.m.q, []
        for c in range(DC):
            slot, free = ring.take()
            ps = self.m.psum[:, slot * S:(slot + 1) * S]
            for t in range(BT):
                tr = q.pe(lambda e, t=t, c=c, ps=ps: e.transpose(
                    ps[:, t * P:(t + 1) * P], src[:, t, c * P:(c + 1) * P], self.m.ident[:, :]), ready, *free)
            cp = q.dve(lambda e, c=c, ps=ps: e.tensor_copy(dst[:, c, :], ps), tr, *dst_free)
            ring.free(slot, cp)
            made.append(cp)
            yield
        return made

    def batch(self, b, ring, ready):
        m, q = self.m, self.m.q
        x, x1, xn1, omT, xnT = self.x, self.x1, self.xn1, self.omT, self.xnT
        got = q.dma("c_x_in", x[:, :, :], self.x_src[b, :, :, :], *self.x_free)
        biased = q.pool(lambda e: e.tensor_tensor(x[:, :, :], x[:, :, :], repeat(self.bo[:, :], BT), ALU.add), got)
        made = yield from self.turn(self.om[:, b * BT:(b + 1) * BT, :], omT, ring, ready, self.omT_free)
        for t0 in range(0, BT, 2):
            slot, free = ring.take()
            ps = m.psum[:, slot * S:slot * S + 2 * D]
            for t in (t0, t0 + 1):
                for k in range(DC):
                    mm = q.pe(lambda e, t=t, k=k, ps=ps, t0=t0: e.matmul(
                        ps[:, (t - t0) * D:(t - t0 + 1) * D], omT[:, k, t * P:(t + 1) * P], self.wo[:, k, :],
                        start=(k == 0), stop=(k == DC - 1)), *made, *free)
            added = q.dve(lambda e, t0=t0, ps=ps: e.tensor_tensor(
                x1[:, t0:t0 + 2, :], ps.rearrange("p (t d) -> p t d", d=D), x[:, t0:t0 + 2, :], ALU.add),
                mm, biased, *self.x1_free)
            ring.free(slot, added)
            yield
        self.omT_free, self.x_free = (mm,), (added,)
        sent = q.dma("x1_out", self.x1_dst[b, :, :, :], x1[:, :, :], added)
        normed = yield from layernorm_steps(m, self.lnw, x1, xn1, added, *self.xn1_free)
        self.x1_free = (normed, sent)
        sent = q.dma("rows_out", self.rows_dst[b, :, :, :], xn1[:, :, :], normed)
        yield
        made = yield from self.turn(xn1, xnT, ring, normed, self.xnT_free)
        self.xn1_free = (*made, sent)
        slot, free = ring.take()
        ps = m.psum[:, slot * S:slot * S + BT * EXPERTS]
        for t in range(BT):
            for k in range(DC):
                mm = q.pe(lambda e, t=t, k=k, ps=ps: e.matmul(
                    ps[:, t * EXPERTS:(t + 1) * EXPERTS], xnT[:, k, t * P:(t + 1) * P], self.gate[:, k, :],
                    start=(k == 0), stop=(k == DC - 1)), *made, *free)
        self.xnT_free = (mm,)
        scaled = q.dve(lambda e, ps=ps: e.tensor_scalar(
            self.la[:, b * BT:(b + 1) * BT, :], ps.rearrange("p (t e) -> p t e", e=EXPERTS),
            -1.0 / SINKHORN_EPS, None, ALU.mult), mm)
        ring.free(slot, scaled)


def sinkhorn(m, la, pi, beside):
    next(beside)
    q = m.q
    sb = Arena(m.nc)
    E = EXPERTS
    mx = sb("s_mx", [P, NT])
    ex = sb("s_ex", [P, NT, E])
    sm = sb("s_sm", [P, NT])
    cm = sb("s_cm", [P, E])
    gm = sb("s_gm", [E, 1])
    dg = sb("s_dg", [E, E])
    cs = sb("s_cs", [P, E])
    cl = sb("s_cl", [P, E])
    ps_t = m.psum[0:E, 0:P]
    ps_m = m.psum[:, HALF:HALF + E]
    ps_s = m.psum[:, 2 * HALF:2 * HALF + E]
    by_expert = la[:, :, :].rearrange("p t e -> p e t")
    a = None
    for _ in range(SINKHORN_ITERS):
        next(beside, None)
        a = q.dve(lambda e: e.reduce_max(mx[:, :], la[:, :, :], AX.X), a)
        a = q.dve(lambda e: e.tensor_tensor(la[:, :, :], la[:, :, :], widen(mx[:, :], E), ALU.subtract), a)
        a = q.act(lambda e: e.activation(ex[:, :, :], la[:, :, :], ACT.Exp), a)
        a = q.dve(lambda e: e.reduce_sum(sm[:, :], ex[:, :, :], AX.X), a)
        a = q.act(lambda e: e.activation(sm[:, :], sm[:, :], ACT.Ln), a)
        a = q.dve(lambda e: e.tensor_tensor(la[:, :, :], la[:, :, :], widen(sm[:, :], E), ALU.subtract), a)
        a = q.dve(lambda e: e.reduce_max(cm[:, :], by_expert, AX.X), a)
        a = q.pe(lambda e: e.transpose(ps_t, cm[:, :], m.ident[:, :]), a)
        a = q.dve(lambda e: e.reduce_max(gm[:, :], ps_t, AX.X), a)
        a = q.dve(lambda e: e.tensor_scalar(dg[:, :], m.ident[0:E, 0:E], gm[:, 0:1], None, ALU.mult), a)
        a = q.pe(lambda e: e.matmul(ps_m, m.ones[0:E, :], dg[:, :], start=True, stop=True), a)
        a = q.dve(lambda e: e.tensor_tensor(la[:, :, :], la[:, :, :], repeat(ps_m, NT), ALU.subtract), a)
        a = q.act(lambda e: e.activation(ex[:, :, :], la[:, :, :], ACT.Exp), a)
        a = q.dve(lambda e: e.reduce_sum(cs[:, :], ex[:, :, :].rearrange("p t e -> p e t"), AX.X), a)
        a = q.pe(lambda e: e.matmul(ps_s, m.ones[:, :], cs[:, :], start=True, stop=True), a)
        a = q.act(lambda e: e.activation(cl[:, :], ps_s, ACT.Ln), a)
        a = q.dve(lambda e: e.tensor_tensor(la[:, :, :], la[:, :, :], repeat(cl[:, :], NT), ALU.subtract), a)
    for _ in beside:
        pass
    q.act(lambda e: e.activation(pi[:, :, :], la[:, :, :], ACT.Exp), a)
    q.barrier()
    sb.close()


W_BUFS = 2
AHEAD = W_BUFS + 1


def route(m, pi, slots, tokens, plan, fetch_first_expert):
    q = m.q
    sb = Arena(m.nc)
    E = EXPERTS
    key = sb("r_key", [P, NT, E])
    top = sb("r_top", [P, NT])
    eq = sb("r_eq", [P, NT, E])
    rank = sb("r_rank", [P, E])
    pick = [sb(f"r_pick{k}", [P, NT, E]) for k in range(2)]
    both = sb("r_both", [P, NT, E])
    pos = sb("r_pos", [P, NT, E])
    total = sb("r_total", [P, NT, E])
    scan = [sb(f"r_scan{k}", [P, NT, E]) for k in range(2)]
    tiles = sb("r_tiles", [P, E])
    tiles_i = sb("r_tiles_i", [P, E], I32)
    upto = [sb(f"r_upto{k}", [P, E]) for k in range(2)]
    prod = sb("r_prod", [P, NT, E])
    row = sb("r_row", [P, 2, NT])
    place_i = sb("r_place_i", [P, 2, 2 * NT], I32)
    place = sb("r_place", [P, 2, 2 * NT])
    name = sb("r_name", [P, NT])
    n_hot = 8
    row_hot = sb("r_row_hot", [P, n_hot, P])
    tile_hot = sb("r_tile_hot", [P, n_hot, MOE_TILES])
    count_up = sb("r_count_up", [P, P])
    J = MOE_TILES
    j_iota = sb("r_j", [1, J])
    ge = sb("r_ge", [1, J, E])
    ex = sb("r_ex", [1, J])
    new = sb("r_new", [1, J])
    run = [sb(f"r_run{k}", [1, J]) for k in range(2)]
    other = sb("r_other", [1, J])
    seat = sb("r_seat", [1, E])
    score = sb("r_score", [1, E])
    later = sb("r_later", [1, E, E])
    follower = sb("r_follower", [1, AHEAD, E])
    is_tile = sb("r_is_tile", [1, J, E])
    ahead = sb("r_ahead", [1, AHEAD, J])
    r0 = q.pool(lambda e: e.iota(rank[:, :], pattern=[[-1, E]], base=E, channel_multiplier=0,
                                 allow_small_or_imprecise_dtypes=True))
    j0 = q.pool(lambda e: e.iota(j_iota[:, :], pattern=[[1, J]], base=0, channel_multiplier=0,
                                 allow_small_or_imprecise_dtypes=True))
    c0 = q.pool(lambda e: e.iota(count_up[:, :], pattern=[[1, P]], base=0, channel_multiplier=0,
                                 allow_small_or_imprecise_dtypes=True))
    j0 = q.pool(lambda e: e.iota(name[:, :], pattern=[[1, NT]], base=0, channel_multiplier=NT,
                                 allow_small_or_imprecise_dtypes=True), j0, c0)
    a = q.dve(lambda e: e.tensor_scalar(eq[:, :, :], pi[:, :, :], TINY, None, ALU.is_ge), r0, j0)
    a = q.dve(lambda e: e.tensor_tensor(key[:, :, :], pi[:, :, :], eq[:, :, :], ALU.mult), a)
    for k in range(2):
        a = q.dve(lambda e: e.reduce_max(top[:, :], key[:, :, :], AX.X), a)
        a = q.dve(lambda e: e.tensor_tensor(eq[:, :, :], key[:, :, :], widen(top[:, :], E), ALU.is_equal), a)
        a = q.dve(lambda e: e.tensor_tensor(eq[:, :, :], eq[:, :, :], repeat(rank[:, :], NT), ALU.mult), a)
        a = q.dve(lambda e: e.reduce_max(top[:, :], eq[:, :, :], AX.X), a)
        a = q.dve(lambda e, k=k: e.tensor_tensor(pick[k][:, :, :], eq[:, :, :], widen(top[:, :], E),
                                                 ALU.is_equal), a)
        if k == 0:
            a = q.dve(lambda e: e.scalar_tensor_tensor(out=key[:, :, :], in0=pick[0][:, :, :], scalar=-4.0,
                                                       in1=key[:, :, :], op0=ALU.mult, op1=ALU.add), a)
    a = q.dve(lambda e: e.tensor_tensor(both[:, :, :], pick[0][:, :, :], pick[1][:, :, :], ALU.add), a)
    flat = both[:, :, :].rearrange("p t e -> p (t e)")
    p1 = q.pe(lambda e: e.matmul(m.psum[:, 0:NT * E], m.before[:, :], flat, start=True, stop=True), a)
    p2 = q.pe(lambda e: e.matmul(m.psum[:, HALF:HALF + NT * E], m.ones[:, :], flat, start=True, stop=True), a)
    a = q.dve(lambda e: e.tensor_copy(pos[:, :, :].rearrange("p t e -> p (t e)"), m.psum[:, 0:NT * E]), p1)
    a = q.dve(lambda e: e.tensor_copy(total[:, :, :].rearrange("p t e -> p (t e)"),
                                      m.psum[:, HALF:HALF + NT * E]), p2, a)
    cur, at, step = total, 0, 1
    while step < NT:
        dst = scan[at]
        q.dve(lambda e, cur=cur, dst=dst, step=step: e.tensor_copy(dst[:, 0:step, :], cur[:, 0:step, :]), a)
        a = q.dve(lambda e, cur=cur, dst=dst, step=step: e.tensor_tensor(
            dst[:, step:NT, :], cur[:, step:NT, :], cur[:, 0:NT - step, :], ALU.add), a)
        cur, at, step = dst, 1 - at, 2 * step
    count = cur[:, NT - 1, :]
    a = q.dve(lambda e, cur=cur: e.tensor_tensor(pos[:, :, :], pos[:, :, :], cur[:, :, :], ALU.add), a)
    a = q.dve(lambda e: e.tensor_tensor(pos[:, :, :], pos[:, :, :], total[:, :, :], ALU.subtract), a)
    a = q.dve(lambda e, count=count: e.tensor_scalar(tiles_i[:, :], count, float(P - 1), None, ALU.add), a)
    a = q.dve(lambda e: e.tensor_scalar(tiles_i[:, :], tiles_i[:, :], P.bit_length() - 1, None,
                                        ALU.logical_shift_right), a)
    a = q.dve(lambda e: e.tensor_copy(tiles[:, :], tiles_i[:, :]), a)
    a = q.dve(lambda e: e.tensor_scalar(seat[:, :], rank[0:1, :], -1.0, float(E), ALU.mult, ALU.add), a)
    a = q.dve(lambda e: e.tensor_scalar(score[:, :], tiles[0:1, :], 0.0, None, ALU.is_gt), a)
    a = q.dve(lambda e: e.scalar_tensor_tensor(out=score[:, :], in0=rank[0:1, :], scalar=-1.0, in1=score[:, :],
                                               op0=ALU.add, op1=ALU.mult), a)
    for k in range(AHEAD):
        of = follower[:, k - 1, :] if k else seat[:, :]
        a = q.dve(lambda e, of=of: e.tensor_tensor(later[:, :, :], repeat(seat[:, :], E), widen(of, E), ALU.is_gt), a)
        a = q.dve(lambda e: e.tensor_tensor(later[:, :, :], later[:, :, :], repeat(score[:, :], E), ALU.mult), a)
        a = q.dve(lambda e, k=k: e.reduce_max(follower[:, k, :], later[:, :, :], AX.X), a)
        a = q.dve(lambda e, k=k: e.tensor_scalar(follower[:, k, :], follower[:, k, :], -1.0, float(E - 1),
                                                 ALU.mult, ALU.add), a)
    cur, at, step = tiles, 0, 1
    while step < E:
        dst = upto[at]
        q.dve(lambda e, cur=cur, dst=dst, step=step: e.tensor_copy(dst[:, 0:step], cur[:, 0:step]), a)
        a = q.dve(lambda e, cur=cur, dst=dst, step=step: e.tensor_tensor(
            dst[:, step:E], cur[:, step:E], cur[:, 0:E - step], ALU.add), a)
        cur, at, step = dst, 1 - at, 2 * step
    end = cur
    a = q.dve(lambda e, end=end: e.tensor_tensor(tiles[:, :], end[:, :], tiles[:, :], ALU.subtract), a)
    a = q.dve(lambda e: e.scalar_tensor_tensor(out=pos[:, :, :], in0=repeat(tiles[:, :], NT), scalar=float(P),
                                               in1=pos[:, :, :], op0=ALU.mult, op1=ALU.add), a)
    for k in range(2):
        a = q.dve(lambda e, k=k: e.tensor_tensor(prod[:, :, :], pick[k][:, :, :], pos[:, :, :], ALU.mult), a)
        a = q.dve(lambda e, k=k: e.reduce_sum(row[:, k, :], prod[:, :, :], AX.X), a)
    a = q.dve(lambda e: e.tensor_copy(slots[:, :, :], row[:, :, :]), a)
    a = q.dve(lambda e, end=end: e.tensor_tensor(ge[:, :, :], widen(j_iota[:, :], E), repeat(end[0:1, :], J),
                                                 ALU.is_ge), a)
    a = q.dve(lambda e: e.reduce_sum(ex[:, :], ge[:, :, :], AX.X), a)
    a = q.dve(lambda e: e.tensor_scalar(ex[:, :], ex[:, :], float(E - 1), None, ALU.min), a)
    a = q.dve(lambda e: e.memset(new[:, 0:1], 1.0), a)
    a = q.dve(lambda e: e.tensor_tensor(new[:, 1:J], ex[:, 1:J], ex[:, 0:J - 1], ALU.not_equal), a)
    cur, at, step = new, 0, 1
    while step < J:
        dst = run[at]
        q.dve(lambda e, cur=cur, dst=dst, step=step: e.tensor_copy(dst[:, 0:step], cur[:, 0:step]), a)
        a = q.dve(lambda e, cur=cur, dst=dst, step=step: e.tensor_tensor(
            dst[:, step:J], cur[:, step:J], cur[:, 0:J - step], ALU.add), a)
        cur, at, step = dst, 1 - at, 2 * step
    for least in range(W_BUFS * (E // W_BUFS), 0, -W_BUFS):
        a = q.dve(lambda e, cur=cur, least=least: e.tensor_scalar(other[:, :], cur[:, :], float(least),
                                                                  -float(W_BUFS), ALU.is_ge, ALU.mult), a)
        a = q.dve(lambda e, cur=cur: e.tensor_tensor(cur[:, :], cur[:, :], other[:, :], ALU.add), a)
    a = q.dve(lambda e, cur=cur: e.tensor_scalar(other[:, :], cur[:, :], -1.0, 1.0, ALU.mult, ALU.add), a)
    a = q.dve(lambda e: e.tensor_tensor(is_tile[:, :, :], widen(ex[:, :], E), repeat(seat[:, :], J), ALU.is_equal), a)
    for k in range(AHEAD):
        a = q.dve(lambda e, k=k: e.tensor_tensor(ge[:, :, :], is_tile[:, :, :], repeat(follower[:, k, :], J),
                                                 ALU.mult), a)
        a = q.dve(lambda e, k=k: e.reduce_sum(ahead[:, k, :], ge[:, :, :], AX.X), a)
    for i, src in enumerate((ex[:, :], *(ahead[:, k, :] for k in range(AHEAD)), new[:, :], cur[:, :], other[:, :])):
        a = q.dve(lambda e, i=i, src=src: e.tensor_copy(plan[0:1, i, :], src), a)
    first = fetch_first_expert(a)
    flat_slots = slots[:, :, :].rearrange("p k t -> p (k t)")
    h = q.dve(lambda e: e.tensor_scalar(place_i[:, 0, :], flat_slots, P.bit_length() - 1, None,
                                        ALU.logical_shift_right), a)
    h = q.dve(lambda e: e.tensor_scalar(place_i[:, 1, :], flat_slots, P - 1, None, ALU.bitwise_and), h)
    h = q.dve(lambda e: e.tensor_copy(place[:, :, :], place_i[:, :, :]), h)
    hot_ring = Ring(n_hot)
    T = m.psum[:, 2 * HALF:2 * HALF + MOE_TILES]
    for i in range(2 * NT):
        s, free = hot_ring.take()
        r_hot = q.dve(lambda e, s=s, i=i: e.tensor_scalar(row_hot[:, s, :], count_up[:, :],
                                                          place[:, 1, i:i + 1], None, ALU.is_equal), h, *free)
        t_hot = (q.pool if i % 4 == 3 else q.dve)(lambda e, s=s, i=i: e.tensor_scalar(
            tile_hot[:, s, :], count_up[:, 0:MOE_TILES], place[:, 0, i:i + 1], name[:, i % NT:i % NT + 1],
            ALU.is_equal, ALU.mult), h, *free)
        mm = q.pe(lambda e, s=s, i=i: e.matmul(T, row_hot[:, s, :], tile_hot[:, s, :], start=(i == 0),
                                               stop=(i == 2 * NT - 1)), r_hot, t_hot)
        hot_ring.free(s, mm)
    q.dve(lambda e: e.tensor_copy(tokens[:, :], T), mm)
    q.barrier()
    sb.close()
    return first


EXPERT, SECOND, THIRD, FOURTH, IS_NEW, BUFFER, OTHER_BUFFER = range(7)
ROW_BUFS = 6


WIDE = 2 * DC * F + FC * D
DOWN_AT = 2 * DC * F
PIECES = ((0, DC * F), (DC * F, DOWN_AT), (DOWN_AT, WIDE))


class Weights:

    def __init__(self, nc):
        self.sb = Arena(nc)
        self.raw, self.low, self.high = (self.sb(f"e_w_{name}", [P, W_BUFS, WIDE]) for name in
                                         ("raw", "low", "high"))

    def fetch_first(self, m, plan, weights, planned_by):
        done = []
        for i, (a, b) in enumerate(PIECES):
            got = m.q.dma_by("sync", f"first_in{i}", lambda e, a=a, b=b: e.dma_start(
                self.raw[:, 1, a:b],
                weights[bass.ds(e.value_load(plan[0:1, EXPERT, 0:1], min_val=0, max_val=EXPERTS - 1), 1), :,
                        a:b].rearrange("e p n -> p (e n)")), planned_by)
            done.append(m.q.act(lambda e, a=a, b=b: e.activation(
                self.high[:, 1, a:b].bitcast(FP32R), self.raw[:, 1, a:b], ACT.Copy), got))
        return done


def experts(m, tokens, plan, first, buffers, weights, rows_dram, queue_y):
    q = m.q
    sb = Arena(m.nc)
    w_raw, w_low, w_high = buffers.raw, buffers.low, buffers.high
    x = sb("e_x", [P, ROW_BUFS, D])
    xT = sb("e_xT", [P, 2, 2, DC, P])
    act = sb("e_act", [P, F])
    hid = sb("e_hid", [P, F])
    hT = sb("e_hT", [P, 2, FC, P])
    y = sb("e_y", [P, 2, D])
    J = MOE_TILES
    GU = m.psum[:, 0:2 * F].rearrange("p (a f) -> p a f", a=2)
    HT = m.psum[:, 2 * F:3 * F]
    XT = m.psum[:, 3 * F:3 * F + DC * P]
    Y = m.psum[:, 3 * F + HALF:3 * F + HALF + D]
    x_ring, xT_ring, y_ring = Ring(ROW_BUFS), Ring(2), Ring(2)
    buffer_of = {}

    def planned(eng, row, j):
        return eng.value_load(plan[0:1, row, j:j + 1], min_val=0, max_val=(1 if row == IS_NEW else
                                                                           W_BUFS - 1 if row >= BUFFER else
                                                                           EXPERTS - 1))

    def fetch_first(row, buf, a, b, lane, *after):
        return q.dma_by("sync", lane, lambda e: e.dma_start(
            w_raw[:, buf, a:b], weights[bass.ds(planned(e, row, 0), 1), :, a:b].rearrange("e p n -> p (e n)")),
            *after)

    def fetch(j, cond, after):

        def emit(e):
            only_if = {"cond": planned(e, IS_NEW, j) > 0} if cond else {}
            return e.dma_start(w_raw[:, bass.ds(planned(e, OTHER_BUFFER, j), 1), :],
                               weights[bass.ds(planned(e, FOURTH, j), 1), :, :].rearrange("e p n -> p e n"),
                               **only_if)

        return q.dma_by("sync", "weights_in", emit, after)

    def high_part(j, a, b, got, *free, flag=None, is_set=1):
        got.needed = True

        def emit(e):
            buf = bass.ds(planned(e, OTHER_BUFFER, j), 1)
            is_new = planned(e, IS_NEW, j if flag is None else flag)
            with e.If(is_new > 0 if is_set else is_new < 1):
                e.wait_ge(got.sem.handle, got.value)
                e.activation(w_high[:, buf, a:b].bitcast(FP32R), w_raw[:, buf, a:b], ACT.Copy)
            return e.drain()

        return q.act(emit, *free)

    def low_part(j, high, flag=None, is_set=1):

        def emit(e):
            buf = bass.ds(planned(e, OTHER_BUFFER, j), 1)
            is_new = planned(e, IS_NEW, j if flag is None else flag)
            with e.If(is_new > 0 if is_set else is_new < 1):
                e.tensor_tensor(w_low[:, buf, :].bitcast(FP32R), w_raw[:, buf, :], w_high[:, buf, :], ALU.subtract)
            return e.drain()

        return q.pool(emit, high)

    def load_rows(j):
        s, free = x_ring.take()
        return s, q.dma_by("gpsimd", f"rows_in{s}", lambda e: e.indirect_dma_start(
            out=x[:, s, :], out_offset=None, in_=rows_dram,
            in_offset=bass.IndirectOffsetOnAxis(ap=tokens[:, j:j + 1], axis=0)), *free)

    XT_free = Y_free = HT_free = act_free = hid_free = hT_free = ()

    def turn(s, got):
        nonlocal XT_free
        for c in range(DC):
            tr = q.pe(lambda e, c=c, s=s: e.transpose(XT[:, c * P:(c + 1) * P], x[:, s, c * P:(c + 1) * P],
                                                      m.ident[:, :]), got, *XT_free)
        x_ring.free(s, tr)
        o, free = xT_ring.take()
        high, low = (xT[:, o, i, :, :].rearrange("p c n -> p (c n)") for i in range(2))
        h = q.dve(lambda e: e.tensor_copy(high.bitcast(FP32R), XT), tr, *free)
        l = q.dve(lambda e: e.tensor_tensor(low.bitcast(FP32R), XT, high, ALU.subtract), h)
        XT_free = (l,)
        return o, l

    def buffer(e, j):
        if j not in buffer_of:
            buffer_of[j] = planned(e, BUFFER, j)
        return buffer_of[j]

    def wait_for_weights(j):
        usual = None if j == 1 else split_done["second"] if j == 2 else split_done[j - 2]
        late = split_done[j - 1]

        def emit(e):
            with e.If(buffer(e, j) != buffer(e, j - 1)):
                if usual is not None:
                    e.wait_ge(usual.sem.handle, usual.value)
                    with e.If(buffer(e, j - 1) != buffer(e, j - 2)):
                        e.wait_ge(late.sem.handle, late.value)
                else:
                    e.wait_ge(late.sem.handle, late.value)

        for done in (usual, late):
            if done is not None:
                done.needed = True
        q.steps["tensor"].append((emit, [], None))

    def product(j, out, left, at, n, start, stop, ready, free):
        for i, (part, w) in enumerate(((0, w_high), (0, w_low), (1, w_high))):

            def emit(e, part=part, w=w, i=i):
                moving = w[:, bass.ds(buffer(e, j), 1), at:at + n].rearrange("p a n -> p (a n)")
                return e.matmul(out, left[part].bitcast(FP32R), moving.bitcast(FP32R),
                                start=start and i == 0, stop=stop and i == 2)

            mm = q.pe(emit, *ready, *free)
        return mm

    def up_product(j, which, o, ready, free):
        for half in range(F // HALF):
            for c in range(DC):
                mm = product(j, GU[:, which, half * HALF:(half + 1) * HALF],
                             (xT[:, o, 0, c, :], xT[:, o, 1, c, :]), (which * DC + c) * F + half * HALF, HALF,
                             c == 0, c == DC - 1, ready, free)
        return mm

    def turn_hidden(done):
        nonlocal HT_free, hid_free
        for f in range(FC):
            tr = q.pe(lambda e, f=f: e.transpose(HT[:, f * P:(f + 1) * P], hid[:, f * P:(f + 1) * P],
                                                 m.ident[:, :]), done, *HT_free)
        hid_free = (tr,)
        high, low = (hT[:, i, :, :].rearrange("p f n -> p (f n)") for i in range(2))
        h = q.act(lambda e: e.activation(high.bitcast(FP32R), HT, ACT.Copy), tr, *hT_free)
        l = q.dve(lambda e: e.tensor_tensor(low.bitcast(FP32R), HT, high, ALU.subtract), h)
        HT_free = (l,)
        return l

    def down(j, ready):
        nonlocal Y_free, hT_free
        for f in range(FC):
            mm = product(j, Y, (hT[:, 0, f, :], hT[:, 1, f, :]), DOWN_AT + f * D, D, f == 0, f == FC - 1,
                         ready, Y_free)
        hT_free = (mm,)
        o, free = y_ring.take()
        cp = q.act(lambda e: e.activation(y[:, o, :], Y, ACT.Copy), mm, *free)
        Y_free = (cp,)
        y_ring.free(o, q.dma(f"y_out{o}", queue_y[j * P:(j + 1) * P, :], y[:, o, :], cp, queue="scalar"))
        return mm

    rows = {j: load_rows(j) for j in range(ROW_BUFS)}
    second_in = fetch_first(SECOND, 0, 0, WIDE, "second_in", rows[1][1])

    def first_low(a, b, high):
        return q.dve(lambda e: e.tensor_tensor(w_low[:, 1, a:b].bitcast(FP32R), w_raw[:, 1, a:b],
                                               w_high[:, 1, a:b], ALU.subtract), high)

    turned = {0: turn(*rows.pop(0))}
    first_ready = [first_low(*piece, high) for piece, high in zip(PIECES, first)]
    gate_ready, up_ready, down_ready = first_ready
    last_fetch = fetch_first(THIRD, 1, 0, WIDE, "weights_in", down_ready)
    split_done = {}
    g_free = u_free = ()
    u = None
    pending = None
    for j in range(J):
        o, xready = turned.pop(j)
        if j in (1, 2):
            how = {"flag": 1, "is_set": int(j == 1)}
            split_done[0 if j == 1 else "second"] = low_part(0, high_part(0, 0, WIDE, second_in, **how), **how)
        if j == 2:
            last_fetch = fetch(0, False, split_done["second"])
        if j >= 1:
            wait_for_weights(j)
        u_before = u
        g = up_product(j, 0, o, (xready, gate_ready), g_free)
        sg = q.act(lambda e: e.activation(act[:, :], GU[:, 0, :], ACT.Silu), g, *act_free)
        g_free = (sg,)
        if j >= 1:
            hidden = turn_hidden(pending)
            high_part(j, 0, DOWN_AT, last_fetch, u_before)
        u = up_product(j, 1, o, (xready, up_ready), u_free)
        xT_ring.free(o, u)
        pending = q.dve(lambda e: e.tensor_tensor(hid[:, :], act[:, :], GU[:, 1, :], ALU.mult), sg, u, *hid_free)
        act_free = u_free = (pending,)
        if j + 1 < J:
            turned[j + 1] = turn(*rows.pop(j + 1))
        if j + ROW_BUFS < J:
            rows[j + ROW_BUFS] = load_rows(j + ROW_BUFS)
        if j >= 1:
            down_done = down(j - 1, (hidden, down_ready))
            split_done[j] = low_part(j, high_part(j, DOWN_AT, WIDE, last_fetch, down_done))
            last_fetch = fetch(j, True, split_done[j])
    down(J - 1, (turn_hidden(pending), down_ready))
    q.barrier()
    sb.close()


def combine_tokens(m, sb, x1_dram, x2_dram, pi, slots, queue_y):
    q = m.q
    x1_src = x1_dram.rearrange("(b t p) d -> b p t d", p=P, t=BT)
    x2_dst = x2_dram.rearrange("(b t p) d -> b p t d", p=P, t=BT)
    rows = [sb(f"g_rows{k}", [P, 2, BT, D]) for k in range(2)]
    rings = [Ring(2), Ring(2)]

    def open_batch(b, slot, x, free):
        got = q.dma(f"x1_in{slot}", x, x1_src[b, :, :, :], *free)
        gathered = {}
        for k in range(2):
            r, r_free = rings[k].take()
            for i in range(BT):
                t = b * BT + i
                here = q.dma_by("gpsimd", f"rows_back{k}{r}", lambda e, k=k, r=r, i=i, t=t: e.indirect_dma_start(
                    out=rows[k][:, r, i, :], out_offset=None, in_=queue_y,
                    in_offset=bass.IndirectOffsetOnAxis(ap=slots[:, k, t:t + 1], axis=0)), *r_free)
            gathered[k] = (r, here)
        return lambda: combine(b, slot, x, got, gathered)

    def combine(b, slot, x, got, gathered):
        for k in range(2):
            r, here = gathered[k]
            for i in range(BT):
                t = b * BT + i
                done = q.dve(lambda e, k=k, r=r, i=i, t=t, x=x: e.scalar_tensor_tensor(
                    out=x[:, i, :], in0=rows[k][:, r, i, :], scalar=pi[:, t, k:k + 1], in1=x[:, i, :],
                    op0=ALU.mult, op1=ALU.add), here, got)
            rings[k].free(r, done)
            got = done
        return done, (q.dma(f"x2_out{slot}", x2_dst[b, :, :, :], x, done),)

    return open_batch


def bias_tables(m, sb, amplitudes, sharpness, offsets, tables_dram, table_range):
    q = m.q
    terms = 21
    groups = 3
    R = H * terms // groups
    W = 2 * S
    coef = sb("b_coef", [R, 3, groups])
    mask = sb("b_mask", [R, groups, H])
    rel = sb("b_rel", [R, W])
    d = sb("b_d", [R, groups, W])
    table = sb("b_table", [H, W])
    mirror = sb("b_mirror", [H, W])
    ends = sb("b_ends", [H, 2])
    ends_row = sb("b_ends_row", [1, 2, H])
    for i, src in enumerate((amplitudes, sharpness, offsets)):
        got = q.dma("coef_in", coef[:, i, :], src)
    a = q.pool(lambda e: e.memset(mask[:, :, :], 1.0))
    a = q.pool(lambda e: e.affine_select(out=mask[:, :, :], in_=mask[:, :, :], compare_op=ALU.is_ge, fill=0.0,
                                         base=0, pattern=[[R, groups], [-terms, H]], channel_multiplier=1), a)
    a = q.pool(lambda e: e.affine_select(out=mask[:, :, :], in_=mask[:, :, :], compare_op=ALU.is_ge, fill=0.0,
                                         base=terms - 1, pattern=[[-R, groups], [terms, H]],
                                         channel_multiplier=-1), a)
    i0 = q.pool(lambda e: e.iota(rel[:, :], pattern=[[1, W]], base=-(S - 1), channel_multiplier=0,
                                 allow_small_or_imprecise_dtypes=True))
    sharp = sb("b_sharp", [R, groups])
    s1 = q.dve(lambda e: e.tensor_scalar(sharp[:, :], coef[:, 1, :], -1.0, None, ALU.mult), got)
    s1 = q.dve(lambda e: e.tensor_tensor(sharp[:, :], sharp[:, :], coef[:, 1, :], ALU.min), s1)
    masked = a
    for g in range(groups):
        mk = q.dve(lambda e, g=g: e.tensor_scalar(mask[:, g, :], mask[:, g, :], coef[:, 0, g:g + 1], None,
                                                  ALU.mult), masked, got)
        a = q.dve(lambda e, g=g: e.tensor_scalar(d[:, g, :], rel[:, :], coef[:, 2, g:g + 1], None,
                                                 ALU.subtract), i0, got)
        a = q.dve(lambda e, g=g: e.scalar_tensor_tensor(out=d[:, g, :], in0=d[:, g, :], scalar=sharp[:, g:g + 1],
                                                        in1=d[:, g, :], op0=ALU.mult, op1=ALU.mult), a, s1)
        ex = q.act(lambda e, g=g: e.activation(d[:, g, :], d[:, g, :], ACT.Exp), a)
        yield
    for j in range(W // HALF):
        for g in range(groups):
            mm = q.pe(lambda e, j=j, g=g: e.matmul(m.psum[0:H, W + j * HALF:W + (j + 1) * HALF], mask[:, g, :],
                                                   d[:, g, j * HALF:(j + 1) * HALF], start=(g == 0),
                                                   stop=(g == groups - 1)), ex, mk)
            yield
    L = W - 1
    t1 = q.dve(lambda e: e.tensor_copy(table[:, :], m.psum[0:H, W:2 * W]), mm)
    t2 = q.dve(lambda e: e.tensor_copy(mirror[:, 0:L], table[:, 0:L][:, ::-1]), t1)
    t2 = q.dve(lambda e: e.tensor_copy(mirror[:, L:W], table[:, L:W]), t2)
    q.dma("tables_out", tables_dram[0, :, :], table[:, :], t1)
    yield
    q.dma("tables_out", tables_dram[1, :, :], mirror[:, :], t2)
    x1 = q.dve(lambda e: e.reduce_max(ends[:, 0:1], table[:, 0:L], AX.X), t2)
    x2 = q.dve(lambda e: e.tensor_reduce(out=ends[:, 1:2], in_=table[:, 0:L], axis=AX.X, op=ALU.min, negate=True), x1)
    for k in range(2):
        tr = q.pe(lambda e, k=k: e.transpose(m.psum[0:1, W + k * H:W + (k + 1) * H], ends[:, k:k + 1],
                                             m.ident[0:H, 0:H]), x2)
        yield
    a = q.dve(lambda e: e.tensor_copy(ends_row[:, :, :].rearrange("a k h -> a (k h)"),
                                      m.psum[0:1, W:W + 2 * H]), tr)
    a = q.dve(lambda e: e.reduce_max(table_range[:, :], ends_row[:, :, :], AX.X), a)
    q.dve(lambda e: e.tensor_scalar(table_range[:, :], table_range[:, :], 0.0, None, ALU.max), a)


FP8_MAX = 448.0


def close_second_layer(m, om, x2_dram, wg_dram, bg_dram, w8_dram, b8_dram, scales_dram, out_dram):
    q = m.q
    sb = Arena(m.nc)
    wg = sb("f_wg", [P, DC, 2 * D])
    bg = sb("f_bg", [P, 2 * D])
    w8 = sb("f_w8", [P, DC, D])
    w8_high = sb("f_w8_high", [P, DC, D])
    w8_low = sb("f_w8_low", [P, DC, D])
    b8 = sb("f_b8", [P, D])
    sc = sb("f_sc", [P, 2])
    inv = sb("f_inv", [P, 1])
    omT = sb("f_omT", [P, DC, S])
    x = sb("f_x", [P, 2, BT, D])
    gated = sb("f_gated", [P, 2, BT, 2, D])
    xn = sb("f_xn", [P, 2, BT, D])
    step = sb("f_step", [P, BT, D])
    xqT = sb("f_xqT", [P, DC, S])
    lnw = layernorm_scratch(sb, "f_")
    x2_src = x2_dram.rearrange("(b t p) d -> b p t d", p=P, t=BT)
    out_dst = out_dram.rearrange("(b t p) d -> b p t d", p=P, t=BT)
    ring = Ring(4)
    x_ring, xn_ring = Ring(2), Ring(2)
    omT_ring, xqT_ring, gated_ring, step_ring = Ring(1), Ring(1), Ring(2), Ring(1)

    def fetch(b):
        s, free = x_ring.take()
        return s, q.dma(f"x2_in{s}", x[:, s, :, :], x2_src[b, :, :, :], *free)

    fetched = [fetch(b) for b in range(2)]
    q.dma("f_w_in", wg[:, :, :], wg_dram.rearrange("(c p) n -> p c n", p=P), queue="scalar")
    q.dma("f_w_in", w8[:, :, :], w8_dram.rearrange("(c p) n -> p c n", p=P), queue="scalar")
    q.dma("f_w_in", bg[:, :], across(bg_dram, P), queue="scalar")
    q.dma("f_w_in", b8[:, :], across(b8_dram, P), queue="scalar")
    got_w = q.dma("f_w_in", sc[:, :], across(scales_dram, P), queue="scalar")
    r = q.dve(lambda e: e.reciprocal(inv[:, :], sc[:, 0:1]), got_w)
    w8s = q.dve(lambda e: e.tensor_scalar(w8[:, :, :], w8[:, :, :], sc[:, 1:2], sc[:, 0:1], ALU.mult, ALU.mult),
                got_w)
    w8s = q.dve(lambda e: e.tensor_copy(w8_high[:, :, :].bitcast(FP32R), w8[:, :, :]), w8s)
    w8s = q.dve(lambda e: e.tensor_tensor(w8_low[:, :, :].bitcast(FP32R), w8[:, :, :], w8_high[:, :, :],
                                          ALU.subtract), w8s)

    def gate(b):
        _, free = omT_ring.take()
        made = transpose_batch(m, ring, om[:, b * BT:(b + 1) * BT, :], omT[:, :, :], None, free)
        yield
        gs, g_free = gated_ring.take()
        for i in range(0, BT, 2):
            slot, free = ring.take()
            ps = m.psum[:, slot * S:(slot + 1) * S]
            for t in (i, i + 1):
                for k in range(DC):
                    mm = q.pe(lambda e, t=t, i=i, k=k, ps=ps: e.matmul(
                        ps[:, (t - i) * 2 * D:(t - i + 1) * 2 * D], omT[:, k, t * P:(t + 1) * P], wg[:, k, :],
                        start=(k == 0), stop=(k == DC - 1)), *made, got_w, *free)
            d = q.dve(lambda e, i=i, ps=ps: e.tensor_tensor(
                gated[:, gs, i:i + 2, :, :].rearrange("p t a n -> p t (a n)"),
                ps.rearrange("p (t n) -> p t n", n=2 * D), repeat(bg[:, :], 2), ALU.add), mm, *g_free)
            ring.free(slot, d)
            yield
        omT_ring.free(0, mm)
        gates[b] = gs, d, q.act(lambda e: e.activation(gated[:, gs, :, 1, :], gated[:, gs, :, 1, :], ACT.Sigmoid), d)

    def round_off(b, gs, d, sg):
        s, got = fetched[b]
        x3 = x[:, s, :, :]
        a = q.dve(lambda e: e.tensor_tensor(gated[:, gs, :, 0, :], gated[:, gs, :, 0, :], gated[:, gs, :, 1, :],
                                            ALU.mult), sg, d)
        yield
        a = q.dve(lambda e, x3=x3: e.tensor_tensor(x3, x3, gated[:, gs, :, 0, :], ALU.add), a, got)
        gated_ring.free(gs, a)
        yield
        n, n_free = xn_ring.take()
        y = xn[:, n, :, :]
        a = yield from layernorm_steps(m, lnw, x3, y, a, r, *n_free, factor=inv[:, 0:1])
        yield
        a = q.dve(lambda e, y=y: e.tensor_scalar(y, y, FP8_MAX, -FP8_MAX, ALU.min, ALU.max), a)
        _, s_free = step_ring.take()
        a = q.dve(lambda e, y=y: e.tensor_scalar(step[:, :, :].bitcast(I32), y.bitcast(I32), 0x7F800000,
                                                 None, ALU.bitwise_and), a, *s_free)
        yield
        a = q.dve(lambda e: e.tensor_scalar(step[:, :, :], step[:, :, :], 2.0 ** -6, 1.5 * 2.0 ** 20,
                                            ALU.max, ALU.mult), a)
        yield
        a = q.dve(lambda e, y=y: e.tensor_tensor(y, y, step[:, :, :], ALU.add), a)
        a = q.dve(lambda e, y=y: e.tensor_tensor(y, y, step[:, :, :], ALU.subtract), a)
        step_ring.free(0, a)
        xb = q.pool(lambda e, x3=x3: e.tensor_tensor(x3, x3, repeat(b8[:, :], BT), ALU.add), a)
        rounded[b] = s, n, a, xb

    def product(b, s, n, ready, xb):
        x3 = x[:, s, :, :]
        _, free = xqT_ring.take()
        made = transpose_batch(m, ring, xn[:, n, :, :], xqT[:, :, :].bitcast(FP32R), ready, free)
        yield
        xn_ring.free(n, *made)
        for half in range(2):
            slot, free = ring.take()
            ps = m.psum[:, slot * S:(slot + 1) * S]
            for i in range(BT // 2):
                t = half * (BT // 2) + i
                for k in range(DC):
                    for part in (w8_high, w8_low):
                        mm = q.pe(lambda e, i=i, t=t, k=k, ps=ps, part=part: e.matmul(
                            ps[:, i * D:(i + 1) * D], xqT[:, k, t * P:(t + 1) * P].bitcast(FP32R),
                            part[:, k, :].bitcast(FP32R), start=(k == 0 and part is w8_high),
                            stop=(k == DC - 1 and part is w8_low)), *made, w8s, *free)
            h0 = half * (BT // 2)
            a = q.dve(lambda e, x3=x3, h0=h0, ps=ps: e.tensor_tensor(
                x3[:, h0:h0 + BT // 2, :], ps.rearrange("p (t d) -> p t d", d=D), x3[:, h0:h0 + BT // 2, :],
                ALU.add), mm, xb)
            ring.free(slot, a)
            yield
        xqT_ring.free(0, mm)
        x_ring.free(s, q.dma(f"out{s}", out_dst[b, :, :, :], x3, a))
        if b + 2 < B:
            fetched.append(fetch(b + 2))

    def take_turns(*programs):
        running = list(programs)
        while running:
            running = [p for p in running if next(p, q) is not q]

    gates, rounded = {}, {}
    take_turns(gate(0))
    take_turns(round_off(0, *gates[0]), gate(1))
    for b in range(B):
        on_pe = chain(product(b, *rounded[b]), gate(b + 2) if b + 2 < B else ())
        take_turns(*([round_off(b + 1, *gates[b + 1])] if b + 1 < B else []), on_pe)
    q.barrier()
    sb.close()


def build_program(nc, ctx, t, out_dram):
    m = Machine()
    m.nc, m.q, m.keep = nc, Queues(nc, ctx), Arena(nc)
    q = m.q
    m.psum = ctx.enter_context(nc.psum_tensor("psum", [P, 8 * HALF], FP32))[:, :]

    def scratch(name, shape, dtype=FP32):
        return nc.dram_tensor(name, shape, dtype, kind="Internal").ap()

    parts = scratch("qk_parts", [2, 3, B, D, S], BF16)
    x1_dram, x2_dram = scratch("x1", [N, D]), scratch("x2", [N, D])
    rows, queue_y = scratch("token_rows", [N, D]), scratch("queue_y", [MOE_TILES * P, D])
    tables = scratch("tables", [2, H, 2 * S])

    make_constants(m)
    m.norms = m.keep("norms", [H // DC, 2, DC * B])
    m.bound = m.keep("bound", [H // DC, 16])
    m.shift = m.keep("shift", [P, 1])
    m.flag = m.keep("flag", [1, 1], I32)
    table_range = m.keep("table_range", [1, 2])
    la = m.keep("la", [P, NT, EXPERTS])
    pi = m.keep("pi", [P, NT, EXPERTS])
    slots = m.keep("slots", [P, 2, NT], I32)

    def attend(layer, om, tables, order, beside=None):
        main = m.q
        paths = []
        for row_max in (False, True):
            m.q = Queues(nc, ctx, f"a{layer}{'rowmax' if row_max else 'shift'}")
            attention(m, layer, parts, tables, om, order, row_max, beside)
            paths.append(m.q)
        m.q = main
        main.either(m.flag[0:1, 0:1], *paths)
        main.barrier()
        main.load_tables(LN_EXP)

    q.load_tables(LN_EXP)
    first = Arena(nc)
    m.v = first("v0", [P, NT, H * VW + HD])
    om = first("om0", [P, NT, D])
    project(m, 0, load_tokens(m, t["x"]), [t["wq"], t["wk"], t["wv"]], [t["bq"], t["bk"], t["bv"]], parts)
    close = FirstClose(m, om, t["x"], t["wo"], t["bo"], t["gate"], x1_dram, rows, la)
    score_bound(m, 0, None)
    q.barrier()
    attend(0, om, None, [(g, b) for b in range(B) for g in range(NG)], close)
    close.sb.close()
    first.close()

    beside = Arena(nc)
    sinkhorn(m, la, pi, bias_tables(m, beside, t["amplitudes"], t["sharpness"], t["offsets"], tables, table_range))
    beside.close()
    routing = Arena(nc)
    plan = routing("plan", [1, 7, MOE_TILES], I32)
    tokens = routing("tokens", [P, MOE_TILES], I32)
    buffers = Weights(nc)
    first_expert = route(m, pi, slots, tokens, plan, lambda planned_by: buffers.fetch_first(
        m, plan, t["experts"], planned_by))
    experts(m, tokens, plan, first_expert, buffers, t["experts"], rows, queue_y)
    buffers.sb.close()
    routing.close()
    q.load_tables(LN_EXP)

    second = Arena(nc)
    m.v = second("v1", [P, NT, H * VW + HD])
    om = second("om1", [P, NT, D])
    gather = Arena(nc)
    project(m, 1, combine_tokens(m, gather, x1_dram, x2_dram, pi, slots, queue_y),
            [t["w_q"], t["w_k"], t["w_v"]], None, parts)
    gather.close()
    score_bound(m, 1, table_range[:, :])
    q.barrier()
    attend(1, om, tables, [(g, b) for g in range(NG) for b in range(B)])
    close_second_layer(m, om, x2_dram, t["w_gate"], t["b_gate"], t["w8"], t["b8"], t["scales"], out_dram)
    second.close()
    q.emit()


def kernel(**inputs):
    import numpy as np
    import concourse.bacc as bacc
    from concourse import mybir
    from concourse.bass_utils import run_bass_kernel_spmd

    a = {k: np.asarray(v) for k, v in inputs.items()}

    def circulant(c):
        n = np.arange(D)
        return c[(n[None, :] - n[:, None]) % D]

    def by_chunk(v):
        return v.reshape(-1, P).T

    def by_rows(v):
        return v.reshape(3, -1).T

    def expert_rows(wg, wu, wd):
        up = [w.transpose(0, 2, 1).reshape(EXPERTS, DC, P, F).transpose(0, 2, 1, 3).reshape(EXPERTS, P, -1)
              for w in (wg, wu)]
        down = wd.transpose(0, 2, 1).reshape(EXPERTS, FC, P, D).transpose(0, 2, 1, 3).reshape(EXPERTS, P, -1)
        return np.concatenate([*up, down], axis=2)

    w_in = a["L1_attn_w_in"]
    laid = {
        "x": a["L0_attn_x"].reshape(N, D),
        **{f"w{i}": circulant(a[f"L0_attn_w{i}_c"]) for i in "qkvo"},
        **{f"b{i}": by_chunk(a[f"L0_attn_w{i}_b"]) for i in "qk"},
        **{f"b{i}": a[f"L0_attn_w{i}_b"] for i in "vo"},
        "gate": a["L0_ffn_gate_W"].T,
        "experts": expert_rows(a["L0_ffn_W_gate"], a["L0_ffn_W_up"], a["L0_ffn_W_down"]),
        "w_k": w_in[:, 0:D], "w_v": w_in[:, D:2 * D], "w_q": w_in[:, 2 * D:3 * D],
        "w_gate": a["L1_attn_w_gate"], "b_gate": a["L1_attn_b_gate"],
        "amplitudes": by_rows(a["L1_attn_amplitudes"]), "sharpness": by_rows(a["L1_attn_sharpness"]),
        "offsets": by_rows(a["L1_attn_offsets"]),
        "w8": a["L1_ffn_weight_fp8"].T, "b8": a["L1_ffn_bias"],
        "scales": np.concatenate([a["L1_ffn_input_scale"], a["L1_ffn_weight_scale"]]),
    }
    nc = bacc.Bacc("TRN2", target_bir_lowering=False, num_devices=1)
    arrays, tensors = {}, {}
    for name, value in laid.items():
        value = np.ascontiguousarray(value)
        arrays[f"in_{name}"] = value
        tensors[name] = nc.dram_tensor(f"in_{name}", value.shape, mybir.dt.from_np(value.dtype),
                                       kind="ExternalInput").ap()
    out = nc.dram_tensor("out_x", [N, D], FP32, kind="ExternalOutput").ap()
    with ExitStack() as ctx:
        build_program(nc, ctx, tensors, out)
    result = run_bass_kernel_spmd(nc, [arrays], core_ids=[0])
    return result.results[0]["out_x"].reshape(B, S, D)
```
